# Optimizing a Trainium2 kernel written in Bass

```python
import numpy as np
import jax
import jax.numpy as jnp

def _softmax(x, axis=-1):
    return jax.nn.softmax(x, axis=axis)

def _gelu(x):
    return jax.nn.gelu(x, approximate=True)

def _silu(x):
    return jax.nn.silu(x)

def _sigmoid(x):
    return jax.nn.sigmoid(x)

def _layernorm(x, axis=-1, eps=1e-05):
    m = jnp.mean(x, axis=axis, keepdims=True)
    v = jnp.var(x, axis=axis, keepdims=True)
    return (x - m) / jnp.sqrt(v + eps)

def _scatter_add(tgt, idx, src, axis=0):
    return tgt.at[idx].add(src)

def _segment_sum(src, seg, n):
    return jax.ops.segment_sum(src, seg, n)
kernel_name = 'mk_seq_preln_d1_jaxref_r4_edf942'

def setup_inputs(seed: int=0):
    np.random.seed(seed)
    _w = jnp.asarray

    def _L0_attn_setup():
        import jax, jax.numpy as jnp
        import numpy as np
        import math
        B, S, D = (8, 512, 256)

        def _trunc_normal(key, shape, fan_in, fan_out):
            std = math.sqrt(2.0 / (fan_in + fan_out))
            return jax.random.truncated_normal(key, -3.0, 3.0, shape, jnp.float32) * std
        key = jax.random.key(seed)
        kx, kq, kk, kv, ko = jax.random.split(key, 5)
        return {'in_features': jax.random.normal(kx, (B, S, D), jnp.float32), 'Wq': _trunc_normal(kq, (D, D), D, D), 'Wk': _trunc_normal(kk, (D, D), D, D), 'Wv': _trunc_normal(kv, (D, D), D, D), 'Wo': _trunc_normal(ko, (D, D), D, D)}
    _L0_attn_in = _L0_attn_setup()

    def _L0_ffn_setup():
        import jax, jax.numpy as jnp
        import numpy as np
        E = 8
        D = 256
        H = 512
        TOP_K = 2
        key = jax.random.key(seed)
        k_x, k_g, k_w1, k_w2 = jax.random.split(key, 4)
        B, S = (4, 512)
        inp = {'input': jax.random.normal(k_x, (B, S, D), dtype=jnp.float32), 'Wg': jax.random.normal(k_g, (D, E), dtype=jnp.float32) * 0.02, 'W1': jax.random.normal(k_w1, (E, D, H), dtype=jnp.float32) * 0.02, 'b1': jnp.zeros((E, H), dtype=jnp.float32), 'W2': jax.random.normal(k_w2, (E, H, D), dtype=jnp.float32) * 0.02, 'b2': jnp.zeros((E, D), dtype=jnp.float32)}
        return inp
    _L0_ffn_in = _L0_ffn_setup()
    _d = {'L0_attn_in_features': _L0_attn_in['in_features'], 'L0_attn_Wq': _L0_attn_in['Wq'], 'L0_attn_Wk': _L0_attn_in['Wk'], 'L0_attn_Wv': _L0_attn_in['Wv'], 'L0_attn_Wo': _L0_attn_in['Wo'], 'L0_ffn_Wg': _L0_ffn_in['Wg'], 'L0_ffn_W1': _L0_ffn_in['W1'], 'L0_ffn_b1': _L0_ffn_in['b1'], 'L0_ffn_W2': _L0_ffn_in['W2'], 'L0_ffn_b2': _L0_ffn_in['b2']}
    _x0 = _d['L0_attn_in_features']
    _d['L0_attn_in_features'] = jax.random.normal(jax.random.fold_in(jax.random.key(seed), 1), (1, 4096, 256), dtype=_x0.dtype)
    del _x0
    return _d

def reference(L0_attn_in_features, L0_attn_Wq, L0_attn_Wk, L0_attn_Wv, L0_attn_Wo, L0_ffn_Wg, L0_ffn_W1, L0_ffn_b1, L0_ffn_W2, L0_ffn_b2):

    def _L0_attn_ref(in_features, Wq, Wk, Wv, Wo):
        import jax, jax.numpy as jnp
        import numpy as np
        import math
        B, S, D = (8, 512, 256)

        def _trunc_normal(key, shape, fan_in, fan_out):
            std = math.sqrt(2.0 / (fan_in + fan_out))
            return jax.random.truncated_normal(key, -3.0, 3.0, shape, jnp.float32) * std
        d_k = Wq.shape[0]
        scale = 1.0 / math.sqrt(d_k)
        x = in_features
        Q = x @ Wq.T
        K = x @ Wk.T
        V = x @ Wv.T
        scores = jnp.einsum('bqd,bkd->bqk', Q, K) * scale
        seq_len = x.shape[-2]
        causal = jnp.tril(jnp.ones((seq_len, seq_len), dtype=bool))
        scores = jnp.where(causal, scores, -jnp.inf)
        attn = jax.nn.softmax(scores, axis=-1)
        out = jnp.einsum('bqk,bkd->bqd', attn, V)
        return out @ Wo.T

    def _L0_ffn_ref(input, Wg, W1, b1, W2, b2):
        import jax, jax.numpy as jnp
        import numpy as np
        E = 8
        D = 256
        H = 512
        TOP_K = 2
        logits = jnp.einsum('bsd,de->bse', input, Wg)
        probs = jax.nn.softmax(logits, axis=-1)
        top_vals, top_idx = jax.lax.top_k(probs, TOP_K)
        top_vals = top_vals / jnp.sum(top_vals, axis=-1, keepdims=True)
        onehot = jax.nn.one_hot(top_idx, E, dtype=input.dtype)
        mask = jnp.sum(onehot, axis=2)
        scores = jnp.sum(onehot * top_vals[..., None], axis=2)
        xm = input[None] * jnp.moveaxis(mask, -1, 0)[..., None]
        h = jnp.einsum('ebsd,edh->ebsh', xm, W1) + b1[:, None, None, :]
        h = jax.nn.relu(h)
        y = jnp.einsum('ebsh,ehd->ebsd', h, W2) + b2[:, None, None, :]
        out = jnp.sum(y * jnp.moveaxis(scores, -1, 0)[..., None], axis=0)
        return out
    x = L0_attn_in_features
    x = x + _L0_attn_ref(_layernorm(x, axis=-1), L0_attn_Wq, L0_attn_Wk, L0_attn_Wv, L0_attn_Wo)
    x = x + _L0_ffn_ref(_layernorm(x, axis=-1), L0_ffn_Wg, L0_ffn_W1, L0_ffn_b1, L0_ffn_W2, L0_ffn_b2)
    return x

_drawn_inputs = setup_inputs


def setup_inputs(seed=0):
    import zlib

    import numpy as np

    out = dict(_drawn_inputs(seed))
    spreads = {'L0_ffn_b1': (0.0, 0.365), 'L0_ffn_b2': (0.0, 0.1)}
    factors = {}
    for name, (base, spread) in spreads.items():
        noise = np.random.default_rng([zlib.crc32(name.encode()), seed]).standard_normal(out[name].shape)
        drawn = base * np.exp(spread * noise) if base else spread * noise
        out[name] = jnp.asarray(drawn.astype(out[name].dtype))
    for name, factor in factors.items():
        out[name] = (out[name] * factor).astype(out[name].dtype)
    return out
```

```python
from contextlib import ExitStack

import numpy as np
import concourse.bass as bass
from concourse import mybir

F32, F32R, I32, U32 = (mybir.dt.float32, mybir.dt.float32r, mybir.dt.int32, mybir.dt.uint32)
ALU, ACT, AX = mybir.AluOpType, mybir.ActivationFunctionType, mybir.AxisListType

P = 128
S, D, E, H = 4096, 256, 8, 512
DC, HC = D // P, H // P
QB = 512
NB = S // QB
TB = QB // P
NT = S // P
NP2 = NT // 2
SCALE = 1.0 / float(np.sqrt(D))
EPS = 1e-5
LOW = -3.0e38
REGION = S + P
ZERO_TILE = E * REGION
ROW = D + 4
C_TOK, C_E1, C_GD, C_G2 = D, D + 1, D + 2, D + 3
FT = 2 * S // P + E
FU = 4
OUT_ROWS = S + P


def chunk0(qb, j):
    return 2 * qb * (qb + 1) + j * (qb + 1)


def moe_block(nc, x, wq, wk, wv, wo, wg, w1, b1, w2, b2, out):
    xg = nc.dram_tensor("xg_rows", (ZERO_TILE + P, ROW), F32, kind="Internal").ap()
    x_tiles = x[0].rearrange("(n p) d -> p n d", p=P)
    out_tiles = out.rearrange("(n p) d -> p n d", p=P)
    es = ExitStack()
    with es:
        def sb(name, shape, dt=F32, stack=es):
            return stack.enter_context(nc.sbuf_tensor(name, shape, dt))

        def sem(name):
            return es.enter_context(nc.semaphore(name))

        ident = sb("ident", [P, P])
        ones = sb("ones", [P, P])
        upper = sb("upper", [P, P])
        causal = sb("causal", [P, P])
        half_neg = sb("half_neg", [P, 2])
        iota_e = sb("iota_e", [P, E])
        lane = sb("lane", [P, 1])
        tok_ids = sb("tok_ids", [P, NT], I32)
        wg_sb = sb("wg_sb", [P, DC, E])
        cum = sb("cum", [P, E])
        pad_row = sb("pad_row", [P, ROW])
        tile_e = sb("tile_e", [P, FT])
        tab = sb("tab", [P, 2, FT], I32)
        ends = sb("ends", [P, 2, E])
        pad_slot = sb("pad_slot", [P, E], I32)
        tmpf = sb("tmpf", [P, 4, FT])
        iota_t = sb("iota_t", [P, FT])

        at = es.enter_context(ExitStack())
        A = lambda name, shape, dt=F32: sb(name, shape, dt, at)
        xt_hi, xt_lo = (A(n, [P, DC, S], F32R) for n in ("xt_hi", "xt_lo"))
        v_hi, v_lo = (A(n, [P, NT, D], F32R) for n in ("v_hi", "v_lo"))
        wa_hi, wa_lo, wb_hi, wb_lo = (A(n, [P, DC, D], F32R) for n in ("wa_hi", "wa_lo", "wb_hi", "wb_lo"))
        q_hi, q_lo = (A(n, [P, DC, QB], F32R) for n in ("q_hi", "q_lo"))
        s_sb = A("s_sb", [P, 2, S - QB])
        s_diag = A("s_diag", [P, 2, QB])
        probs = A("probs", [P, QB])
        pt_hi, pt_lo = (A(n, [P, TB, P], F32R) for n in ("pt_hi", "pt_lo"))
        x_in = A("x_in", [P, 2, 2, D])
        xn = A("xn", [P, 2, D])
        xs_hi, xs_lo = (A(n, [P, DC, 2 * P], F32R) for n in ("xs_hi", "xs_lo"))
        x_res = A("x_res", [P, 2, D])
        x1 = A("x1", [P, 2, D])
        rows = A("rows", [P, 4, ROW])
        x2t = A("x2t", [P, DC, P])
        stat = A("stat", [P, 2, 6])
        mv = A("mv", [P, 2, 2])
        rstd = A("rstd", [P, 2, 2])
        stat2 = A("stat2", [P, 6])
        mv2 = A("mv2", [P, 2, 2])
        rstd2 = A("rstd2", [P, 2, 2])
        run_max = A("run_max", [P, 2])
        neg_max = A("neg_max", [P, 2])
        sums = A("sums", [P, 2, 8])
        lsum = A("lsum", [P, 2])
        top = A("top", [P, 2, 8])
        top_i = A("top_i", [P, 2, 8], U32)
        top_f = A("top_f", [P, 2, 2])
        hot = A("hot", [P, 2, 2, E])
        mask = A("mask", [P, E])
        junk = A("junk", [P, 2, E])
        slot_f = A("slot_f", [P, 2, 2])
        slot_i = A("slot_i", [P, 4, 2], I32)
        ex = A("ex", [P, 2])
        den = A("den", [P, 3])
        raw = s_sb[:, 1, 0:4 * DC * D].rearrange("p (w c n) -> p w c n", w=4, c=DC)
        wot = s_sb[:, 1, 4 * DC * D:5 * DC * D].rearrange("p (c n) -> p c n", c=DC)
        at.close()

        ff = es.enter_context(ExitStack())
        B = lambda name, shape, dt=F32: sb(name, shape, dt, ff)
        w1_hi, w1_lo = (B(n, [P, E, DC, H], F32R) for n in ("w1_hi", "w1_lo"))
        w2_hi, w2_lo = (B(n, [P, E, HC, D], F32R) for n in ("w2_hi", "w2_lo"))
        w_raw = B("w_raw", [P, 2, 2, DC * H])
        b1_sb = B("b1_sb", [P, E, H])
        b2_sb = B("b2_sb", [P, E, D])
        xf = B("xf", [P, FU, ROW])
        fx_hi, fx_lo = (B(n, [P, 2, DC, P], F32R) for n in ("fx_hi", "fx_lo"))
        h_sb = B("h_sb", [P, 2, H])
        ht_hi, ht_lo = (B(n, [P, 2, HC, P], F32R) for n in ("ht_hi", "ht_lo"))
        y_b = B("y_b", [P, 2, D])
        y_sb = B("y_sb", [P, 2, D])
        gate = B("gate", [P, FU])
        gsel = B("gsel", [P, FU])
        dest = B("dest", [P, FU], I32)
        e_now = B("e_now", [P, FU])

        ps = es.enter_context(nc.psum_tensor("ps", [P, 8, 512], F32))
        ps_s = ps[:, 0, :]
        ps_pt = ps[:, 1:3, 0:2 * P]
        ps_o = ps[:, 3:5, 0:D]
        ps_x, ps_v, ps_r = ps[:, 5, :], ps[:, 6, :], ps[:, 7, :]

        consts_ready, wload, wstage_ps, wstage_sb, wstage_hi = map(
            sem, ("consts_ready", "wload", "wstage_ps", "wstage_sb", "wstage_hi"))
        x_loaded = [sem("x_loaded0"), sem("x_loaded1")]
        x_stats, x_stats1, x_rstd, x_normed = map(sem, ("x_stats", "x_stats1", "x_rstd", "x_normed"))
        xt_ps, xs_hi_done, xs_done = map(sem, ("xt_ps", "xs_hi_done", "xs_done"))
        xt_stored = [sem("xt_stored0"), sem("xt_stored1")]
        v_ps, v_hi_done, v_done = map(sem, ("v_ps", "v_hi_done", "v_done"))
        q_ps, q_hi_done, q_done = map(sem, ("q_ps", "q_hi_done", "q_done"))
        scores_ps, scores_saved, max_ready, probs_ready = map(
            sem, ("scores_ps", "scores_saved", "max_ready", "probs_ready"))
        pt_ps, pt_hi_done, pt_done, pv_done = map(sem, ("pt_ps", "pt_hi_done", "pt_done", "pv_done"))
        diag_part = sem("diag_part")
        res_loaded = [sem("res_loaded0"), sem("res_loaded1")]
        x1_chain, x1_done, x1_stats, rstd2_ready = map(sem, ("x1_chain", "x1_done", "x1_stats", "rstd2_ready"))
        x1_stored = [sem("x1_stored0"), sem("x1_stored1")]
        x2_ready, x2t_ps, x2t_sb, logits_ps = map(sem, ("x2_ready", "x2t_ps", "x2t_sb", "logits_ps"))
        top_chain, top_ready, hot_chain, hot_ready = map(sem, ("top_chain", "top_ready", "hot_chain", "hot_ready"))
        ex_ready, rank_ps, cum_ready, slot_chain, slots_ready = map(
            sem, ("ex_ready", "rank_ps", "cum_ready", "slot_chain", "slots_ready"))
        scattered = [sem(f"scattered{i}") for i in range(4)]
        pool_chain, x_eps, row_chain, row_ready = map(sem, ("pool_chain", "x_eps", "row_chain", "row_ready"))
        counts_ps, tab_chain, tab_ready = map(sem, ("counts_ps", "tab_chain", "tab_ready"))
        padded = sem("padded")
        fw_loaded = [sem("fw_loaded0"), sem("fw_loaded1")]
        fb_loaded, fw_hi_done, fw_done = map(sem, ("fb_loaded", "fw_hi_done", "fw_done"))
        xf_loaded = [sem(f"xf_loaded{i}") for i in range(FU)]
        fx_ps, fx_hi_done, fx_done = map(sem, ("fx_ps", "fx_hi_done", "fx_done"))
        h_ps, h_done, ht_ps, ht_hi_done, ht_done = map(sem, ("h_ps", "h_done", "ht_ps", "ht_hi_done", "ht_done"))
        y_ps, y_biased, y_done, added = map(sem, ("y_ps", "y_biased", "y_done", "added"))
        meta_chain, gate_ready = sem("meta_chain"), sem("gate_ready")
        block = es.enter_context(nc.Block())

        def over_blocks(eng, body):
            body(0)
            with eng.Fori(1, NB - 1) as qb:
                body(qb)
            body(NB - 1)

        def over_chunks(eng, qb, body):
            if isinstance(qb, int) and qb == 0:
                return
            with eng.Fori(0, qb) as kc:
                body(kc)

        def has_next(qb):
            return not (isinstance(qb, int) and qb == NB - 1)

        def tile(qb, j):
            return qb * TB + j

        def routed(qb, j, back):
            if isinstance(qb, int):
                t = tile(qb, j) - back
                return (t if t >= 0 else None), t % TB
            return tile(qb, j) - back, (j - back) % TB

        def apart(eng):
            eng.nop(nofuse=True)

        def to3(ap, n):
            return ap.rearrange("p (c n) -> p c n", n=n)

        @block.sync
        def _(sp):
            for n, w in enumerate((wq, wk, wv, wo)):
                sp.dma_start(raw[:, n], w.rearrange("(c p) n -> p c n", p=P)).then_inc(wload, 16)

            def load_pair(nb, k):
                if not (isinstance(nb, int) and nb == 0):
                    sp.wait_ge(x_normed, 2 * nb + k - 1)
                sp.dma_start(x_in[:, k], x_tiles[:, bass.ds(2 * (2 * nb + k), 2), :]).then_inc(x_loaded[k], 16)

            def load_residual(t, j):
                if not (isinstance(t, int) and t < 2):
                    sp.wait_ge(x1_done, t - 1)
                sp.dma_start(x_res[:, j % 2], x_tiles[:, bass.ds(t, 1), :].rearrange("p a d -> p (a d)")
                             ).then_inc(res_loaded[j % 2], 16)

            def store_xt(nb, k):
                sp.wait_ge(xs_done, 2 * nb + k + 1)
                at_tok = bass.ds((2 * nb + k) * 2 * P, 2 * P)
                sp.dma_start(xt_hi[:, :, at_tok].bitcast(F32), xs_hi[:].bitcast(F32)).then_inc(xt_stored[k], 16)
                sp.dma_start(xt_lo[:, :, at_tok].bitcast(F32), xs_lo[:].bitcast(F32)).then_inc(xt_stored[k], 16)

            def store_x1(t, j):
                sp.wait_ge(x1_done, t + 1)
                sp.dma_start(out_tiles[:, bass.ds(t, 1), :].rearrange("p a d -> p (a d)"), x1[:, j % 2]
                             ).then_inc(x1_stored[j % 2], 16)

            load_pair(0, 0)
            load_pair(0, 1)
            sp.dma_start(wg_sb[:], wg.rearrange("(c p) e -> p c e", p=P)).then_inc(wload, 16)
            load_residual(0, 0)
            store_xt(0, 0)
            store_xt(0, 1)

            def body(qb):
                nxt = has_next(qb)
                if nxt:
                    load_pair(qb + 1, 0)
                    load_pair(qb + 1, 1)
                for j in range(TB):
                    t1, j1 = routed(qb, j, 1)
                    if nxt and j in (1, 2):
                        store_xt(qb + 1, j - 1)
                    if t1 is not None:
                        store_x1(t1, j1)
                    if nxt or j < TB - 1:
                        load_residual(tile(qb, j) + 1, (j + 1) % TB)

            over_blocks(sp, body)
            store_x1(NT - 1, TB - 1)

            sp.wait_ge(pv_done, chunk0(NB, 0))
            sp.wait_ge(probs_ready, chunk0(NB, 0))
            sp.wait_ge(slots_ready, NT)
            for k in range(4):
                sp.wait_ge(scattered[k], 32 * (NT // 4) + (16 if k == 3 else 0))
            for k in range(2):
                sp.wait_ge(x1_stored[k], 16 * (NT // 2))
            for e in range(E):
                if e >= 2:
                    sp.wait_ge(fw_done, e - 1)
                sp.dma_start(w_raw[:, e % 2, 0].rearrange("p (c n) -> p c n", c=DC),
                             w1[e].rearrange("(c p) n -> p c n", p=P)).then_inc(fw_loaded[e % 2], 16)
                sp.dma_start(w_raw[:, e % 2, 1].rearrange("p (c n) -> p c n", c=HC),
                             w2[e].rearrange("(c p) n -> p c n", p=P)).then_inc(fw_loaded[e % 2], 16)
                if e == 1:
                    sp.dma_start(b1_sb[:], b1[None, :, :].to_broadcast([P, E, H])).then_inc(fb_loaded, 16)
                    sp.dma_start(b2_sb[:], b2[None, :, :].to_broadcast([P, E, D])).then_inc(fb_loaded, 16)
            sp.wait_ge(tab_ready, 1)
            sp.wait_ge(padded, 16 * E)

            def load_rows(t, u, first):
                if not first:
                    sp.wait_ge(fx_ps, t - FU + 1)
                    sp.wait_ge(gate_ready, t - FU + 1)
                row0 = sp.value_load(tab[0:1, 1, bass.ds(t, 1)], min_val=0, max_val=ZERO_TILE)
                sp.dma_start(xf[:, u, :], xg[bass.ds(row0, P), :]).then_inc(xf_loaded[u], 16)

            for u in range(FU):
                load_rows(u, u, True)
            with sp.Fori(1, FT // FU) as r:
                for u in range(FU):
                    load_rows(r * FU + u, u, False)
            sp.wait_ge(added, 16 * FT)

        @block.tensor
        def _(pe):
            def three(dst, pairs, start=True, stop=True, check=True):
                n = 3 * len(pairs)
                k = 0
                for (a_hi, a_lo), (b_hi, b_lo) in pairs:
                    for a, b in ((a_hi, b_hi), (a_hi, b_lo), (a_lo, b_hi)):
                        ins = nc.tensor.matmul(dst, a, b, start=start and k == 0, stop=stop and k == n - 1,
                                               skip_group_check=not check)
                        k += 1
                return ins

            pe.wait_ge(wload, 16 * 5)
            pe.wait_ge(consts_ready, 1)
            for ic in range(DC):
                for oc in range(DC):
                    ins = nc.tensor.matmul(ps_x[:, ic * D:(ic + 1) * D], raw[:, 0, oc, ic * P:(ic + 1) * P],
                                           raw[:, 1, oc, :], start=(oc == 0), stop=(oc == DC - 1))
            ins.then_inc(wstage_ps, 1)
            for oc in range(DC):
                for cc in range(DC):
                    ins = nc.tensor.transpose(ps_v[:, oc * D + cc * P:oc * D + (cc + 1) * P],
                                              raw[:, 3, cc, oc * P:(oc + 1) * P], ident[:])
            ins.then_inc(wstage_ps, 1)
            pe.wait_ge(wstage_sb, 2)
            for dc in range(DC):
                for oc in range(DC):
                    ins = nc.tensor.matmul(ps_x[:, dc * D:(dc + 1) * D], raw[:, 2, oc, dc * P:(dc + 1) * P],
                                           wot[:, oc, :], start=(oc == 0), stop=(oc == DC - 1))
            ins.then_inc(wstage_ps, 1)

            def transpose_pair(nb, k):
                p = 2 * nb + k
                pe.wait_ge(x_normed, p + 1)
                if isinstance(nb, int) and nb == 0:
                    pe.wait_ge(wstage_sb, 3) if k == 0 else pe.wait_ge(xs_done, p)
                else:
                    pe.wait_ge(q_done, 2 * nb) if k == 0 else pe.wait_ge(xs_done, p)
                for c in range(DC):
                    for a in range(2):
                        ins = nc.tensor.transpose(ps_x[:, c * 2 * P + a * P:c * 2 * P + (a + 1) * P],
                                                  xn[:, a, c * P:(c + 1) * P], ident[:])
                ins.then_inc(xt_ps, 1)

            def values(nb, k):
                p = 2 * nb + k
                pe.wait_ge(xs_done, p + 1)
                if k == 1:
                    pe.wait_ge(v_done, p)
                elif not (isinstance(nb, int) and nb == 0):
                    pe.wait_ge(q_done, 2 * nb)
                for a in range(2):
                    tok = slice(a * P, (a + 1) * P)
                    ins = three(ps_v[:, a * D:(a + 1) * D],
                                [((xs_hi[:, c, tok], xs_lo[:, c, tok]), (wb_hi[:, c], wb_lo[:, c]))
                                 for c in range(DC)])
                ins.then_inc(v_ps, 1)

            def queries_first(nb):
                pe.wait_ge(xt_stored[0], 32 * (nb + 1))
                pe.wait_ge(xs_done, 2 * nb + 2)
                tok = bass.ds(nb * QB, P)
                for m in range(DC):
                    col = slice(m * P, (m + 1) * P)
                    ins = three(ps_x[:, m * P:(m + 1) * P],
                                [((wa_hi[:, c, col], wa_lo[:, c, col]), (xt_hi[:, c, tok], xt_lo[:, c, tok]))
                                 for c in range(DC)])
                ins.then_inc(q_ps, 1)

            def queries_rest(nb):
                pe.wait_ge(xt_stored[1], 32 * (nb + 1))
                pe.wait_ge(q_done, 2 * nb + 1)
                pe.wait_ge(v_done, 2 * nb + 2)
                tok = bass.ds(nb * QB + P, QB - P)
                for m, bank in enumerate((ps_x, ps_v)):
                    col = slice(m * P, (m + 1) * P)
                    ins = three(bank[:, 0:QB - P],
                                [((wa_hi[:, c, col], wa_lo[:, c, col]), (xt_hi[:, c, tok], xt_lo[:, c, tok]))
                                 for c in range(DC)])
                ins.then_inc(q_ps, 1)

            def scores(n, j, key0, width):
                if not (isinstance(n, int) and n == 0):
                    pe.wait_ge(scores_saved, n)
                q = slice(j * P, (j + 1) * P)
                keys = bass.ds(key0, width)
                three(ps_s[:, 0:width], [((q_hi[:, c, q], q_lo[:, c, q]), (xt_hi[:, c, keys], xt_lo[:, c, keys]))
                                         for c in range(DC)]).then_inc(scores_ps, 1)

            def transpose_probs(n, blocks):
                pe.wait_ge(probs_ready, n + 1)
                for b in range(blocks):
                    ins = nc.tensor.transpose(ps_pt[:, b // 2, (b % 2) * P:(b % 2 + 1) * P],
                                              probs[:, b * P:(b + 1) * P], ident[:])
                    if b == blocks - 1:
                        ins.then_inc(pt_ps, 2 if blocks <= 2 else 1)
                    elif b == 1:
                        ins.then_inc(pt_ps, 1)

            def weigh_values(n, j, blocks, v0, first):
                for b in range(blocks):
                    if b == 0:
                        pe.wait_ge(pt_done, 2 * n + (1 if blocks > 2 else 2))
                    if b == 2:
                        pe.wait_ge(pt_done, 2 * n + 2)
                    ins = three(ps_o[:, j % 2], [((pt_hi[:, b], pt_lo[:, b]),
                                                  (v_hi[:, v0 + b] if isinstance(v0, int) else
                                                   v_hi[:, bass.ds(v0 + b, 1), :].rearrange("p a d -> p (a d)"),
                                                   v_lo[:, v0 + b] if isinstance(v0, int) else
                                                   v_lo[:, bass.ds(v0 + b, 1), :].rearrange("p a d -> p (a d)")))],
                                start=first and b == 0, stop=b == blocks - 1, check=False)
                ins.then_inc(pv_done, 1)

            def transpose_x2(t, j):
                pe.wait_ge(x2_ready, t + 1)
                for c in range(DC):
                    ins = nc.tensor.transpose(ps_r[:, c * P:(c + 1) * P], rows[:, j, c * P:(c + 1) * P], ident[:])
                ins.then_inc(x2t_ps, 1)

            def logits(t):
                pe.wait_ge(x2t_sb, t + 1)
                for c in range(DC):
                    ins = nc.tensor.matmul(ps_r[:, D:D + E], x2t[:, c], wg_sb[:, c], start=(c == 0), stop=(c == DC - 1))
                ins.then_inc(logits_ps, 1)

            def rank(t):
                pe.wait_ge(hot_ready, t + 1)
                nc.tensor.matmul(ps_r[:, D + 16:D + 16 + E], upper[:], mask[:], start=True, stop=False)
                nc.tensor.matmul(ps_r[:, D + 16:D + 16 + E], ones[:], cum[:], start=False, stop=True
                                 ).then_inc(rank_ps, 1)

            def routing(qb, j):
                t2, j2 = routed(qb, j, 2)
                t3, _ = routed(qb, j, 3)
                t4, _ = routed(qb, j, 4)
                t5, _ = routed(qb, j, 5)
                if t3 is not None and (not isinstance(t3, int) or t3 < NT):
                    pe.wait_ge(x2t_sb, t3 + 1)
                if t4 is not None:
                    pe.wait_ge(top_ready, t4 + 1)
                if t5 is not None:
                    pe.wait_ge(slots_ready, t5 + 1)
                if t4 is not None:
                    rank(t4)
                if t3 is not None and (not isinstance(t3, int) or t3 < NT):
                    logits(t3)
                if t2 is not None and (not isinstance(t2, int) or t2 < NT):
                    transpose_x2(t2, j2)

            pe.wait_ge(wstage_sb, 3)
            transpose_pair(0, 0)
            values(0, 0)
            transpose_pair(0, 1)
            values(0, 1)
            queries_first(0)
            queries_rest(0)
            pe.wait_ge(q_done, 1)
            scores(0, 0, 0, P)

            def body(qb):
                nxt = has_next(qb)
                for j in range(TB):
                    t, n0, n1 = tile(qb, j), chunk0(qb, j), chunk0(qb, j) + qb + 1
                    if nxt and j == 2:
                        values(qb + 1, 0)
                        transpose_pair(qb + 1, 1)
                    if nxt and j == 3:
                        values(qb + 1, 1)
                    routing(qb, j)
                    if nxt and j == 1:
                        transpose_pair(qb + 1, 0)
                    transpose_probs(n0, j + 1)
                    if j < TB - 1:
                        pe.wait_ge(q_done, 2 * qb + 2)
                        scores(n1, j + 1, qb * QB, (j + 2) * P)
                    elif nxt:
                        pe.wait_ge(q_done, 2 * (qb + 1) + 1)
                        scores(n1, 0, (qb + 1) * QB, P)
                        scores(n1 + 1, 0, qb * QB, QB)
                    pe.wait_ge(v_done, 2 * (qb + 1))
                    if not (isinstance(t, int) and t < 2):
                        pe.wait_ge(x1_done, t - 1)
                    weigh_values(n0, j, j + 1, qb * TB, True)

                    def chunk(kc):
                        transpose_probs(n0 + 1 + kc, TB)
                        if j < TB - 1:
                            scores(n1 + 1 + kc, j + 1, kc * QB, QB)
                        elif nxt:
                            scores(n1 + 2 + kc, 0, kc * QB, QB)
                        weigh_values(n0 + 1 + kc, j, TB, kc * TB, False)

                    over_chunks(pe, qb, chunk)
                    if nxt and j == 2:
                        queries_first(qb + 1)
                    if nxt and j == 3:
                        queries_rest(qb + 1)

            over_blocks(pe, body)
            for j in range(4):
                routing(NB, j)

            pe.wait_ge(cum_ready, NT)
            pe.wait_ge(slots_ready, NT)
            nc.tensor.matmul(ps_r[:, 0:E], ones[:], cum[:], start=True, stop=True).then_inc(counts_ps, 1)

            pe.wait_ge(tab_ready, 1)

            def transpose_rows(t, u, early):
                pe.wait_ge(xf_loaded[u], 16 * (t // FU + 1) if isinstance(t, int) else 16 * early)
                if not (isinstance(t, int) and t < 2):
                    pe.wait_ge(fx_done, t - 1)
                for c in range(DC):
                    ins = nc.tensor.transpose(ps[:, 2 + u % 2, c * P:(c + 1) * P], xf[:, u, c * P:(c + 1) * P], ident[:])
                ins.then_inc(fx_ps, 1)

            def up(t, u, e):
                pe.wait_ge(fx_done, t + 1)
                if not (isinstance(t, int) and t < 2):
                    pe.wait_ge(h_done, t - 1)
                w = lambda m, c: m[:, bass.ds(e, 1), c, :].rearrange("p a n -> p (a n)")
                three(ps[:, u % 2, :], [((fx_hi[:, u % 2, c], fx_lo[:, u % 2, c]), (w(w1_hi, c), w(w1_lo, c)))
                                        for c in range(DC)]).then_inc(h_ps, 1)

            def down(t, u, e):
                pe.wait_ge(ht_done, t + 1)
                if not (isinstance(t, int) and t < 2):
                    pe.wait_ge(y_biased, t - 1)
                w = lambda m, c: m[:, bass.ds(e, 1), c, :].rearrange("p a n -> p (a n)")
                three(ps[:, 6 + u % 2, 0:D], [((ht_hi[:, u % 2, c], ht_lo[:, u % 2, c]), (w(w2_hi, c), w(w2_lo, c)))
                                              for c in range(HC)]).then_inc(y_ps, 1)

            def transpose_h(t, u):
                pe.wait_ge(h_done, t + 1)
                if not (isinstance(t, int) and t < 2):
                    pe.wait_ge(ht_done, t - 1)
                for c in range(HC):
                    ins = nc.tensor.transpose(ps[:, 4 + u % 2, c * P:(c + 1) * P], h_sb[:, u % 2, c * P:(c + 1) * P], ident[:])
                ins.then_inc(ht_ps, 1)

            transpose_rows(0, 0, 1)
            pe.wait_ge(fw_done, E)

            def turn(t, u, r):
                e = pe.value_load(tab[0:1, 0, bass.ds(t, 1)], min_val=0, max_val=E - 1)
                up(t, u, e)
                if not (isinstance(t, int) and t == FT - 1):
                    transpose_rows(t + 1, (u + 1) % FU, r + 1 if u < FU - 1 else r + 2)
                if not (isinstance(t, int) and t == 0):
                    e_last = pe.value_load(tab[0:1, 0, bass.ds(t - 1, 1)], min_val=0, max_val=E - 1)
                    down(t - 1, (u - 1) % FU, e_last)
                transpose_h(t, u)

            for u in range(FU):
                turn(u, u, 0)
            with pe.Fori(1, FT // FU - 1) as r:
                for u in range(FU):
                    turn(r * FU + u, u, r)
            for u in range(FU):
                turn(FT - FU + u, u, FT // FU - 1)
            e = pe.value_load(tab[0:1, 0, FT - 1:FT], min_val=0, max_val=E - 1)
            down(FT - 1, FU - 1, e)

        @block.scalar
        def _(act):
            copy = nc.scalar.copy
            act.wait_ge(wstage_ps, 1)
            copy(wa_hi[:].rearrange("p c n -> p (c n)"), ps_x[:]).then_inc(wstage_hi, 1)
            act.wait_ge(wstage_ps, 2)
            copy(wot.rearrange("p c n -> p (c n)"), ps_v[:]).then_inc(wstage_sb, 1)
            act.wait_ge(wstage_ps, 3)
            copy(wb_hi[:].rearrange("p c n -> p (c n)"), ps_x[:]).then_inc(wstage_hi, 1)

            def xs_high(nb, k):
                p = 2 * nb + k
                act.wait_ge(xt_ps, p + 1)
                if k == 1:
                    act.wait_ge(v_ps, p)
                    act.wait_ge(xt_stored[0], 32 * (nb + 1))
                elif not (isinstance(nb, int) and nb == 0):
                    act.wait_ge(v_ps, p)
                    act.wait_ge(xt_stored[1], 32 * nb)
                copy(xs_hi[:].rearrange("p c n -> p (c n)"), ps_x[:]).then_inc(xs_hi_done, 1)

            def v_high(nb, k):
                p = 2 * nb + k
                act.wait_ge(v_ps, p + 1)
                copy(v_hi[:, bass.ds(2 * p, 2), :], to3(ps_v, D)).then_inc(v_hi_done, 1)

            def q_high_first(nb):
                act.wait_ge(q_ps, 2 * nb + 1)
                copy(q_hi[:, :, 0:P], to3(ps_x[:, 0:DC * P], P)).then_inc(q_hi_done, 1)

            def q_high_rest(nb):
                act.wait_ge(q_ps, 2 * nb + 2)
                copy(q_hi[:, 0, P:QB], ps_x[:, 0:QB - P])
                copy(q_hi[:, 1, P:QB], ps_v[:, 0:QB - P]).then_inc(q_hi_done, 1)

            def exps(n, j, src, width, col):
                if not (isinstance(n, int) and n == 0):
                    act.wait_ge(pt_ps, 2 * n)
                apart(act)
                nc.scalar.activation(probs[:, 0:width], src, ACT.Exp, bias=neg_max[:, j % 2:j % 2 + 1],
                                     scale=SCALE, accum_out=sums[:, j % 2, col]).then_inc(probs_ready, 1)

            def pt_high(n, blocks):
                if not (isinstance(n, int) and n == 0):
                    act.wait_ge(pv_done, n)
                act.wait_ge(pt_ps, 2 * n + (1 if blocks > 2 else 2))
                w = min(blocks, 2)
                copy(pt_hi[:, 0:w], to3(ps_pt[:, 0, 0:w * P], P)).then_inc(pt_hi_done, 1 if blocks > 2 else 2)
                if blocks > 2:
                    act.wait_ge(pt_ps, 2 * n + 2)
                    w = blocks - 2
                    copy(pt_hi[:, 2:2 + w], to3(ps_pt[:, 1, 0:w * P], P)).then_inc(pt_hi_done, 1)

            def routing(qb, j):
                t2, _ = routed(qb, j, 2)
                if t2 is not None and (not isinstance(t2, int) or t2 < NT):
                    act.wait_ge(x2t_ps, t2 + 1)
                    if not (isinstance(t2, int) and t2 == 0):
                        act.wait_ge(logits_ps, t2)
                    copy(x2t[:].rearrange("p c n -> p (c n)"), ps_r[:, 0:D]).then_inc(x2t_sb, 1)

            def gate_exp(qb, j):
                t3, j3 = routed(qb, j, 3)
                if t3 is not None and (not isinstance(t3, int) or t3 < NT):
                    act.wait_ge(top_ready, t3 + 1)
                    k = j3 % 2
                    if not (isinstance(t3, int) and t3 < 2):
                        act.wait_ge(row_ready, t3 - 1)
                    nc.scalar.activation(ex[:, k:k + 1], top[:, k, 0:1], ACT.Exp, bias=top[:, k, 1:2],
                                         scale=-1.0).then_inc(ex_ready, 1)

            xs_high(0, 0)
            v_high(0, 0)
            xs_high(0, 1)
            v_high(0, 1)
            q_high_first(0)
            q_high_rest(0)
            act.wait_ge(consts_ready, 1)

            def diagonal_exps(qb, j):
                act.wait_ge(max_ready, tile(qb, j) + 1)
                if not (isinstance(qb, int) and qb == 0 and j < 2):
                    act.wait_ge(x1_done, tile(qb, j) - 1)
                exps(chunk0(qb, j), j, s_diag[:, j % 2, 0:(j + 1) * P], (j + 1) * P, slice(7, 8))

            diagonal_exps(0, 0)

            def body(qb):
                nxt = has_next(qb)
                for j in range(TB):
                    n0 = chunk0(qb, j)
                    pt_high(n0, j + 1)
                    routing(qb, j)
                    if nxt and j == 1:
                        xs_high(qb + 1, 0)
                    if nxt and j == 2:
                        v_high(qb + 1, 0)
                        xs_high(qb + 1, 1)
                    if nxt and j == 3:
                        v_high(qb + 1, 1)

                    def chunk(kc):
                        exps(n0 + 1 + kc, j, s_sb[:, j % 2, bass.ds(kc * QB, QB)], QB, bass.ds(kc, 1))
                        pt_high(n0 + 1 + kc, TB)

                    over_chunks(act, qb, chunk)
                    if j < TB - 1:
                        diagonal_exps(qb, j + 1)
                    elif nxt:
                        diagonal_exps(qb + 1, 0)
                    if nxt and j == 2:
                        q_high_first(qb + 1)
                    if nxt and j == 3:
                        q_high_rest(qb + 1)
                    gate_exp(qb, j)

            over_blocks(act, body)
            for j in range(3):
                routing(NB, j)
                gate_exp(NB, j)

            for e in range(E):
                act.wait_ge(fw_loaded[e % 2], 32 * (e // 2 + 1))
                copy(w1_hi[:, e].rearrange("p c n -> p (c n)"), w_raw[:, e % 2, 0])
                copy(w2_hi[:, e].rearrange("p c n -> p (c n)"), w_raw[:, e % 2, 1]).then_inc(fw_hi_done, 1)

            def fx_high(t, u):
                act.wait_ge(fx_ps, t + 1)
                if not (isinstance(t, int) and t < 2):
                    act.wait_ge(h_ps, t - 1)
                copy(fx_hi[:, u % 2].rearrange("p c n -> p (c n)"), ps[:, 2 + u % 2, 0:D]).then_inc(fx_hi_done, 1)

            def ht_high(t, u):
                act.wait_ge(ht_ps, t + 1)
                if not (isinstance(t, int) and t < 2):
                    act.wait_ge(y_ps, t - 1)
                nc.scalar.activation(ht_hi[:, u % 2].rearrange("p c n -> p (c n)"), ps[:, 4 + u % 2, :], ACT.Relu
                                     ).then_inc(ht_hi_done, 1)

            def y_gated(t, u):
                act.wait_ge(y_biased, t + 1)
                act.wait_ge(gate_ready, t + 1)
                if not (isinstance(t, int) and t < 2):
                    act.wait_ge(added, 16 * (t - 1))
                nc.scalar.activation(y_sb[:, u % 2], y_b[:, u % 2], ACT.Copy, scale=gate[:, u:u + 1]).then_inc(y_done, 1)

            fx_high(0, 0)

            def turn(t, u):
                if not (isinstance(t, int) and t == FT - 1):
                    fx_high(t + 1, (u + 1) % FU)
                ht_high(t, u)
                if not (isinstance(t, int) and t == 0):
                    y_gated(t - 1, (u - 1) % FU)

            for u in range(FU):
                turn(u, u)
            with act.Fori(1, FT // FU - 1) as r:
                for u in range(FU):
                    turn(r * FU + u, u)
            for u in range(FU):
                turn(FT - FU + u, u)
            y_gated(FT - 1, FU - 1)

        @block.vector
        def _(dve):
            V = nc.vector

            def low(dst, src, high):
                return V.tensor_tensor(dst, src, high.bitcast(F32), ALU.subtract)

            dve.wait_ge(wstage_hi, 1)
            low(wa_lo[:].rearrange("p c n -> p (c n)"), ps_x[:], wa_hi[:].rearrange("p c n -> p (c n)")
                ).then_inc(wstage_sb, 1)

            def x_statistics(nb, k):
                p = 2 * nb + k
                dve.wait_ge(x_loaded[k], 16 * (nb + 1))
                for a in range(2):
                    V.bn_stats(stat[:, a], x_in[:, k, a]).then_inc(x_stats1, 1)
                dve.wait_ge(x_stats1, 2 * p + 2)
                if not (isinstance(nb, int) and nb == 0 and k == 0):
                    dve.wait_ge(x_rstd, p)
                apart(dve)
                for a in range(2):
                    ins = V.bn_aggr(mv[:, a], stat[:, a])
                ins.then_inc(x_stats, 1)

            def x_normalise(nb, k):
                p = 2 * nb + k
                dve.wait_ge(x_rstd, p + 1)
                if not (isinstance(nb, int) and nb == 0 and k == 0):
                    dve.wait_ge(xt_ps, p)
                for a in range(2):
                    ins = V.tensor_scalar(xn[:, a], x_in[:, k, a], mv[:, a, 0:1], rstd[:, a, 1:2],
                                          ALU.subtract, ALU.mult)
                ins.then_inc(x_normed, 1)

            def xs_low(nb, k):
                p = 2 * nb + k
                dve.wait_ge(xs_hi_done, p + 1)
                low(xs_lo[:].rearrange("p c n -> p (c n)"), ps_x[:], xs_hi[:].rearrange("p c n -> p (c n)")
                    ).then_inc(xs_done, 1)

            def v_low(nb, k):
                p = 2 * nb + k
                dve.wait_ge(v_hi_done, p + 1)
                pair = bass.ds(2 * p, 2)
                low(v_lo[:, pair, :], to3(ps_v, D), v_hi[:, pair, :]).then_inc(v_done, 1)

            def q_low_first(nb):
                dve.wait_ge(q_hi_done, 2 * nb + 1)
                low(q_lo[:, :, 0:P], to3(ps_x[:, 0:DC * P], P), q_hi[:, :, 0:P]).then_inc(q_done, 1)

            def q_low_rest(nb):
                dve.wait_ge(q_hi_done, 2 * nb + 2)
                low(q_lo[:, 0, P:QB], ps_x[:, 0:QB - P], q_hi[:, 0, P:QB])
                low(q_lo[:, 1, P:QB], ps_v[:, 0:QB - P], q_hi[:, 1, P:QB]).then_inc(q_done, 1)

            def save_diagonal(n, qb, j):
                dve.wait_ge(scores_ps, n + 1)
                if not (isinstance(n, int) and n <= 1):
                    dve.wait_ge(probs_ready, chunk0(qb, j - 1) if j else chunk0(qb - 1, TB - 1))
                m = run_max[:, j % 2:j % 2 + 1]
                if j:
                    V.tensor_scalar(s_diag[:, j % 2, 0:j * P], ps_s[:, 0:j * P], 1.0, LOW, ALU.mult,
                                    ALU.max, accum_out=m).then_inc(diag_part, 1)
                    dve.wait_ge(diag_part, qb * (TB - 1) + j)
                apart(dve)
                V.tensor_tensor_reduce(s_diag[:, j % 2, j * P:(j + 1) * P], ps_s[:, j * P:(j + 1) * P], causal[:],
                                       1.0, m if j else LOW, ALU.add, ALU.max, m).then_inc(scores_saved, 1)

            def save_scores(n, j, key0):
                dve.wait_ge(scores_ps, n + 1)
                dve.wait_ge(scores_saved, n)
                m = run_max[:, j % 2:j % 2 + 1]
                V.tensor_scalar(s_sb[:, j % 2, bass.ds(key0, QB)], ps_s[:], 1.0, m, ALU.mult, ALU.max,
                                accum_out=m).then_inc(scores_saved, 1)

            def negate_max(t, j, n):
                dve.wait_ge(scores_saved, n)
                V.tensor_scalar(neg_max[:, j % 2:j % 2 + 1], run_max[:, j % 2:j % 2 + 1], -SCALE, None, ALU.mult
                                ).then_inc(max_ready, 1)

            def pt_low(n, blocks):
                dve.wait_ge(pt_hi_done, 2 * n + (1 if blocks > 2 else 2))
                w = min(blocks, 2)
                low(pt_lo[:, 0:w], to3(ps_pt[:, 0, 0:w * P], P), pt_hi[:, 0:w]).then_inc(pt_done, 1 if blocks > 2 else 2)
                if blocks > 2:
                    dve.wait_ge(pt_hi_done, 2 * n + 2)
                    w = blocks - 2
                    low(pt_lo[:, 2:2 + w], to3(ps_pt[:, 1, 0:w * P], P), pt_hi[:, 2:2 + w]).then_inc(pt_done, 1)

            def attention_out(t, j, n_end, half):
                k = j % 2
                dve.wait_ge(probs_ready, n_end)
                V.tensor_reduce(lsum[:, 0:1], sums[:, k, :], AX.X, ALU.add).then_inc(x1_chain, 1)
                dve.wait_ge(x1_chain, 4 * t + 1)
                V.reciprocal(lsum[:, 1:2], lsum[:, 0:1]).then_inc(x1_chain, 1)
                dve.wait_ge(x1_chain, 4 * t + 2)
                dve.wait_ge(res_loaded[k], 16 * half)
                if not (isinstance(t, int) and t < 2):
                    dve.wait_ge(x1_stored[k], 16 * (half - 1))
                dve.wait_ge(pv_done, n_end)
                V.scalar_tensor_tensor(x1[:, k], ps_o[:, k], lsum[:, 1:2], x_res[:, k], ALU.mult, ALU.add
                                       ).then_inc(x1_done, 1)
                dve.wait_ge(x1_done, t + 1)
                V.bn_stats(stat2[:], x1[:, k]).then_inc(x1_chain, 1)
                dve.wait_ge(x1_chain, 4 * t + 3)
                apart(dve)
                V.bn_aggr(mv2[:, k], stat2[:]).then_inc(x1_chain, 1)
                dve.wait_ge(x1_chain, 4 * t + 4)
                V.tensor_scalar(rstd2[:, k, 0:1], mv2[:, k, 1:2], EPS, None, ALU.add).then_inc(x1_stats, 1)

            def x2_normalise(t, j, turn4):
                k = j % 2
                dve.wait_ge(rstd2_ready, t + 1)
                if not (isinstance(t, int) and t < 4):
                    dve.wait_ge(scattered[j], 32 * turn4 + (16 if j == 3 else 0))
                V.tensor_scalar(rows[:, j, 0:D], x1[:, k], mv2[:, k, 0:1], rstd2[:, k, 1:2], ALU.subtract, ALU.mult
                                ).then_inc(x2_ready, 1)

            def choose(t, j):
                k = j % 2
                dve.wait_ge(logits_ps, t + 1)
                if not (isinstance(t, int) and t < 2):
                    dve.wait_ge(hot_ready, t - 1)
                apart(dve)
                V.max(top[:, k], ps_r[:, D:D + E]).then_inc(top_chain, 1)
                dve.wait_ge(top_chain, t + 1)
                apart(dve)
                V.max_index(top_i[:, k], top[:, k], ps_r[:, D:D + E]).then_inc(top_ready, 1)

            def slots(t, j):
                k = j % 2
                dve.wait_ge(rank_ps, t + 1)
                dve.wait_ge(ex_ready, t + 1)
                if not (isinstance(t, int) and t < 2):
                    dve.wait_ge(row_ready, t - 1)
                for c in range(2):
                    V.tensor_tensor_reduce(junk[:, c], ps_r[:, D + 16:D + 16 + E], hot[:, k, c], 1.0, 0.0, ALU.mult,
                                           ALU.add, slot_f[:, k, c:c + 1])
                V.tensor_scalar(den[:, 0:1], ex[:, k:k + 1], 1.0, None, ALU.add).then_inc(slot_chain, 1)
                dve.wait_ge(slot_chain, t + 1)
                V.reciprocal(den[:, 1 + k:2 + k], den[:, 0:1]).then_inc(slots_ready, 1)

            def routing(qb, j):
                t2, _ = routed(qb, j, 2)
                t3, j3 = routed(qb, j, 3)
                t4, j4 = routed(qb, j, 4)
                live = lambda t: t is not None and (not isinstance(t, int) or t < NT)
                if live(t2) and live(t3):
                    dve.wait_ge(x2t_sb, t2 + 1)
                if live(t3):
                    choose(t3, j3)
                if t4 is not None:
                    slots(t4, j4)

            def t1_half(qb, j):
                return 2 * qb + (j - 1) // 2 + 1

            x_statistics(0, 0)
            x_normalise(0, 0)
            dve.wait_ge(wstage_hi, 2)
            low(wb_lo[:].rearrange("p c n -> p (c n)"), ps_x[:], wb_hi[:].rearrange("p c n -> p (c n)")
                ).then_inc(wstage_sb, 1)
            x_statistics(0, 1)
            xs_low(0, 0)
            x_normalise(0, 1)
            v_low(0, 0)
            xs_low(0, 1)
            v_low(0, 1)
            q_low_first(0)
            q_low_rest(0)
            dve.wait_ge(consts_ready, 1)
            save_diagonal(0, 0, 0)
            negate_max(0, 0, 1)

            def body(qb):
                nxt = has_next(qb)
                for j in range(TB):
                    t, n0, n1 = tile(qb, j), chunk0(qb, j), chunk0(qb, j) + qb + 1
                    t1, j1 = routed(qb, j, 1)
                    pt_low(n0, j + 1)
                    if j < TB - 1:
                        save_diagonal(n1, qb, j + 1)
                    elif nxt:
                        save_diagonal(n1, qb + 1, 0)
                        save_scores(n1 + 1, 0, qb * QB)
                    if nxt and j == 0:
                        x_statistics(qb + 1, 0)
                    if nxt and j == 1:
                        xs_low(qb + 1, 0)
                    if nxt and j == 2:
                        v_low(qb + 1, 0)
                        xs_low(qb + 1, 1)
                    if nxt and j == 3:
                        v_low(qb + 1, 1)

                    def chunk(kc):
                        pt_low(n0 + 1 + kc, TB)
                        if j < TB - 1:
                            save_scores(n1 + 1 + kc, j + 1, kc * QB)
                        elif nxt:
                            save_scores(n1 + 2 + kc, 0, kc * QB)

                    if not (isinstance(qb, int) and qb == 0):
                        chunk(0)
                    routing(qb, j)
                    if t1 is not None:
                        attention_out(t1, j1, n0, t1_half(qb, j))
                    if nxt and j == 1:
                        x_normalise(qb + 1, 1)
                    if not (isinstance(qb, int) and qb <= 1):
                        with dve.Fori(1, qb) as kc:
                            chunk(kc)
                    if j < TB - 1:
                        negate_max(t + 1, j + 1, n1 + qb + 1)
                    elif nxt:
                        negate_max(t + 1, 0, n1 + qb + 2)
                    if t1 is not None:
                        x2_normalise(t1, j1, qb if j >= 1 else qb - 1)
                    if nxt and j == 0:
                        x_normalise(qb + 1, 0)
                        x_statistics(qb + 1, 1)
                    if nxt and j == 2:
                        q_low_first(qb + 1)
                    if nxt and j == 3:
                        q_low_rest(qb + 1)

            body(0)
            body(1)
            with dve.Fori(2, NB - 1) as qb:
                body(qb)
            body(NB - 1)
            attention_out(NT - 1, TB - 1, chunk0(NB, 0), NT // 2)
            x2_normalise(NT - 1, TB - 1, NB - 1)
            for j in range(4):
                routing(NB, j)

            link_n = [0]

            def link(ins):
                link_n[0] += 1
                ins.then_inc(tab_chain, 1)
                dve.wait_ge(tab_chain, link_n[0])

            dve.wait_ge(counts_ps, 1)
            link(V.tensor_scalar(tmpf[:, 0, 0:E], ps_r[:, 0:E], lane[:, 0:1], None, ALU.add))
            V.tensor_copy(pad_slot[:], tmpf[:, 0, 0:E]).then_inc(tab_ready, 1)
            link(V.scalar_tensor_tensor(tmpf[:, 1, 0:E], iota_e[:], -float(REGION), ps_r[:, 0:E], ALU.mult, ALU.add))
            link(V.tensor_scalar(tmpf[:, 2, 0:E], tmpf[:, 1, 0:E], 1.0 / P, (P - 1.0) / P - 127.5 / 256, ALU.mult, ALU.add))
            link(V.tensor_copy(tab[:, 0, 0:E], tmpf[:, 2, 0:E]))
            link(V.tensor_copy(ends[:, 0], tab[:, 0, 0:E]))
            link(V.tensor_tensor_scan(ends[:, 1], ones[:, 0:E], ends[:, 0], 0.0, ALU.mult, ALU.add))
            link(V.memset(tmpf[:, 0:2, :], 0.0))
            for e in range(E):
                V.tensor_scalar(tmpf[:, 2, :], iota_t[:], ends[:, 1, e:e + 1], None, ALU.is_ge)
                link(V.scalar_tensor_tensor(tmpf[:, 0, :], iota_t[:], ends[:, 1, e:e + 1], tmpf[:, 0, :], ALU.is_ge, ALU.add))
                link(V.scalar_tensor_tensor(tmpf[:, 1, :], tmpf[:, 2, :], ends[:, 0, e:e + 1], tmpf[:, 1, :], ALU.mult, ALU.add))
            link(V.tensor_tensor(tmpf[:, 2, :], iota_t[:], tmpf[:, 1, :], ALU.subtract))
            link(V.tensor_scalar(tmpf[:, 2, :], tmpf[:, 2, :], float(P), None, ALU.mult))
            link(V.scalar_tensor_tensor(tmpf[:, 2, :], tmpf[:, 0, :], float(REGION), tmpf[:, 2, :], ALU.mult, ALU.add))
            link(V.tensor_scalar(tmpf[:, 2, :], tmpf[:, 2, :], float(ZERO_TILE), None, ALU.min))
            link(V.tensor_scalar(tile_e[:], tmpf[:, 0, :], E - 1.0, None, ALU.min))
            link(V.tensor_copy(tab[:, 1, :], tmpf[:, 2, :]))
            link(V.tensor_copy(tab[:, 0, :], tile_e[:]))
            V.tensor_copy(tmpf[:, 3, 0:1], tile_e[:, 0:1]).then_inc(tab_ready, 1)

            for e in range(E):
                dve.wait_ge(fw_hi_done, e + 1)
                V.tensor_tensor(w1_lo[:, e].rearrange("p c n -> p (c n)"), w_raw[:, e % 2, 0],
                                w1_hi[:, e].rearrange("p c n -> p (c n)").bitcast(F32), ALU.subtract)
                V.tensor_tensor(w2_lo[:, e].rearrange("p c n -> p (c n)"), w_raw[:, e % 2, 1],
                                w2_hi[:, e].rearrange("p c n -> p (c n)").bitcast(F32), ALU.subtract).then_inc(fw_done, 1)
            dve.wait_ge(fb_loaded, 32)

            def add_b1(t, u, e):
                dve.wait_ge(h_ps, t + 1)
                if not (isinstance(t, int) and t < 2):
                    dve.wait_ge(ht_ps, t - 1)
                V.tensor_tensor(h_sb[:, u % 2], ps[:, u % 2, :],
                                b1_sb[:, bass.ds(e, 1), :].rearrange("p a n -> p (a n)"), ALU.add).then_inc(h_done, 1)

            def fx_low(t, u):
                dve.wait_ge(fx_hi_done, t + 1)
                low(fx_lo[:, u % 2].rearrange("p c n -> p (c n)"), ps[:, 2 + u % 2, 0:D],
                    fx_hi[:, u % 2].rearrange("p c n -> p (c n)")).then_inc(fx_done, 1)

            def ht_low(t, u):
                dve.wait_ge(ht_hi_done, t + 1)
                V.scalar_tensor_tensor(ht_lo[:, u % 2].rearrange("p c n -> p (c n)"), ps[:, 4 + u % 2, :], 0.0,
                                       ht_hi[:, u % 2].rearrange("p c n -> p (c n)").bitcast(F32), ALU.max,
                                       ALU.subtract).then_inc(ht_done, 1)

            def add_b2(t, u, e):
                dve.wait_ge(y_ps, t + 1)
                if not (isinstance(t, int) and t < 2):
                    dve.wait_ge(y_done, t - 1)
                V.tensor_tensor(y_b[:, u % 2], ps[:, 6 + u % 2, 0:D],
                                b2_sb[:, bass.ds(e, 1), :].rearrange("p a n -> p (a n)"), ALU.add).then_inc(y_biased, 1)

            def expert(t):
                return dve.value_load(tab[0:1, 0, bass.ds(t, 1)], min_val=0, max_val=E - 1)

            fx_low(0, 0)

            def turn(t, u):
                add_b1(t, u, expert(t))
                if not (isinstance(t, int) and t == FT - 1):
                    fx_low(t + 1, (u + 1) % FU)
                if not (isinstance(t, int) and t == 0):
                    add_b2(t - 1, (u - 1) % FU, expert(t - 1))
                ht_low(t, u)

            for u in range(FU):
                turn(u, u)
            with dve.Fori(1, FT // FU - 1) as r:
                for u in range(FU):
                    turn(r * FU + u, u)
            for u in range(FU):
                turn(FT - FU + u, u)
            add_b2(FT - 1, FU - 1, expert(FT - 1))

        @block.gpsimd
        def _(pool):
            G = nc.gpsimd
            n = [0]

            def link(ins):
                n[0] += 1
                ins.then_inc(pool_chain, 1)
                pool.wait_ge(pool_chain, n[0])

            G.memset(ident[:], 0.0).then_inc(pool_chain, 1)
            G.memset(upper[:], 0.0).then_inc(pool_chain, 1)
            G.memset(causal[:], LOW).then_inc(pool_chain, 1)
            G.memset(half_neg[:], -0.5).then_inc(pool_chain, 1)
            G.memset(sums[:], 0.0).then_inc(pool_chain, 1)
            G.memset(pad_row[:], 0.0).then_inc(pool_chain, 1)
            G.memset(cum[:], 0.0).then_inc(pool_chain, 1)
            G.memset(ones[:], 1.0).then_inc(pool_chain, 1)
            n[0] = 8
            pool.wait_ge(pool_chain, 8)
            link(G.affine_select(out=ident[:], in_=ident[:], compare_op=ALU.not_equal, fill=1.0, base=0,
                                 pattern=[[-1, P]], channel_multiplier=1))
            link(G.affine_select(out=upper[:], in_=upper[:], compare_op=ALU.is_ge, fill=1.0, base=0,
                                 pattern=[[-1, P]], channel_multiplier=1))
            link(G.affine_select(out=causal[:], in_=causal[:], compare_op=ALU.is_gt, fill=0.0, base=0,
                                 pattern=[[1, P]], channel_multiplier=-1))
            link(G.iota(iota_e[:], pattern=[[1, E]], base=0, channel_multiplier=0, allow_small_or_imprecise_dtypes=True))
            link(G.iota(iota_t[:], pattern=[[1, FT]], base=0, channel_multiplier=0, allow_small_or_imprecise_dtypes=True))
            link(G.iota(lane[:], pattern=[[1, 1]], base=0, channel_multiplier=1, allow_small_or_imprecise_dtypes=True))
            link(G.iota(tok_ids[:], pattern=[[P, NT]], base=0, channel_multiplier=1))
            link(G.iota(pad_row[:, C_TOK:C_TOK + 1].bitcast(I32), pattern=[[1, 1]], base=S, channel_multiplier=1))
            link(G.tensor_scalar(cum[0:1, :], iota_e[0:1, :], float(REGION), None, ALU.mult))
            G.tensor_copy(slot_f[:, 0], half_neg[:]).then_inc(consts_ready, 1)
            pool.dma_start(xg[ZERO_TILE:ZERO_TILE + P, :], pad_row[:]).then_inc(scattered[3], 16)

            def x_rsqrt(nb, k):
                p = 2 * nb + k
                pool.wait_ge(x_stats, p + 1)
                if not (isinstance(nb, int) and nb == 0 and k == 0):
                    pool.wait_ge(x_normed, p)
                apart(pool)
                G.tensor_scalar(rstd[:, :, 0:1], mv[:, :, 1:2], EPS, None, ALU.add).then_inc(x_eps, 1)
                pool.wait_ge(x_eps, p + 1)
                G.tensor_tensor(rstd[:, :, 1:2], rstd[:, :, 0:1], half_neg[:].rearrange("p (a b) -> p a b", b=1), ALU.pow
                                ).then_inc(x_rstd, 1)

            x_rsqrt(0, 0)
            x_rsqrt(0, 1)

            def x1_rsqrt(t, j):
                k = j % 2
                pool.wait_ge(x1_stats, t + 1)
                if not (isinstance(t, int) and t < 2):
                    pool.wait_ge(x2_ready, t - 1)
                G.tensor_tensor(rstd2[:, k, 1:2], rstd2[:, k, 0:1], half_neg[:, 0:1], ALU.pow).then_inc(rstd2_ready, 1)

            def one_hots(t, j):
                k = j % 2
                pool.wait_ge(top_ready, t + 1)
                if not (isinstance(t, int) and t == 0):
                    add_choices(t - 1)
                if not (isinstance(t, int) and t < 2):
                    pool.wait_ge(slots_ready, t - 1)
                apart(pool)
                G.tensor_copy(top_f[:, k], top_i[:, k, 0:2]).then_inc(hot_chain, 1)
                pool.wait_ge(hot_chain, 3 * t + 1)
                apart(pool)
                G.tensor_copy(rows[:, j, C_E1:C_E1 + 1], top_f[:, k, 0:1])
                for c in range(2):
                    G.tensor_scalar(hot[:, k, c], iota_e[:], top_f[:, k, c:c + 1], None, ALU.is_equal
                                    ).then_inc(hot_chain, 1)
                pool.wait_ge(hot_chain, 3 * t + 3)
                G.tensor_tensor(mask[:], hot[:, k, 0], hot[:, k, 1], ALU.add).then_inc(hot_ready, 1)

            def add_choices(t):
                pool.wait_ge(rank_ps, t + 1)
                pool.wait_ge(hot_ready, t + 1)
                G.tensor_tensor(cum[:], cum[:], mask[:], ALU.add).then_inc(cum_ready, 1)
                pool.wait_ge(cum_ready, t + 1)

            def scatter(t, j):
                k = j % 2
                pool.wait_ge(slots_ready, t + 1)
                apart(pool)
                G.tensor_tensor(rows[:, j, C_G2:C_G2 + 1], ex[:, k:k + 1], den[:, 1 + k:2 + k], ALU.mult
                                ).then_inc(row_chain, 1)
                G.tensor_copy(slot_i[:, j], slot_f[:, k])
                G.tensor_copy(rows[:, j, C_TOK:C_TOK + 1].bitcast(I32), tok_ids[:, bass.ds(t, 1)])
                pool.wait_ge(row_chain, t + 1)
                apart(pool)
                G.tensor_scalar(rows[:, j, C_GD:C_GD + 1], rows[:, j, C_G2:C_G2 + 1], -2.0, 1.0, ALU.mult, ALU.add
                                ).then_inc(row_ready, 1)
                pool.wait_ge(row_ready, t + 1)
                apart(pool)
                for c in range(2):
                    G.indirect_dma_start(out=xg, out_offset=bass.IndirectOffsetOnAxis(ap=slot_i[:, j, c:c + 1].bitcast(U32), axis=0),
                                         in_=rows[:, j, :], in_offset=None).then_inc(scattered[j], 16)

            def body(qb):
                nxt = has_next(qb)
                for j in range(TB):
                    if nxt and j < 2:
                        x_rsqrt(qb + 1, j)
                    t1, j1 = routed(qb, j, 1)
                    t3, j3 = routed(qb, j, 3)
                    t4, j4 = routed(qb, j, 4)
                    if t3 is not None:
                        one_hots(t3, j3)
                    if t1 is not None:
                        x1_rsqrt(t1, j1)
                    if t4 is not None:
                        scatter(t4, j4)

            over_blocks(pool, body)
            x1_rsqrt(NT - 1, TB - 1)
            for j in range(4):
                t3, j3 = routed(NB, j, 3)
                t4, j4 = routed(NB, j, 4)
                if t3 < NT:
                    one_hots(t3, j3)
                else:
                    add_choices(NT - 1)
                scatter(t4, j4)

            pool.wait_ge(tab_ready, 1)
            for e in range(E):
                G.indirect_dma_start(out=xg, out_offset=bass.IndirectOffsetOnAxis(ap=pad_slot[:, e:e + 1].bitcast(U32), axis=0),
                                     in_=pad_row[:], in_offset=None).then_inc(padded, 16)
            for k in range(2):
                pool.wait_ge(x1_stored[k], 16 * (NT // 2))
            pool.wait_ge(tab_ready, 2)

            def read_columns(t, u, r):
                pool.wait_ge(xf_loaded[u], 16 * (r + 1))
                if not (isinstance(t, int) and t < FU):
                    pool.wait_ge(y_done, t - FU + 1)
                apart(pool)
                G.tensor_copy(dest[:, u:u + 1], xf[:, u, C_TOK:C_TOK + 1].bitcast(I32))
                G.tensor_copy(e_now[:, u:u + 1], tile_e[:, bass.ds(t, 1)]).then_inc(meta_chain, 1)
                pool.wait_ge(meta_chain, 3 * t + 1)
                apart(pool)
                G.tensor_scalar(gsel[:, u:u + 1], xf[:, u, C_E1:C_E1 + 1], e_now[:, u:u + 1], None, ALU.is_equal
                                ).then_inc(meta_chain, 1)
                pool.wait_ge(meta_chain, 3 * t + 2)
                G.tensor_tensor(gsel[:, u:u + 1], gsel[:, u:u + 1], xf[:, u, C_GD:C_GD + 1], ALU.mult).then_inc(meta_chain, 1)
                pool.wait_ge(meta_chain, 3 * t + 3)
                G.tensor_tensor(gate[:, u:u + 1], gsel[:, u:u + 1], xf[:, u, C_G2:C_G2 + 1], ALU.add).then_inc(gate_ready, 1)

            def add_rows(t, u):
                pool.wait_ge(y_done, t + 1)
                pool.wait_ge(gate_ready, t + 1)
                if not (isinstance(t, int) and t == 0):
                    pool.wait_ge(added, 16 * t)
                apart(pool)
                G.indirect_dma_start(out=out, out_offset=bass.IndirectOffsetOnAxis(ap=dest[:, u:u + 1].bitcast(U32), axis=0),
                                     in_=y_sb[:, u % 2], in_offset=None, compute_op=ALU.add).then_inc(added, 16)

            def turn(t, u, r):
                read_columns(t, u, r)
                if not (isinstance(t, int) and t == 0):
                    add_rows(t - 1, (u - 1) % FU)

            for u in range(FU):
                turn(u, u, 0)
            with pool.Fori(1, FT // FU) as r:
                for u in range(FU):
                    turn(r * FU + u, u, r)
            add_rows(FT - 1, FU - 1)
            pool.wait_ge(added, 16 * FT)


_INS = ["L0_attn_in_features", "L0_attn_Wq", "L0_attn_Wk", "L0_attn_Wv", "L0_attn_Wo", "L0_ffn_Wg", "L0_ffn_W1",
        "L0_ffn_b1", "L0_ffn_W2", "L0_ffn_b2"]


def kernel(**inputs):
    import numpy as _np
    import concourse.bacc as _bacc
    from concourse import mybir as _mybir
    from concourse.bass_utils import run_bass_kernel_spmd as _run

    nc = _bacc.Bacc("TRN2", target_bir_lowering=False, num_devices=1)
    arrays, args = {}, []
    for name in _INS:
        a = _np.ascontiguousarray(inputs[name])
        arrays[f"in_{name}"] = a
        args.append(nc.dram_tensor(f"in_{name}", a.shape, _mybir.dt.from_np(a.dtype), kind="ExternalInput").ap())
    args.append(nc.dram_tensor("out_0", (OUT_ROWS, D), _mybir.dt.float32, kind="ExternalOutput").ap())
    moe_block(nc, *args)
    r = _run(nc, [arrays], core_ids=[0])
    return r.results[0]["out_0"][:S].reshape(1, S, D)
```

```python
from contextlib import ExitStack

import numpy as np
import concourse.bass as bass
from concourse import mybir

F32, F32R, I32, U32 = (mybir.dt.float32, mybir.dt.float32r, mybir.dt.int32, mybir.dt.uint32)
ALU, ACT, AX = mybir.AluOpType, mybir.ActivationFunctionType, mybir.AxisListType

P = 128
S, D, E, H = 4096, 256, 8, 512
DC, HC = D // P, H // P
QB = 512
NB = S // QB
TB = QB // P
NT = S // P
NP2 = NT // 2
SCALE = 1.0 / float(np.sqrt(D))
EPS = 1e-5
LOW = -3.0e38
REGION = S + P
ZERO_TILE = E * REGION
ROW = D + 4
C_TOK, C_E1, C_GD, C_G2 = D, D + 1, D + 2, D + 3
FT = 2 * S // P + E
E_BITS = E.bit_length() - 1
FU = 8
W2_ORDER = (E - 1,) + tuple(range(E - 1))
OUT_ROWS = S + P


def chunk0(qb, j):
    return 2 * qb * (qb + 1) + j * (qb + 1)


def moe_block(nc, x, wq, wk, wv, wo, wg, w1, b1, w2, b2, out):
    xg = nc.dram_tensor("xg_rows", (ZERO_TILE + P, ROW), F32, kind="Internal").ap()
    x_tiles = x[0].rearrange("(n p) d -> p n d", p=P)
    out_tiles = out.rearrange("(n p) d -> p n d", p=P)
    es = ExitStack()
    with es:
        def sb(name, shape, dt=F32, stack=es):
            return stack.enter_context(nc.sbuf_tensor(name, shape, dt))

        def sem(name):
            return es.enter_context(nc.semaphore(name))

        ident = sb("ident", [P, P])
        ones = sb("ones", [P, P])
        upper = sb("upper", [P, P])
        causal = sb("causal", [P, P])
        half_neg = sb("half_neg", [P, 2])
        iota_e = sb("iota_e", [P, E])
        lane = sb("lane", [P, 1])
        tok_ids = sb("tok_ids", [P, NT], I32)
        wg_sb = sb("wg_sb", [P, DC, E])
        cum = sb("cum", [P, E])
        pad_row = sb("pad_row", [P, ROW])
        tile_e = sb("tile_e", [P, FT])
        tab_rows = sb("tab_rows", [P, FT], I32)
        tab_words = sb("tab_words", [P, FT // FU], I32)
        fence = sb("fence", [P, FT], I32)
        digit = sb("digit", [P, FT // FU, FU])
        cnt = sb("cnt", [P, 4, E])
        cnt_i = sb("cnt_i", [P, E], I32)
        pad_slot = sb("pad_slot", [P, E], I32)
        tmpf = sb("tmpf", [P, 2, FT])
        iota_t = sb("iota_t", [P, FT])

        at = es.enter_context(ExitStack())
        A = lambda name, shape, dt=F32: sb(name, shape, dt, at)
        xt_hi, xt_lo = (A(n, [P, DC, S], F32R) for n in ("xt_hi", "xt_lo"))
        v_hi, v_lo = (A(n, [P, NT, D], F32R) for n in ("v_hi", "v_lo"))
        wa_hi, wa_lo, wb_hi, wb_lo = (A(n, [P, DC, D], F32R) for n in ("wa_hi", "wa_lo", "wb_hi", "wb_lo"))
        q_hi, q_lo = (A(n, [P, DC, QB], F32R) for n in ("q_hi", "q_lo"))
        s_sb = A("s_sb", [P, 2, S - QB])
        s_diag = A("s_diag", [P, 2, QB])
        probs = A("probs", [P, QB])
        pt_hi, pt_lo = (A(n, [P, TB, P], F32R) for n in ("pt_hi", "pt_lo"))
        x_in = A("x_in", [P, 2, 2, D])
        xn = A("xn", [P, 2, D])
        xs_hi, xs_lo = (A(n, [P, DC, 2 * P], F32R) for n in ("xs_hi", "xs_lo"))
        x_res = A("x_res", [P, 2, D])
        x1 = A("x1", [P, 2, D])
        rows = A("rows", [P, 4, ROW])
        x2t = A("x2t", [P, DC, P])
        stat = A("stat", [P, 2, 6])
        mv = A("mv", [P, 2, 2])
        rstd = A("rstd", [P, 2, 2])
        stat2 = A("stat2", [P, 6])
        mv2 = A("mv2", [P, 2, 2])
        rstd2 = A("rstd2", [P, 2, 2])
        run_max = A("run_max", [P, 2])
        neg_max = A("neg_max", [P, 2])
        sums = A("sums", [P, 2, 8])
        lsum = A("lsum", [P, 2])
        top = A("top", [P, 2, 8])
        top_i = A("top_i", [P, 2, 8], U32)
        top_f = A("top_f", [P, 2, 2])
        hot = A("hot", [P, 2, 2, E])
        mask = A("mask", [P, E])
        junk = A("junk", [P, 2, E])
        slot_f = A("slot_f", [P, 2, 2])
        slot_i = A("slot_i", [P, 4, 2], I32)
        ex = A("ex", [P, 2])
        den = A("den", [P, 3])
        raw = s_sb[:, 1, 0:4 * DC * D].rearrange("p (w c n) -> p w c n", w=4, c=DC)
        wot = s_sb[:, 1, 4 * DC * D:5 * DC * D].rearrange("p (c n) -> p c n", c=DC)
        at.close()

        ff = es.enter_context(ExitStack())
        B = lambda name, shape, dt=F32: sb(name, shape, dt, ff)
        w1_hi, w1_lo = (B(n, [P, E, DC, H], F32R) for n in ("w1_hi", "w1_lo"))
        w2_hi, w2_lo = (B(n, [P, E, HC, D], F32R) for n in ("w2_hi", "w2_lo"))
        b1_sb = B("b1_sb", [P, E, H])
        b2_sb = B("b2_sb", [P, E, D])
        past = B("past", [P, FT, E])
        past_tiles = B("past_tiles", [P, FT, E])
        cnt_w = B("cnt_w", [P, FT // FU])
        xf = B("xf", [P, FU, ROW])
        fx_hi, fx_lo = (B(n, [P, 2, DC, P], F32R) for n in ("fx_hi", "fx_lo"))
        h_sb = B("h_sb", [P, 2, H])
        ht_hi, ht_lo = (B(n, [P, 2, HC, P], F32R) for n in ("ht_hi", "ht_lo"))
        y_b = B("y_b", [P, 2, D])
        y_sb = B("y_sb", [P, 2, D])
        gate = B("gate", [P, FU])
        gsel = B("gsel", [P, FU])
        dest = B("dest", [P, FU], I32)
        e_now = B("e_now", [P, FU])

        ps = es.enter_context(nc.psum_tensor("ps", [P, 8, 512], F32))
        ps_s = ps[:, 0, :]
        ps_pt = ps[:, 1:3, 0:2 * P]
        ps_o = ps[:, 3:5, 0:D]
        ps_x, ps_v, ps_r = ps[:, 5, :], ps[:, 6, :], ps[:, 7, :]

        consts_ready, wload, wstage_ps, wstage_sb, wstage_hi = map(
            sem, ("consts_ready", "wload", "wstage_ps", "wstage_sb", "wstage_hi"))
        x_loaded = [sem("x_loaded0"), sem("x_loaded1")]
        x_stats, x_stats1, x_rstd, x_normed = map(sem, ("x_stats", "x_stats1", "x_rstd", "x_normed"))
        xt_ps, xs_hi_done, xs_done = map(sem, ("xt_ps", "xs_hi_done", "xs_done"))
        xt_stored = [sem("xt_stored0"), sem("xt_stored1")]
        v_ps, v_hi_done, v_done = map(sem, ("v_ps", "v_hi_done", "v_done"))
        q_ps, q_hi_done, q_done = map(sem, ("q_ps", "q_hi_done", "q_done"))
        scores_ps, scores_saved, max_ready, probs_ready = map(
            sem, ("scores_ps", "scores_saved", "max_ready", "probs_ready"))
        pt_ps, pt_hi_done, pt_done, pv_done = map(sem, ("pt_ps", "pt_hi_done", "pt_done", "pv_done"))
        diag_part = sem("diag_part")
        res_loaded = [sem("res_loaded0"), sem("res_loaded1")]
        x1_chain, x1_done, x1_stats, rstd2_ready = map(sem, ("x1_chain", "x1_done", "x1_stats", "rstd2_ready"))
        x1_stored = [sem("x1_stored0"), sem("x1_stored1")]
        x2_ready, x2t_ps, x2t_sb, logits_ps = map(sem, ("x2_ready", "x2t_ps", "x2t_sb", "logits_ps"))
        top_chain, top_ready, hot_chain, hot_ready = map(sem, ("top_chain", "top_ready", "hot_chain", "hot_ready"))
        ex_ready, rank_ps, cum_ready, slot_chain, slots_ready = map(
            sem, ("ex_ready", "rank_ps", "cum_ready", "slot_chain", "slots_ready"))
        scattered = [sem(f"scattered{i}") for i in range(4)]
        pool_chain, x_eps, row_chain, row_ready = map(sem, ("pool_chain", "x_eps", "row_chain", "row_ready"))
        counts_ps, tab_chain, tab_ready = map(sem, ("counts_ps", "tab_chain", "tab_ready"))
        pads_ready, padded = sem("pads_ready"), sem("padded")
        w1_loaded = [sem(f"w1_loaded{e}") for e in range(E)]
        w2_loaded = [sem(f"w2_loaded{e}") for e in range(E)]
        fb_loaded, w1_hi_done, w2_hi_done, w1_done, w2_done = map(
            sem, ("fb_loaded", "w1_hi_done", "w2_hi_done", "w1_done", "w2_done"))
        xf_loaded = [sem(f"xf_loaded{i}") for i in range(FU)]
        fx_ps, fx_hi_done, fx_done = map(sem, ("fx_ps", "fx_hi_done", "fx_done"))
        h_ps, h_done, ht_ps, ht_hi_done, ht_done = map(sem, ("h_ps", "h_done", "ht_ps", "ht_hi_done", "ht_done"))
        y_ps, y_biased, y_done = map(sem, ("y_ps", "y_biased", "y_done"))
        added = [sem("added0"), sem("added1")]
        meta_chain, gate_ready = sem("meta_chain"), sem("gate_ready")
        block = es.enter_context(nc.Block())

        def over_blocks(eng, body):
            body(0)
            with eng.Fori(1, NB - 1) as qb:
                body(qb)
            body(NB - 1)

        def over_chunks(eng, qb, body):
            if isinstance(qb, int) and qb == 0:
                return
            with eng.Fori(0, qb) as kc:
                body(kc)

        def has_next(qb):
            return not (isinstance(qb, int) and qb == NB - 1)

        def tile(qb, j):
            return qb * TB + j

        def routed(qb, j, back):
            if isinstance(qb, int):
                t = tile(qb, j) - back
                return (t if t >= 0 else None), t % TB
            return tile(qb, j) - back, (j - back) % TB

        def apart(eng):
            eng.nop(nofuse=True)

        def word_registers(eng):
            return [eng.alloc_register(f"{w}_word_{eng.engine.name}") for w in ("last", "next")]

        def load_word(eng, regs, r):
            eng.load(regs[1], tab_words[0:1, bass.ds(r, 1)])

        def next_words(eng, regs):
            words = [eng.snap(reg) for reg in regs]
            eng.reg_mov(regs[0], regs[1])
            return words

        def expert(words, u):
            return (words[1 if u >= 0 else 0] >> (E_BITS * (u % FU))) & (E - 1)

        def pad(eng, e):
            row0 = eng.value_load(pad_slot[0:1, e:e + 1], min_val=0, max_val=ZERO_TILE)
            eng.dma_start(xg[bass.ds(row0, P), :], pad_row[:]).then_inc(padded, 16)

        def to3(ap, n):
            return ap.rearrange("p (c n) -> p c n", n=n)

        @block.sync
        def _(sp):
            for n, w in enumerate((wq, wk, wv, wo)):
                sp.dma_start(raw[:, n], w.rearrange("(c p) n -> p c n", p=P)).then_inc(wload, 16)

            def load_pair(nb, k):
                if not (isinstance(nb, int) and nb == 0):
                    sp.wait_ge(x_normed, 2 * nb + k - 1)
                sp.dma_start(x_in[:, k], x_tiles[:, bass.ds(2 * (2 * nb + k), 2), :]).then_inc(x_loaded[k], 16)

            def load_residual(t, j):
                if not (isinstance(t, int) and t < 2):
                    sp.wait_ge(x1_done, t - 1)
                sp.dma_start(x_res[:, j % 2], x_tiles[:, bass.ds(t, 1), :].rearrange("p a d -> p (a d)")
                             ).then_inc(res_loaded[j % 2], 16)

            def store_xt(nb, k):
                sp.wait_ge(xs_done, 2 * nb + k + 1)
                at_tok = bass.ds((2 * nb + k) * 2 * P, 2 * P)
                sp.dma_start(xt_hi[:, :, at_tok].bitcast(F32), xs_hi[:].bitcast(F32)).then_inc(xt_stored[k], 16)
                sp.dma_start(xt_lo[:, :, at_tok].bitcast(F32), xs_lo[:].bitcast(F32)).then_inc(xt_stored[k], 16)

            def store_x1(t, j):
                sp.wait_ge(x1_done, t + 1)
                sp.dma_start(out_tiles[:, bass.ds(t, 1), :].rearrange("p a d -> p (a d)"), x1[:, j % 2]
                             ).then_inc(x1_stored[j % 2], 16)

            def load_ffn_first():
                sp.wait_ge(scores_saved, chunk0(NB, 0))
                for e in range(E):
                    sp.dma_start(w1_lo[:, e].bitcast(F32), w1[e].rearrange("(c p) n -> p c n", p=P)
                                 ).then_inc(w1_loaded[e], 16)

            load_pair(0, 0)
            load_pair(0, 1)
            sp.dma_start(wg_sb[:], wg.rearrange("(c p) e -> p c e", p=P)).then_inc(wload, 16)
            load_residual(0, 0)
            store_xt(0, 0)
            store_xt(0, 1)

            def body(qb):
                nxt = has_next(qb)
                if nxt:
                    load_pair(qb + 1, 0)
                    load_pair(qb + 1, 1)
                for j in range(TB):
                    t1, j1 = routed(qb, j, 1)
                    if nxt and j in (1, 2):
                        store_xt(qb + 1, j - 1)
                    if not nxt and j == TB - 1:
                        load_ffn_first()
                    if t1 is not None:
                        store_x1(t1, j1)
                    if nxt or j < TB - 1:
                        load_residual(tile(qb, j) + 1, (j + 1) % TB)

            over_blocks(sp, body)
            for i, e in enumerate(W2_ORDER):
                sp.wait_ge(pv_done, chunk0(NB - 1, TB - 1) + i + 1)
                sp.dma_start(w2_lo[:, e].bitcast(F32), w2[e].rearrange("(c p) n -> p c n", p=P)
                             ).then_inc(w2_loaded[e], 16)
            store_x1(NT - 1, TB - 1)
            sp.dma_start(b1_sb[:], b1[None, :, :].to_broadcast([P, E, H])).then_inc(fb_loaded, 16)
            sp.dma_start(b2_sb[:], b2[None, :, :].to_broadcast([P, E, D])).then_inc(fb_loaded, 16)

            sp.wait_ge(pads_ready, 1)
            for e in range(E // 2):
                pad(sp, e)

            sp.wait_ge(tab_ready, 1)
            for k in range(4):
                sp.wait_ge(scattered[k], 32 * (NT // 4))
            for k in range(2):
                sp.wait_ge(added[k], 16)
                sp.wait_ge(x1_stored[k], 16 * (NT // 2))
            sp.wait_ge(padded, 16 * E)

            def load_rows(t, u, first):
                if not first:
                    sp.wait_ge(fx_ps, t - FU + 1)
                    sp.wait_ge(gate_ready, t - FU + 1)
                row0 = sp.value_load(tab_rows[0:1, bass.ds(t, 1)], min_val=0, max_val=ZERO_TILE)
                sp.dma_start(xf[:, u, :], xg[bass.ds(row0, P), :]).then_inc(xf_loaded[u], 16)

            for u in range(FU):
                load_rows(u, u, True)
            with sp.Fori(1, FT // FU) as r:
                for u in range(FU):
                    load_rows(r * FU + u, u, False)
            for k in range(2):
                sp.wait_ge(added[k], 16 * (FT // 2 + 1))

        @block.tensor
        def _(pe):
            def three(dst, pairs, start=True, stop=True, check=True):
                n = 3 * len(pairs)
                k = 0
                for (a_hi, a_lo), (b_hi, b_lo) in pairs:
                    for a, b in ((a_hi, b_hi), (a_hi, b_lo), (a_lo, b_hi)):
                        ins = nc.tensor.matmul(dst, a, b, start=start and k == 0, stop=stop and k == n - 1,
                                               skip_group_check=not check)
                        k += 1
                return ins

            pe.wait_ge(wload, 16 * 5)
            pe.wait_ge(consts_ready, 1)
            for ic in range(DC):
                for oc in range(DC):
                    ins = nc.tensor.matmul(ps_x[:, ic * D:(ic + 1) * D], raw[:, 0, oc, ic * P:(ic + 1) * P],
                                           raw[:, 1, oc, :], start=(oc == 0), stop=(oc == DC - 1))
            ins.then_inc(wstage_ps, 1)
            for oc in range(DC):
                for cc in range(DC):
                    ins = nc.tensor.transpose(ps_v[:, oc * D + cc * P:oc * D + (cc + 1) * P],
                                              raw[:, 3, cc, oc * P:(oc + 1) * P], ident[:])
            ins.then_inc(wstage_ps, 1)
            pe.wait_ge(wstage_sb, 2)
            for dc in range(DC):
                for oc in range(DC):
                    ins = nc.tensor.matmul(ps_x[:, dc * D:(dc + 1) * D], raw[:, 2, oc, dc * P:(dc + 1) * P],
                                           wot[:, oc, :], start=(oc == 0), stop=(oc == DC - 1))
            ins.then_inc(wstage_ps, 1)

            def transpose_pair(nb, k):
                p = 2 * nb + k
                pe.wait_ge(x_normed, p + 1)
                if isinstance(nb, int) and nb == 0:
                    pe.wait_ge(wstage_sb, 3) if k == 0 else pe.wait_ge(xs_done, p)
                else:
                    pe.wait_ge(q_done, 2 * nb) if k == 0 else pe.wait_ge(xs_done, p)
                for c in range(DC):
                    for a in range(2):
                        ins = nc.tensor.transpose(ps_x[:, c * 2 * P + a * P:c * 2 * P + (a + 1) * P],
                                                  xn[:, a, c * P:(c + 1) * P], ident[:])
                ins.then_inc(xt_ps, 1)

            def values(nb, k):
                p = 2 * nb + k
                pe.wait_ge(xs_done, p + 1)
                if k == 1:
                    pe.wait_ge(v_done, p)
                elif not (isinstance(nb, int) and nb == 0):
                    pe.wait_ge(q_done, 2 * nb)
                for a in range(2):
                    tok = slice(a * P, (a + 1) * P)
                    ins = three(ps_v[:, a * D:(a + 1) * D],
                                [((xs_hi[:, c, tok], xs_lo[:, c, tok]), (wb_hi[:, c], wb_lo[:, c]))
                                 for c in range(DC)])
                ins.then_inc(v_ps, 1)

            def queries_first(nb):
                pe.wait_ge(xt_stored[0], 32 * (nb + 1))
                pe.wait_ge(xs_done, 2 * nb + 2)
                tok = bass.ds(nb * QB, P)
                for m in range(DC):
                    col = slice(m * P, (m + 1) * P)
                    ins = three(ps_x[:, m * P:(m + 1) * P],
                                [((wa_hi[:, c, col], wa_lo[:, c, col]), (xt_hi[:, c, tok], xt_lo[:, c, tok]))
                                 for c in range(DC)])
                ins.then_inc(q_ps, 1)

            def queries_rest(nb):
                pe.wait_ge(xt_stored[1], 32 * (nb + 1))
                pe.wait_ge(q_done, 2 * nb + 1)
                pe.wait_ge(v_done, 2 * nb + 2)
                tok = bass.ds(nb * QB + P, QB - P)
                for m, bank in enumerate((ps_x, ps_v)):
                    col = slice(m * P, (m + 1) * P)
                    ins = three(bank[:, 0:QB - P],
                                [((wa_hi[:, c, col], wa_lo[:, c, col]), (xt_hi[:, c, tok], xt_lo[:, c, tok]))
                                 for c in range(DC)])
                ins.then_inc(q_ps, 1)

            def scores(n, j, key0, width):
                if not (isinstance(n, int) and n == 0):
                    pe.wait_ge(scores_saved, n)
                q = slice(j * P, (j + 1) * P)
                keys = bass.ds(key0, width)
                three(ps_s[:, 0:width], [((q_hi[:, c, q], q_lo[:, c, q]), (xt_hi[:, c, keys], xt_lo[:, c, keys]))
                                         for c in range(DC)]).then_inc(scores_ps, 1)

            def transpose_probs(n, blocks):
                pe.wait_ge(probs_ready, n + 1)
                for b in range(blocks):
                    ins = nc.tensor.transpose(ps_pt[:, b // 2, (b % 2) * P:(b % 2 + 1) * P],
                                              probs[:, b * P:(b + 1) * P], ident[:])
                    if b == blocks - 1:
                        ins.then_inc(pt_ps, 2 if blocks <= 2 else 1)
                    elif b == 1:
                        ins.then_inc(pt_ps, 1)

            def weigh_values(n, j, blocks, v0, first):
                for b in range(blocks):
                    if b == 0:
                        pe.wait_ge(pt_done, 2 * n + (1 if blocks > 2 else 2))
                    if b == 2:
                        pe.wait_ge(pt_done, 2 * n + 2)
                    ins = three(ps_o[:, j % 2], [((pt_hi[:, b], pt_lo[:, b]),
                                                  (v_hi[:, v0 + b] if isinstance(v0, int) else
                                                   v_hi[:, bass.ds(v0 + b, 1), :].rearrange("p a d -> p (a d)"),
                                                   v_lo[:, v0 + b] if isinstance(v0, int) else
                                                   v_lo[:, bass.ds(v0 + b, 1), :].rearrange("p a d -> p (a d)")))],
                                start=first and b == 0, stop=b == blocks - 1, check=False)
                ins.then_inc(pv_done, 1)

            def transpose_x2(t, j):
                pe.wait_ge(x2_ready, t + 1)
                for c in range(DC):
                    ins = nc.tensor.transpose(ps_r[:, c * P:(c + 1) * P], rows[:, j, c * P:(c + 1) * P], ident[:])
                ins.then_inc(x2t_ps, 1)

            def logits(t):
                pe.wait_ge(x2t_sb, t + 1)
                for c in range(DC):
                    ins = nc.tensor.matmul(ps_r[:, D:D + E], x2t[:, c], wg_sb[:, c], start=(c == 0), stop=(c == DC - 1))
                ins.then_inc(logits_ps, 1)

            def rank(t):
                pe.wait_ge(hot_ready, t + 1)
                nc.tensor.matmul(ps_r[:, D + 16:D + 16 + E], upper[:], mask[:], start=True, stop=False)
                nc.tensor.matmul(ps_r[:, D + 16:D + 16 + E], ones[:], cum[:], start=False, stop=True
                                 ).then_inc(rank_ps, 1)

            def routing(qb, j):
                t2, j2 = routed(qb, j, 2)
                t3, _ = routed(qb, j, 3)
                t4, _ = routed(qb, j, 4)
                t5, _ = routed(qb, j, 5)
                if t3 is not None and (not isinstance(t3, int) or t3 < NT):
                    pe.wait_ge(x2t_sb, t3 + 1)
                if t4 is not None:
                    pe.wait_ge(top_ready, t4 + 1)
                if t5 is not None:
                    pe.wait_ge(slots_ready, t5 + 1)
                if t4 is not None:
                    rank(t4)
                if t3 is not None and (not isinstance(t3, int) or t3 < NT):
                    logits(t3)
                if t2 is not None and (not isinstance(t2, int) or t2 < NT):
                    transpose_x2(t2, j2)

            pe.wait_ge(wstage_sb, 3)
            transpose_pair(0, 0)
            values(0, 0)
            transpose_pair(0, 1)
            values(0, 1)
            queries_first(0)
            queries_rest(0)
            pe.wait_ge(q_done, 1)
            scores(0, 0, 0, P)

            def body(qb):
                nxt = has_next(qb)
                for j in range(TB):
                    t, n0, n1 = tile(qb, j), chunk0(qb, j), chunk0(qb, j) + qb + 1
                    if nxt and j == 2:
                        values(qb + 1, 0)
                        transpose_pair(qb + 1, 1)
                    if nxt and j == 3:
                        values(qb + 1, 1)
                    routing(qb, j)
                    if nxt and j == 1:
                        transpose_pair(qb + 1, 0)
                    transpose_probs(n0, j + 1)
                    if j < TB - 1:
                        pe.wait_ge(q_done, 2 * qb + 2)
                        scores(n1, j + 1, qb * QB, (j + 2) * P)
                    elif nxt:
                        pe.wait_ge(q_done, 2 * (qb + 1) + 1)
                        scores(n1, 0, (qb + 1) * QB, P)
                        scores(n1 + 1, 0, qb * QB, QB)
                    pe.wait_ge(v_done, 2 * (qb + 1))
                    if not (isinstance(t, int) and t < 2):
                        pe.wait_ge(x1_done, t - 1)
                    weigh_values(n0, j, j + 1, qb * TB, True)

                    def chunk(kc):
                        transpose_probs(n0 + 1 + kc, TB)
                        if j < TB - 1:
                            scores(n1 + 1 + kc, j + 1, kc * QB, QB)
                        elif nxt:
                            scores(n1 + 2 + kc, 0, kc * QB, QB)
                        weigh_values(n0 + 1 + kc, j, TB, kc * TB, False)

                    over_chunks(pe, qb, chunk)
                    if nxt and j == 2:
                        queries_first(qb + 1)
                    if nxt and j == 3:
                        queries_rest(qb + 1)

            over_blocks(pe, body)
            for j in range(4):
                routing(NB, j)

            nc.tensor.matmul(ps_s[:, 0:E], ones[:], mask[:], start=True, stop=False)
            nc.tensor.matmul(ps_s[:, 0:E], ones[:], cum[:], start=False, stop=True).then_inc(counts_ps, 1)

            pe.wait_ge(tab_ready, 2)

            def transpose_rows(t, u, early):
                pe.wait_ge(xf_loaded[u], 16 * (t // FU + 1) if isinstance(t, int) else 16 * early)
                if not (isinstance(t, int) and t < 2):
                    pe.wait_ge(fx_done, t - 1)
                for c in range(DC):
                    ins = nc.tensor.transpose(ps[:, 2 + u % 2, c * P:(c + 1) * P], xf[:, u, c * P:(c + 1) * P], ident[:])
                ins.then_inc(fx_ps, 1)

            def up(t, u, e):
                pe.wait_ge(fx_done, t + 1)
                if not (isinstance(t, int) and t < 2):
                    pe.wait_ge(h_done, t - 1)
                w = lambda m, c: m[:, bass.ds(e, 1), c, :].rearrange("p a n -> p (a n)")
                three(ps[:, u % 2, :], [((fx_hi[:, u % 2, c], fx_lo[:, u % 2, c]), (w(w1_hi, c), w(w1_lo, c)))
                                        for c in range(DC)]).then_inc(h_ps, 1)

            def down(t, u, e):
                pe.wait_ge(ht_done, t + 1)
                if not (isinstance(t, int) and t < 2):
                    pe.wait_ge(y_biased, t - 1)
                w = lambda m, c: m[:, bass.ds(e, 1), c, :].rearrange("p a n -> p (a n)")
                three(ps[:, 6 + u % 2, 0:D], [((ht_hi[:, u % 2, c], ht_lo[:, u % 2, c]), (w(w2_hi, c), w(w2_lo, c)))
                                              for c in range(HC)]).then_inc(y_ps, 1)

            def transpose_h(t, u):
                pe.wait_ge(h_done, t + 1)
                if not (isinstance(t, int) and t < 2):
                    pe.wait_ge(ht_done, t - 1)
                for c in range(HC):
                    ins = nc.tensor.transpose(ps[:, 4 + u % 2, c * P:(c + 1) * P], h_sb[:, u % 2, c * P:(c + 1) * P], ident[:])
                ins.then_inc(ht_ps, 1)

            transpose_rows(0, 0, 1)
            pe.wait_ge(w1_done, E)

            def turn(t, u, r):
                up(t, u, expert(words, u))
                if not (isinstance(t, int) and t == FT - 1):
                    transpose_rows(t + 1, (u + 1) % FU, r + 1 if u < FU - 1 else r + 2)
                if not (isinstance(t, int) and t < 2):
                    if isinstance(t, int) and t == 2:
                        pe.wait_ge(w2_done, E)
                    down(t - 2, (u - 2) % FU, expert(words, u - 2))
                transpose_h(t, u)

            regs = word_registers(pe)
            load_word(pe, regs, 0)
            pe.reg_mov(regs[0], regs[1])
            words = next_words(pe, regs)
            load_word(pe, regs, 1)
            for u in range(FU):
                turn(u, u, 0)
            with pe.Fori(1, FT // FU - 1) as r:
                words = next_words(pe, regs)
                for u in range(FU):
                    turn(r * FU + u, u, r)
                    if u == FU // 2:
                        load_word(pe, regs, r + 1)
            words = next_words(pe, regs)
            for u in range(FU):
                turn(FT - FU + u, u, FT // FU - 1)
            for u in (FU - 2, FU - 1):
                down(FT - FU + u, u, expert(words, u))

        @block.scalar
        def _(act):
            copy = nc.scalar.copy
            act.wait_ge(wstage_ps, 1)
            copy(wa_hi[:].rearrange("p c n -> p (c n)"), ps_x[:]).then_inc(wstage_hi, 1)
            act.wait_ge(wstage_ps, 2)
            copy(wot.rearrange("p c n -> p (c n)"), ps_v[:]).then_inc(wstage_sb, 1)
            act.wait_ge(wstage_ps, 3)
            copy(wb_hi[:].rearrange("p c n -> p (c n)"), ps_x[:]).then_inc(wstage_hi, 1)

            def xs_high(nb, k):
                p = 2 * nb + k
                act.wait_ge(xt_ps, p + 1)
                if k == 1:
                    act.wait_ge(v_ps, p)
                    act.wait_ge(xt_stored[0], 32 * (nb + 1))
                elif not (isinstance(nb, int) and nb == 0):
                    act.wait_ge(v_ps, p)
                    act.wait_ge(xt_stored[1], 32 * nb)
                copy(xs_hi[:].rearrange("p c n -> p (c n)"), ps_x[:]).then_inc(xs_hi_done, 1)

            def v_high(nb, k):
                p = 2 * nb + k
                act.wait_ge(v_ps, p + 1)
                copy(v_hi[:, bass.ds(2 * p, 2), :], to3(ps_v, D)).then_inc(v_hi_done, 1)

            def q_high_first(nb):
                act.wait_ge(q_ps, 2 * nb + 1)
                copy(q_hi[:, :, 0:P], to3(ps_x[:, 0:DC * P], P)).then_inc(q_hi_done, 1)

            def q_high_rest(nb):
                act.wait_ge(q_ps, 2 * nb + 2)
                copy(q_hi[:, 0, P:QB], ps_x[:, 0:QB - P])
                copy(q_hi[:, 1, P:QB], ps_v[:, 0:QB - P]).then_inc(q_hi_done, 1)

            def exps(n, j, src, width, col):
                if not (isinstance(n, int) and n == 0):
                    act.wait_ge(pt_ps, 2 * n)
                apart(act)
                nc.scalar.activation(probs[:, 0:width], src, ACT.Exp, bias=neg_max[:, j % 2:j % 2 + 1],
                                     scale=SCALE, accum_out=sums[:, j % 2, col]).then_inc(probs_ready, 1)

            def pt_high(n, blocks):
                if not (isinstance(n, int) and n == 0):
                    act.wait_ge(pv_done, n)
                act.wait_ge(pt_ps, 2 * n + (1 if blocks > 2 else 2))
                w = min(blocks, 2)
                copy(pt_hi[:, 0:w], to3(ps_pt[:, 0, 0:w * P], P)).then_inc(pt_hi_done, 1 if blocks > 2 else 2)
                if blocks > 2:
                    act.wait_ge(pt_ps, 2 * n + 2)
                    w = blocks - 2
                    copy(pt_hi[:, 2:2 + w], to3(ps_pt[:, 1, 0:w * P], P)).then_inc(pt_hi_done, 1)

            def routing(qb, j):
                t2, _ = routed(qb, j, 2)
                if t2 is not None and (not isinstance(t2, int) or t2 < NT):
                    act.wait_ge(x2t_ps, t2 + 1)
                    if not (isinstance(t2, int) and t2 == 0):
                        act.wait_ge(logits_ps, t2)
                    copy(x2t[:].rearrange("p c n -> p (c n)"), ps_r[:, 0:D]).then_inc(x2t_sb, 1)

            def gate_exp(qb, j):
                t3, j3 = routed(qb, j, 3)
                if t3 is not None and (not isinstance(t3, int) or t3 < NT):
                    act.wait_ge(top_ready, t3 + 1)
                    k = j3 % 2
                    if not (isinstance(t3, int) and t3 < 2):
                        act.wait_ge(row_ready, t3 - 1)
                    nc.scalar.activation(ex[:, k:k + 1], top[:, k, 0:1], ACT.Exp, bias=top[:, k, 1:2],
                                         scale=-1.0).then_inc(ex_ready, 1)

            xs_high(0, 0)
            v_high(0, 0)
            xs_high(0, 1)
            v_high(0, 1)
            q_high_first(0)
            q_high_rest(0)
            act.wait_ge(consts_ready, 1)

            def diagonal_exps(qb, j):
                act.wait_ge(max_ready, tile(qb, j) + 1)
                if not (isinstance(qb, int) and qb == 0 and j < 2):
                    act.wait_ge(x1_done, tile(qb, j) - 1)
                exps(chunk0(qb, j), j, s_diag[:, j % 2, 0:(j + 1) * P], (j + 1) * P, slice(7, 8))

            diagonal_exps(0, 0)

            def weights_high(hi, raw_at, loaded, done, e):
                act.wait_ge(loaded[e], 16)
                copy(hi[:, e].rearrange("p c n -> p (c n)"), raw_at[:, e].bitcast(F32).rearrange("p c n -> p (c n)")
                     ).then_inc(done, 1)

            def body(qb):
                nxt = has_next(qb)
                for j in range(TB):
                    n0 = chunk0(qb, j)
                    pt_high(n0, j + 1)
                    routing(qb, j)
                    if nxt and j == 1:
                        xs_high(qb + 1, 0)
                    if nxt and j == 2:
                        v_high(qb + 1, 0)
                        xs_high(qb + 1, 1)
                    if nxt and j == 3:
                        v_high(qb + 1, 1)

                    def chunk(kc):
                        exps(n0 + 1 + kc, j, s_sb[:, j % 2, bass.ds(kc * QB, QB)], QB, bass.ds(kc, 1))
                        pt_high(n0 + 1 + kc, TB)

                    if nxt or j < TB - 1:
                        over_chunks(act, qb, chunk)
                    else:
                        for kc in range(NB - 1):
                            exps(n0 + 1 + kc, j, s_sb[:, j % 2, kc * QB:(kc + 1) * QB], QB, slice(kc, kc + 1))
                            weights_high(w1_hi, w1_lo, w1_loaded, w1_hi_done, kc)
                            pt_high(n0 + 1 + kc, TB)
                    if j < TB - 1:
                        diagonal_exps(qb, j + 1)
                    elif nxt:
                        diagonal_exps(qb + 1, 0)
                    if nxt and j == 2:
                        q_high_first(qb + 1)
                    if nxt and j == 3:
                        q_high_rest(qb + 1)
                    gate_exp(qb, j)

            over_blocks(act, body)

            for j in range(4):
                routing(NB, j)
                if j < 3:
                    gate_exp(NB, j)
                if j == 0:
                    weights_high(w1_hi, w1_lo, w1_loaded, w1_hi_done, E - 1)
                for e in W2_ORDER[2 * j:2 * j + 2]:
                    weights_high(w2_hi, w2_lo, w2_loaded, w2_hi_done, e)
            act.wait_ge(pads_ready, 1)
            for e in range(E // 2, E):
                pad(act, e)

            def fx_high(t, u):
                act.wait_ge(fx_ps, t + 1)
                if not (isinstance(t, int) and t < 2):
                    act.wait_ge(h_ps, t - 1)
                copy(fx_hi[:, u % 2].rearrange("p c n -> p (c n)"), ps[:, 2 + u % 2, 0:D]).then_inc(fx_hi_done, 1)

            def ht_high(t, u):
                act.wait_ge(ht_ps, t + 1)
                if not (isinstance(t, int) and t < 2):
                    act.wait_ge(y_ps, t - 1)
                nc.scalar.activation(ht_hi[:, u % 2].rearrange("p c n -> p (c n)"), ps[:, 4 + u % 2, :], ACT.Relu
                                     ).then_inc(ht_hi_done, 1)

            def y_gated(t, u, half):
                act.wait_ge(y_biased, t + 1)
                act.wait_ge(gate_ready, t + 1)
                if not (isinstance(t, int) and t < 2):
                    act.wait_ge(added[u % 2], 16 * (half + 1))
                nc.scalar.activation(y_sb[:, u % 2], y_b[:, u % 2], ACT.Copy, scale=gate[:, u:u + 1]).then_inc(y_done, 1)

            fx_high(0, 0)

            def turn(t, u, r):
                if not (isinstance(t, int) and t == FT - 1):
                    fx_high(t + 1, (u + 1) % FU)
                ht_high(t, u)
                if not (isinstance(t, int) and t < 2):
                    y_gated(t - 2, (u - 2) % FU, r * (FU // 2) + u // 2 - 1)

            for u in range(FU):
                turn(u, u, 0)
            with act.Fori(1, FT // FU - 1) as r:
                for u in range(FU):
                    turn(r * FU + u, u, r)
            for u in range(FU):
                turn(FT - FU + u, u, FT // FU - 1)
            for t in (FT - 2, FT - 1):
                y_gated(t, t % FU, t // 2)

        @block.vector
        def _(dve):
            V = nc.vector

            def low(dst, src, high):
                return V.tensor_tensor(dst, src, high.bitcast(F32), ALU.subtract)

            dve.wait_ge(wstage_hi, 1)
            low(wa_lo[:].rearrange("p c n -> p (c n)"), ps_x[:], wa_hi[:].rearrange("p c n -> p (c n)")
                ).then_inc(wstage_sb, 1)

            def x_statistics(nb, k):
                p = 2 * nb + k
                dve.wait_ge(x_loaded[k], 16 * (nb + 1))
                for a in range(2):
                    V.bn_stats(stat[:, a], x_in[:, k, a]).then_inc(x_stats1, 1)
                dve.wait_ge(x_stats1, 2 * p + 2)
                if not (isinstance(nb, int) and nb == 0 and k == 0):
                    dve.wait_ge(x_rstd, p)
                apart(dve)
                for a in range(2):
                    ins = V.bn_aggr(mv[:, a], stat[:, a])
                ins.then_inc(x_stats, 1)

            def x_normalise(nb, k):
                p = 2 * nb + k
                dve.wait_ge(x_rstd, p + 1)
                if not (isinstance(nb, int) and nb == 0 and k == 0):
                    dve.wait_ge(xt_ps, p)
                for a in range(2):
                    ins = V.tensor_scalar(xn[:, a], x_in[:, k, a], mv[:, a, 0:1], rstd[:, a, 1:2],
                                          ALU.subtract, ALU.mult)
                ins.then_inc(x_normed, 1)

            def xs_low(nb, k):
                p = 2 * nb + k
                dve.wait_ge(xs_hi_done, p + 1)
                low(xs_lo[:].rearrange("p c n -> p (c n)"), ps_x[:], xs_hi[:].rearrange("p c n -> p (c n)")
                    ).then_inc(xs_done, 1)

            def v_low(nb, k):
                p = 2 * nb + k
                dve.wait_ge(v_hi_done, p + 1)
                pair = bass.ds(2 * p, 2)
                low(v_lo[:, pair, :], to3(ps_v, D), v_hi[:, pair, :]).then_inc(v_done, 1)

            def q_low_first(nb):
                dve.wait_ge(q_hi_done, 2 * nb + 1)
                low(q_lo[:, :, 0:P], to3(ps_x[:, 0:DC * P], P), q_hi[:, :, 0:P]).then_inc(q_done, 1)

            def q_low_rest(nb):
                dve.wait_ge(q_hi_done, 2 * nb + 2)
                low(q_lo[:, 0, P:QB], ps_x[:, 0:QB - P], q_hi[:, 0, P:QB])
                low(q_lo[:, 1, P:QB], ps_v[:, 0:QB - P], q_hi[:, 1, P:QB]).then_inc(q_done, 1)

            def save_diagonal(n, qb, j):
                dve.wait_ge(scores_ps, n + 1)
                if not (isinstance(n, int) and n <= 1):
                    dve.wait_ge(probs_ready, chunk0(qb, j - 1) if j else chunk0(qb - 1, TB - 1))
                m = run_max[:, j % 2:j % 2 + 1]
                if j:
                    V.tensor_scalar(s_diag[:, j % 2, 0:j * P], ps_s[:, 0:j * P], 1.0, LOW, ALU.mult,
                                    ALU.max, accum_out=m).then_inc(diag_part, 1)
                    dve.wait_ge(diag_part, qb * (TB - 1) + j)
                apart(dve)
                V.tensor_tensor_reduce(s_diag[:, j % 2, j * P:(j + 1) * P], ps_s[:, j * P:(j + 1) * P], causal[:],
                                       1.0, m if j else LOW, ALU.add, ALU.max, m).then_inc(scores_saved, 1)

            def save_scores(n, j, key0):
                dve.wait_ge(scores_ps, n + 1)
                dve.wait_ge(scores_saved, n)
                m = run_max[:, j % 2:j % 2 + 1]
                V.tensor_scalar(s_sb[:, j % 2, bass.ds(key0, QB)], ps_s[:], 1.0, m, ALU.mult, ALU.max,
                                accum_out=m).then_inc(scores_saved, 1)

            def negate_max(t, j, n):
                dve.wait_ge(scores_saved, n)
                V.tensor_scalar(neg_max[:, j % 2:j % 2 + 1], run_max[:, j % 2:j % 2 + 1], -SCALE, None, ALU.mult
                                ).then_inc(max_ready, 1)

            def pt_low(n, blocks):
                dve.wait_ge(pt_hi_done, 2 * n + (1 if blocks > 2 else 2))
                w = min(blocks, 2)
                low(pt_lo[:, 0:w], to3(ps_pt[:, 0, 0:w * P], P), pt_hi[:, 0:w]).then_inc(pt_done, 1 if blocks > 2 else 2)
                if blocks > 2:
                    dve.wait_ge(pt_hi_done, 2 * n + 2)
                    w = blocks - 2
                    low(pt_lo[:, 2:2 + w], to3(ps_pt[:, 1, 0:w * P], P), pt_hi[:, 2:2 + w]).then_inc(pt_done, 1)

            def attention_out(t, j, n_end, half):
                k = j % 2
                dve.wait_ge(probs_ready, n_end)
                V.tensor_reduce(lsum[:, 0:1], sums[:, k, :], AX.X, ALU.add).then_inc(x1_chain, 1)
                dve.wait_ge(x1_chain, 4 * t + 1)
                V.reciprocal(lsum[:, 1:2], lsum[:, 0:1]).then_inc(x1_chain, 1)
                dve.wait_ge(x1_chain, 4 * t + 2)
                dve.wait_ge(res_loaded[k], 16 * half)
                if not (isinstance(t, int) and t < 2):
                    dve.wait_ge(x1_stored[k], 16 * (half - 1))
                dve.wait_ge(pv_done, n_end)
                V.scalar_tensor_tensor(x1[:, k], ps_o[:, k], lsum[:, 1:2], x_res[:, k], ALU.mult, ALU.add
                                       ).then_inc(x1_done, 1)
                dve.wait_ge(x1_done, t + 1)
                V.bn_stats(stat2[:], x1[:, k]).then_inc(x1_chain, 1)
                dve.wait_ge(x1_chain, 4 * t + 3)
                apart(dve)
                V.bn_aggr(mv2[:, k], stat2[:]).then_inc(x1_chain, 1)
                dve.wait_ge(x1_chain, 4 * t + 4)
                V.tensor_scalar(rstd2[:, k, 0:1], mv2[:, k, 1:2], EPS, None, ALU.add).then_inc(x1_stats, 1)

            def x2_normalise(t, j, turn4):
                k = j % 2
                dve.wait_ge(rstd2_ready, t + 1)
                if not (isinstance(t, int) and t < 4):
                    dve.wait_ge(scattered[j], 32 * turn4)
                V.tensor_scalar(rows[:, j, 0:D], x1[:, k], mv2[:, k, 0:1], rstd2[:, k, 1:2], ALU.subtract, ALU.mult
                                ).then_inc(x2_ready, 1)

            def choose(t, j):
                k = j % 2
                dve.wait_ge(logits_ps, t + 1)
                if not (isinstance(t, int) and t < 2):
                    dve.wait_ge(hot_ready, t - 1)
                apart(dve)
                V.max(top[:, k], ps_r[:, D:D + E]).then_inc(top_chain, 1)
                dve.wait_ge(top_chain, t + 1)
                apart(dve)
                V.max_index(top_i[:, k], top[:, k], ps_r[:, D:D + E]).then_inc(top_ready, 1)

            def slots(t, j):
                k = j % 2
                dve.wait_ge(rank_ps, t + 1)
                dve.wait_ge(ex_ready, t + 1)
                if not (isinstance(t, int) and t < 2):
                    dve.wait_ge(row_ready, t - 1)
                for c in range(2):
                    V.tensor_tensor_reduce(junk[:, c], ps_r[:, D + 16:D + 16 + E], hot[:, k, c], 1.0, 0.0, ALU.mult,
                                           ALU.add, slot_f[:, k, c:c + 1])
                V.tensor_scalar(den[:, 0:1], ex[:, k:k + 1], 1.0, None, ALU.add).then_inc(slot_chain, 1)
                dve.wait_ge(slot_chain, t + 1)
                V.reciprocal(den[:, 1 + k:2 + k], den[:, 0:1]).then_inc(slots_ready, 1)

            def routing(qb, j):
                t2, _ = routed(qb, j, 2)
                t3, j3 = routed(qb, j, 3)
                t4, j4 = routed(qb, j, 4)
                live = lambda t: t is not None and (not isinstance(t, int) or t < NT)
                if live(t2) and live(t3):
                    dve.wait_ge(x2t_sb, t2 + 1)
                if live(t3):
                    choose(t3, j3)
                if t4 is not None:
                    slots(t4, j4)

            def t1_half(qb, j):
                return 2 * qb + (j - 1) // 2 + 1

            x_statistics(0, 0)
            x_normalise(0, 0)
            dve.wait_ge(wstage_hi, 2)
            low(wb_lo[:].rearrange("p c n -> p (c n)"), ps_x[:], wb_hi[:].rearrange("p c n -> p (c n)")
                ).then_inc(wstage_sb, 1)
            x_statistics(0, 1)
            xs_low(0, 0)
            x_normalise(0, 1)
            v_low(0, 0)
            xs_low(0, 1)
            v_low(0, 1)
            q_low_first(0)
            q_low_rest(0)
            dve.wait_ge(consts_ready, 1)
            save_diagonal(0, 0, 0)
            negate_max(0, 0, 1)

            def weights_low(lo, hi, hi_done, done, i, e):
                dve.wait_ge(hi_done, i + 1)
                flat = lambda m: m[:, e].rearrange("p c n -> p (c n)")
                V.tensor_tensor(flat(lo), flat(lo).bitcast(F32), flat(hi).bitcast(F32), ALU.subtract).then_inc(done, 1)

            def body(qb):
                nxt = has_next(qb)
                for j in range(TB):
                    t, n0, n1 = tile(qb, j), chunk0(qb, j), chunk0(qb, j) + qb + 1
                    t1, j1 = routed(qb, j, 1)
                    pt_low(n0, j + 1)
                    if j < TB - 1:
                        save_diagonal(n1, qb, j + 1)
                    elif nxt:
                        save_diagonal(n1, qb + 1, 0)
                        save_scores(n1 + 1, 0, qb * QB)
                    if nxt and j == 0:
                        x_statistics(qb + 1, 0)
                    if nxt and j == 1:
                        xs_low(qb + 1, 0)
                    if nxt and j == 2:
                        v_low(qb + 1, 0)
                        xs_low(qb + 1, 1)
                    if nxt and j == 3:
                        v_low(qb + 1, 1)

                    def chunk(kc):
                        pt_low(n0 + 1 + kc, TB)
                        if j < TB - 1:
                            save_scores(n1 + 1 + kc, j + 1, kc * QB)
                        elif nxt:
                            save_scores(n1 + 2 + kc, 0, kc * QB)

                    if not (isinstance(qb, int) and qb == 0):
                        chunk(0)
                    routing(qb, j)
                    if not (isinstance(qb, int) and qb < 2):
                        chunk(1)
                    if t1 is not None:
                        attention_out(t1, j1, n0, t1_half(qb, j))
                    if nxt and j == 1:
                        x_normalise(qb + 1, 1)
                    if not nxt and j == TB - 1:
                        for kc in range(2, NB - 1):
                            chunk(kc)
                            weights_low(w1_lo, w1_hi, w1_hi_done, w1_done, kc - 2, kc - 2)
                    elif not (isinstance(qb, int) and qb <= 2):
                        with dve.Fori(2, qb) as kc:
                            chunk(kc)
                    if j < TB - 1:
                        negate_max(t + 1, j + 1, n1 + qb + 1)
                    elif nxt:
                        negate_max(t + 1, 0, n1 + qb + 2)
                    if t1 is not None:
                        x2_normalise(t1, j1, qb if j >= 1 else qb - 1)
                    if nxt and j == 0:
                        x_normalise(qb + 1, 0)
                        x_statistics(qb + 1, 1)
                    if nxt and j == 2:
                        q_low_first(qb + 1)
                    if nxt and j == 3:
                        q_low_rest(qb + 1)

            body(0)
            body(1)
            body(2)
            with dve.Fori(3, NB - 1) as qb:
                body(qb)
            body(NB - 1)
            attention_out(NT - 1, TB - 1, chunk0(NB, 0), NT // 2)
            x2_normalise(NT - 1, TB - 1, NB - 1)

            for j in range(4):
                routing(NB, j)
                if j == 0:
                    for e in range(E - 3, E):
                        weights_low(w1_lo, w1_hi, w1_hi_done, w1_done, e, e)
                elif j < 3:
                    for i in (2 * j - 2, 2 * j - 1):
                        weights_low(w2_lo, w2_hi, w2_hi_done, w2_done, i, W2_ORDER[i])

            link_n = [0]

            def link(ins):
                link_n[0] += 1
                ins.then_inc(tab_chain, 1)
                dve.wait_ge(tab_chain, link_n[0])

            dve.wait_ge(counts_ps, 1)
            V.tensor_copy(pad_slot[:], ps_s[:, 0:E]).then_inc(pads_ready, 1)
            link(V.scalar_tensor_tensor(cnt[:, 0], iota_e[:], -float(REGION), ps_s[:, 0:E], ALU.mult, ALU.add))
            link(V.tensor_scalar(cnt[:, 1], cnt[:, 0], 1.0 / P, (P - 1.0) / P - 127.5 / 256, ALU.mult, ALU.add))
            link(V.tensor_copy(cnt_i[:], cnt[:, 1]))
            link(V.tensor_copy(cnt[:, 2], cnt_i[:]))
            link(V.tensor_tensor_scan(cnt[:, 3], ones[:, 0:E], cnt[:, 2], 0.0, ALU.mult, ALU.add))
            over_t = lambda ap: ap[:, None, :].to_broadcast([P, FT, E])
            link(V.tensor_tensor(past[:], iota_t[:, :, None].to_broadcast([P, FT, E]), over_t(cnt[:, 3]), ALU.is_ge))
            V.tensor_reduce(tmpf[:, 0, :], past[:], AX.X, ALU.add)
            link(V.tensor_scalar(cnt[:, 1], cnt[:, 2], -float(P), float(REGION), ALU.mult, ALU.add))
            V.tensor_tensor(past_tiles[:], past[:], over_t(cnt[:, 2]), ALU.mult)
            link(V.tensor_tensor(past[:], past[:], over_t(cnt[:, 1]), ALU.mult))
            link(V.tensor_reduce(tmpf[:, 1, :], past[:], AX.X, ALU.add))
            link(V.scalar_tensor_tensor(tmpf[:, 1, :], iota_t[:], float(P), tmpf[:, 1, :], ALU.mult, ALU.add))
            V.tensor_scalar(tile_e[:], tmpf[:, 0, :], E - 1.0, None, ALU.min)
            link(V.tensor_scalar(tmpf[:, 1, :], tmpf[:, 1, :], float(ZERO_TILE), None, ALU.min))
            V.tensor_copy(tab_rows[:], tmpf[:, 1, :]).then_inc(tab_ready, 1)
            link(V.tensor_tensor(digit[:], digit[:], tile_e[:].rearrange("p (r u) -> p r u", u=FU), ALU.mult))
            link(V.tensor_reduce(cnt_w[:], digit[:], AX.X, ALU.add))
            V.tensor_copy(tab_words[:], cnt_w[:]).then_inc(tab_ready, 1)
            V.tensor_reduce(tmpf[:, 1, :], past_tiles[:], AX.X, ALU.add)
            link(V.tensor_scalar(tmpf[:, 0, :], tmpf[:, 0, :], float(E), float(FT), ALU.is_ge, ALU.mult))
            link(V.tensor_tensor(tmpf[:, 1, :], tmpf[:, 0, :], tmpf[:, 1, :], ALU.add))
            link(V.tensor_tensor(tmpf[:, 1, :], tmpf[:, 1, :], iota_t[:], ALU.min))
            V.tensor_copy(fence[:], tmpf[:, 1, :]).then_inc(tab_ready, 1)

            def add_b1(t, u, e):
                dve.wait_ge(h_ps, t + 1)
                if not (isinstance(t, int) and t < 2):
                    dve.wait_ge(ht_ps, t - 1)
                V.tensor_tensor(h_sb[:, u % 2], ps[:, u % 2, :],
                                b1_sb[:, bass.ds(e, 1), :].rearrange("p a n -> p (a n)"), ALU.add).then_inc(h_done, 1)

            def fx_low(t, u):
                dve.wait_ge(fx_hi_done, t + 1)
                low(fx_lo[:, u % 2].rearrange("p c n -> p (c n)"), ps[:, 2 + u % 2, 0:D],
                    fx_hi[:, u % 2].rearrange("p c n -> p (c n)")).then_inc(fx_done, 1)

            def ht_low(t, u):
                dve.wait_ge(ht_hi_done, t + 1)
                V.scalar_tensor_tensor(ht_lo[:, u % 2].rearrange("p c n -> p (c n)"), ps[:, 4 + u % 2, :], 0.0,
                                       ht_hi[:, u % 2].rearrange("p c n -> p (c n)").bitcast(F32), ALU.max,
                                       ALU.subtract).then_inc(ht_done, 1)

            def add_b2(t, u, e):
                dve.wait_ge(y_ps, t + 1)
                if not (isinstance(t, int) and t < 2):
                    dve.wait_ge(y_done, t - 1)
                V.tensor_tensor(y_b[:, u % 2], ps[:, 6 + u % 2, 0:D],
                                b2_sb[:, bass.ds(e, 1), :].rearrange("p a n -> p (a n)"), ALU.add).then_inc(y_biased, 1)

            for i in range(4, E):
                if i == E - 2:
                    fx_low(0, 0)
                weights_low(w2_lo, w2_hi, w2_hi_done, w2_done, i, W2_ORDER[i])
            dve.wait_ge(fb_loaded, 32)

            def turn(t, u):
                add_b1(t, u, expert(words, u))
                if not (isinstance(t, int) and t == FT - 1):
                    fx_low(t + 1, (u + 1) % FU)
                if not (isinstance(t, int) and t < 2):
                    add_b2(t - 2, (u - 2) % FU, expert(words, u - 2))
                ht_low(t, u)

            regs = word_registers(dve)
            load_word(dve, regs, 0)
            dve.reg_mov(regs[0], regs[1])
            words = next_words(dve, regs)
            load_word(dve, regs, 1)
            for u in range(FU):
                turn(u, u)
            with dve.Fori(1, FT // FU - 1) as r:
                words = next_words(dve, regs)
                for u in range(FU):
                    turn(r * FU + u, u)
                    if u == FU // 2:
                        load_word(dve, regs, r + 1)
            words = next_words(dve, regs)
            for u in range(FU):
                turn(FT - FU + u, u)
            for u in (FU - 2, FU - 1):
                add_b2(FT - FU + u, u, expert(words, u))

        @block.gpsimd
        def _(pool):
            G = nc.gpsimd
            n = [0]

            def link(ins):
                n[0] += 1
                ins.then_inc(pool_chain, 1)
                pool.wait_ge(pool_chain, n[0])

            G.memset(ident[:], 0.0).then_inc(pool_chain, 1)
            G.memset(upper[:], 0.0).then_inc(pool_chain, 1)
            G.memset(causal[:], LOW).then_inc(pool_chain, 1)
            G.memset(half_neg[:], -0.5).then_inc(pool_chain, 1)
            G.memset(sums[:], 0.0).then_inc(pool_chain, 1)
            G.memset(pad_row[:], 0.0).then_inc(pool_chain, 1)
            G.memset(cum[:], 0.0).then_inc(pool_chain, 1)
            G.memset(ones[:], 1.0).then_inc(pool_chain, 1)
            n[0] = 8
            pool.wait_ge(pool_chain, 8)
            link(G.affine_select(out=ident[:], in_=ident[:], compare_op=ALU.not_equal, fill=1.0, base=0,
                                 pattern=[[-1, P]], channel_multiplier=1))
            link(G.affine_select(out=upper[:], in_=upper[:], compare_op=ALU.is_ge, fill=1.0, base=0,
                                 pattern=[[-1, P]], channel_multiplier=1))
            link(G.affine_select(out=causal[:], in_=causal[:], compare_op=ALU.is_gt, fill=0.0, base=0,
                                 pattern=[[1, P]], channel_multiplier=-1))
            link(G.iota(iota_e[:], pattern=[[1, E]], base=0, channel_multiplier=0, allow_small_or_imprecise_dtypes=True))
            link(G.iota(iota_t[:], pattern=[[1, FT]], base=0, channel_multiplier=0, allow_small_or_imprecise_dtypes=True))
            link(G.iota(lane[:], pattern=[[1, 1]], base=0, channel_multiplier=1, allow_small_or_imprecise_dtypes=True))
            link(G.iota(tok_ids[:], pattern=[[P, NT]], base=0, channel_multiplier=1))
            link(G.iota(pad_row[:, C_TOK:C_TOK + 1].bitcast(I32), pattern=[[1, 1]], base=S, channel_multiplier=1))
            link(G.tensor_scalar(cum[0:1, :], iota_e[0:1, :], float(REGION), None, ALU.mult))
            for u in range(FU):
                G.memset(digit[:, :, u:u + 1], float(E ** u))
            G.tensor_copy(slot_f[:, 0], half_neg[:]).then_inc(consts_ready, 1)
            for k in range(2):
                half = slice(k * P // 2, (k + 1) * P // 2)
                pool.dma_start(xg[ZERO_TILE + k * P // 2:ZERO_TILE + (k + 1) * P // 2, :], pad_row[half]
                               ).then_inc(added[k], 16)

            def x_rsqrt(nb, k):
                p = 2 * nb + k
                pool.wait_ge(x_stats, p + 1)
                if not (isinstance(nb, int) and nb == 0 and k == 0):
                    pool.wait_ge(x_normed, p)
                apart(pool)
                G.tensor_scalar(rstd[:, :, 0:1], mv[:, :, 1:2], EPS, None, ALU.add).then_inc(x_eps, 1)
                pool.wait_ge(x_eps, p + 1)
                G.tensor_tensor(rstd[:, :, 1:2], rstd[:, :, 0:1], half_neg[:].rearrange("p (a b) -> p a b", b=1), ALU.pow
                                ).then_inc(x_rstd, 1)

            x_rsqrt(0, 0)
            x_rsqrt(0, 1)

            def x1_rsqrt(t, j):
                k = j % 2
                pool.wait_ge(x1_stats, t + 1)
                if not (isinstance(t, int) and t < 2):
                    pool.wait_ge(x2_ready, t - 1)
                G.tensor_tensor(rstd2[:, k, 1:2], rstd2[:, k, 0:1], half_neg[:, 0:1], ALU.pow).then_inc(rstd2_ready, 1)

            def one_hots(t, j):
                k = j % 2
                pool.wait_ge(top_ready, t + 1)
                if not (isinstance(t, int) and t == 0):
                    add_choices(t - 1)
                if not (isinstance(t, int) and t < 2):
                    pool.wait_ge(slots_ready, t - 1)
                apart(pool)
                G.tensor_copy(top_f[:, k], top_i[:, k, 0:2]).then_inc(hot_chain, 1)
                pool.wait_ge(hot_chain, 3 * t + 1)
                apart(pool)
                G.tensor_copy(rows[:, j, C_E1:C_E1 + 1], top_f[:, k, 0:1])
                for c in range(2):
                    G.tensor_scalar(hot[:, k, c], iota_e[:], top_f[:, k, c:c + 1], None, ALU.is_equal
                                    ).then_inc(hot_chain, 1)
                pool.wait_ge(hot_chain, 3 * t + 3)
                G.tensor_tensor(mask[:], hot[:, k, 0], hot[:, k, 1], ALU.add).then_inc(hot_ready, 1)

            def add_choices(t):
                pool.wait_ge(rank_ps, t + 1)
                pool.wait_ge(hot_ready, t + 1)
                G.tensor_tensor(cum[:], cum[:], mask[:], ALU.add).then_inc(cum_ready, 1)
                pool.wait_ge(cum_ready, t + 1)

            def prepare_row(t, j):
                k = j % 2
                pool.wait_ge(slots_ready, t + 1)
                apart(pool)
                G.tensor_tensor(rows[:, j, C_G2:C_G2 + 1], ex[:, k:k + 1], den[:, 1 + k:2 + k], ALU.mult
                                ).then_inc(row_chain, 1)
                G.tensor_copy(slot_i[:, j], slot_f[:, k])
                G.tensor_copy(rows[:, j, C_TOK:C_TOK + 1].bitcast(I32), tok_ids[:, bass.ds(t, 1)])
                pool.wait_ge(row_chain, t + 1)
                apart(pool)
                G.tensor_scalar(rows[:, j, C_GD:C_GD + 1], rows[:, j, C_G2:C_G2 + 1], -2.0, 1.0, ALU.mult, ALU.add
                                ).then_inc(row_ready, 1)

            def scatter(t, j):
                pool.wait_ge(row_ready, t + 1)
                apart(pool)
                for c in range(2):
                    G.indirect_dma_start(out=xg, out_offset=bass.IndirectOffsetOnAxis(ap=slot_i[:, j, c:c + 1].bitcast(U32), axis=0),
                                         in_=rows[:, j, :], in_offset=None).then_inc(scattered[j], 16)

            def body(qb):
                nxt = has_next(qb)
                for j in range(TB):
                    if nxt and j < 2:
                        x_rsqrt(qb + 1, j)
                    t1, j1 = routed(qb, j, 1)
                    t3, j3 = routed(qb, j, 3)
                    t4, j4 = routed(qb, j, 4)
                    if t3 is not None:
                        one_hots(t3, j3)
                    if t1 is not None:
                        x1_rsqrt(t1, j1)
                    if t4 is not None:
                        prepare_row(t4, j4)
                        scatter(t4, j4)

            over_blocks(pool, body)
            x1_rsqrt(NT - 1, TB - 1)
            for j in range(4):
                t3, j3 = routed(NB, j, 3)
                t4, j4 = routed(NB, j, 4)
                if t3 < NT:
                    one_hots(t3, j3)
                prepare_row(t4, j4)
                scatter(t4, j4)

            for k in range(2):
                pool.wait_ge(x1_stored[k], 16 * (NT // 2))
            pool.wait_ge(tab_ready, 3)

            def read_columns(t, u, r):
                pool.wait_ge(xf_loaded[u], 16 * (r + 1))
                if not (isinstance(t, int) and t < FU):
                    pool.wait_ge(y_done, t - FU + 1)
                apart(pool)
                G.tensor_copy(dest[:, u:u + 1], xf[:, u, C_TOK:C_TOK + 1].bitcast(I32))
                G.tensor_copy(e_now[:, u:u + 1], tile_e[:, bass.ds(t, 1)]).then_inc(meta_chain, 1)
                pool.wait_ge(meta_chain, 3 * t + 1)
                apart(pool)
                G.tensor_scalar(gsel[:, u:u + 1], xf[:, u, C_E1:C_E1 + 1], e_now[:, u:u + 1], None, ALU.is_equal
                                ).then_inc(meta_chain, 1)
                pool.wait_ge(meta_chain, 3 * t + 2)
                G.tensor_tensor(gsel[:, u:u + 1], gsel[:, u:u + 1], xf[:, u, C_GD:C_GD + 1], ALU.mult).then_inc(meta_chain, 1)
                pool.wait_ge(meta_chain, 3 * t + 3)
                G.tensor_tensor(gate[:, u:u + 1], gsel[:, u:u + 1], xf[:, u, C_G2:C_G2 + 1], ALU.add).then_inc(gate_ready, 1)

            def add_rows(t, u):
                pool.wait_ge(y_done, t + 1)
                pool.wait_ge(gate_ready, t + 1)
                before = pool.value_load(fence[0:1, bass.ds(t, 1)], min_val=0, max_val=FT)
                for k in range(2):
                    pool.wait_ge(added[k], ((before + (1 - k)) >> 1) * 16 + 16)
                apart(pool)
                G.indirect_dma_start(out=out, out_offset=bass.IndirectOffsetOnAxis(ap=dest[:, u:u + 1].bitcast(U32), axis=0),
                                     in_=y_sb[:, u % 2], in_offset=None, compute_op=ALU.add).then_inc(added[u % 2], 16)

            def turn(t, u, r):
                read_columns(t, u, r)
                if not (isinstance(t, int) and t < 2):
                    add_rows(t - 2, (u - 2) % FU)

            for u in range(FU):
                turn(u, u, 0)
            with pool.Fori(1, FT // FU) as r:
                for u in range(FU):
                    turn(r * FU + u, u, r)
            for t in (FT - 2, FT - 1):
                add_rows(t, t % FU)
            for k in range(2):
                pool.wait_ge(added[k], 16 * (FT // 2 + 1))


_INS = ["L0_attn_in_features", "L0_attn_Wq", "L0_attn_Wk", "L0_attn_Wv", "L0_attn_Wo", "L0_ffn_Wg", "L0_ffn_W1",
        "L0_ffn_b1", "L0_ffn_W2", "L0_ffn_b2"]


def kernel(**inputs):
    import numpy as _np
    import concourse.bacc as _bacc
    from concourse import mybir as _mybir
    from concourse.bass_utils import run_bass_kernel_spmd as _run

    nc = _bacc.Bacc("TRN2", target_bir_lowering=False, num_devices=1)
    arrays, args = {}, []
    for name in _INS:
        a = _np.ascontiguousarray(inputs[name])
        arrays[f"in_{name}"] = a
        args.append(nc.dram_tensor(f"in_{name}", a.shape, _mybir.dt.from_np(a.dtype), kind="ExternalInput").ap())
    args.append(nc.dram_tensor("out_0", (OUT_ROWS, D), _mybir.dt.float32, kind="ExternalOutput").ap())
    moe_block(nc, *args)
    r = _run(nc, [arrays], core_ids=[0])
    return r.results[0]["out_0"][:S].reshape(1, S, D)
```

```python
from contextlib import ExitStack

import numpy as np
import concourse.bass as bass
from concourse import mybir

F32, F32R, I32, U32 = (mybir.dt.float32, mybir.dt.float32r, mybir.dt.int32, mybir.dt.uint32)
ALU, ACT, AX = mybir.AluOpType, mybir.ActivationFunctionType, mybir.AxisListType

P = 128
S, D, E, H = 4096, 256, 8, 512
DC, HC = D // P, H // P
QB = 512
NB = S // QB
TB = QB // P
NT = S // P
NP2 = NT // 2
SCALE = 1.0 / float(np.sqrt(D))
EPS = 1e-5
LOW = -3.0e38
REGION = S + P
ZERO_TILE = E * REGION
ROW = D + 4
C_TOK, C_E1, C_GD, C_G2 = D, D + 1, D + 2, D + 3
FT = 2 * S // P + E
E_BITS = E.bit_length() - 1
FU = 8
W2_ORDER = (E - 1,) + tuple(range(E - 1))
LAST_PARTS = ((0, 4), (4, 6), (6, NB - 1))
OUT_ROWS = S + P


def chunk0(qb, j):
    return 2 * qb * (qb + 1) + j * (qb + 1)


def moe_block(nc, x, wq, wk, wv, wo, wg, w1, b1, w2, b2, out):
    xg = nc.dram_tensor("xg_rows", (ZERO_TILE + P, ROW), F32, kind="Internal").ap()
    x_tiles = x[0].rearrange("(n p) d -> p n d", p=P)
    out_tiles = out.rearrange("(n p) d -> p n d", p=P)
    es = ExitStack()
    with es:
        def sb(name, shape, dt=F32, stack=es):
            return stack.enter_context(nc.sbuf_tensor(name, shape, dt))

        def sem(name):
            return es.enter_context(nc.semaphore(name))

        ident = sb("ident", [P, P])
        ones = sb("ones", [P, P])
        upper = sb("upper", [P, P])
        causal = sb("causal", [P, P])
        half_neg = sb("half_neg", [P, 2])
        iota_e = sb("iota_e", [P, E])
        lane = sb("lane", [P, 1])
        tok_ids = sb("tok_ids", [P, NT], I32)
        wg_sb = sb("wg_sb", [P, DC, E])
        cum = sb("cum", [P, E])
        pad_row = sb("pad_row", [P, ROW])
        tile_e = sb("tile_e", [P, FT])
        tab_rows = sb("tab_rows", [P, FT], I32)
        tab_words = sb("tab_words", [P, FT // FU], I32)
        fence = sb("fence", [P, FT], I32)
        digit = sb("digit", [P, FT // FU, FU])
        cnt = sb("cnt", [P, 4, E])
        cnt_i = sb("cnt_i", [P, E], I32)
        pad_slot = sb("pad_slot", [P, E], I32)
        tmpf = sb("tmpf", [P, 2, FT])
        iota_t = sb("iota_t", [P, FT])

        at = es.enter_context(ExitStack())
        A = lambda name, shape, dt=F32: sb(name, shape, dt, at)
        xt_hi, xt_lo = (A(n, [P, DC, S], F32R) for n in ("xt_hi", "xt_lo"))
        v_hi, v_lo = (A(n, [P, NT, D], F32R) for n in ("v_hi", "v_lo"))
        wa_hi, wa_lo, wb_hi, wb_lo = (A(n, [P, DC, D], F32R) for n in ("wa_hi", "wa_lo", "wb_hi", "wb_lo"))
        q_hi, q_lo = (A(n, [P, DC, QB], F32R) for n in ("q_hi", "q_lo"))
        s_sb = A("s_sb", [P, 2, S - QB])
        s_diag = A("s_diag", [P, 2, QB])
        probs = A("probs", [P, QB])
        pt_hi, pt_lo = (A(n, [P, TB, P], F32R) for n in ("pt_hi", "pt_lo"))
        x_in = A("x_in", [P, 2, 2, D])
        xn = A("xn", [P, 2, D])
        xs_hi, xs_lo = (A(n, [P, DC, 2 * P], F32R) for n in ("xs_hi", "xs_lo"))
        x_res = A("x_res", [P, 2, D])
        x1 = A("x1", [P, 2, D])
        rows = A("rows", [P, 4, ROW])
        x2t = A("x2t", [P, DC, P])
        stat = A("stat", [P, 2, 6])
        mv = A("mv", [P, 2, 2])
        rstd = A("rstd", [P, 2, 2])
        stat2 = A("stat2", [P, 6])
        mv2 = A("mv2", [P, 2, 2])
        rstd2 = A("rstd2", [P, 2, 2])
        run_max = A("run_max", [P, 2])
        neg_max = A("neg_max", [P, 2])
        sums = A("sums", [P, 2, 8])
        lsum = A("lsum", [P, 2])
        top = A("top", [P, 2, 8])
        top_i = A("top_i", [P, 2, 8], U32)
        top_f = A("top_f", [P, 2, 2])
        hot = A("hot", [P, 2, 2, E])
        mask = A("mask", [P, E])
        junk = A("junk", [P, 2, E])
        slot_f = A("slot_f", [P, 2, 2])
        slot_i = A("slot_i", [P, 4, 2], I32)
        ex = A("ex", [P, 2])
        den = A("den", [P, 3])
        raw = s_sb[:, 1, 0:4 * DC * D].rearrange("p (w c n) -> p w c n", w=4, c=DC)
        wot = s_sb[:, 1, 4 * DC * D:5 * DC * D].rearrange("p (c n) -> p c n", c=DC)
        at.close()

        ff = es.enter_context(ExitStack())
        B = lambda name, shape, dt=F32: sb(name, shape, dt, ff)
        w1_hi, w1_lo = (B(n, [P, E, DC, H], F32R) for n in ("w1_hi", "w1_lo"))
        w2_hi, w2_lo = (B(n, [P, E, HC, D], F32R) for n in ("w2_hi", "w2_lo"))
        b1_sb = B("b1_sb", [P, E, H])
        b2_sb = B("b2_sb", [P, E, D])
        past = B("past", [P, FT, E])
        past_tiles = B("past_tiles", [P, FT, E])
        cnt_w = B("cnt_w", [P, FT // FU])
        xf = B("xf", [P, FU, ROW])
        fx_hi, fx_lo = (B(n, [P, 2, DC, P], F32R) for n in ("fx_hi", "fx_lo"))
        h_sb = B("h_sb", [P, 2, H])
        ht_hi, ht_lo = (B(n, [P, 2, HC, P], F32R) for n in ("ht_hi", "ht_lo"))
        y_b = B("y_b", [P, 2, D])
        y_sb = B("y_sb", [P, 2, D])
        gate = B("gate", [P, FU])
        gsel = B("gsel", [P, FU])
        dest = B("dest", [P, FU], I32)
        e_now = B("e_now", [P, FU])

        ps = es.enter_context(nc.psum_tensor("ps", [P, 8, 512], F32))
        ps_s = ps[:, 0, :]
        ps_pt = ps[:, 1:3, 0:2 * P]
        ps_o = ps[:, 3:5, 0:D]
        ps_x, ps_v, ps_r = ps[:, 5, :], ps[:, 6, :], ps[:, 7, :]

        ps_a, ps_wot, ps_b = ps[:, 0, :], ps[:, 1, :], ps[:, 2, :]

        consts_ready, wqk_loaded, wvo_loaded, wg_loaded = map(
            sem, ("consts_ready", "wqk_loaded", "wvo_loaded", "wg_loaded"))
        wstage_ps, wstage_sb, wstage_hi = map(sem, ("wstage_ps", "wstage_sb", "wstage_hi"))
        x_loaded = [sem("x_loaded0"), sem("x_loaded1")]
        x_stats, x_stats1, x_rstd, x_normed = map(sem, ("x_stats", "x_stats1", "x_rstd", "x_normed"))
        xt_ps, xs_hi_done, xs_done = map(sem, ("xt_ps", "xs_hi_done", "xs_done"))
        xt_stored = [sem("xt_stored0"), sem("xt_stored1")]
        v_ps, v_hi_done, v_done = map(sem, ("v_ps", "v_hi_done", "v_done"))
        q_ps, q_hi_done, q_done = map(sem, ("q_ps", "q_hi_done", "q_done"))
        scores_ps, scores_saved, max_ready, probs_ready = map(
            sem, ("scores_ps", "scores_saved", "max_ready", "probs_ready"))
        pt_ps, pt_hi_done, pt_done, pv_done = map(sem, ("pt_ps", "pt_hi_done", "pt_done", "pv_done"))
        diag_part = sem("diag_part")
        res_loaded = [sem("res_loaded0"), sem("res_loaded1")]
        x1_chain, x1_done, x1_stats, rstd2_ready = map(sem, ("x1_chain", "x1_done", "x1_stats", "rstd2_ready"))
        x1_stored = [sem("x1_stored0"), sem("x1_stored1")]
        x2_ready, x2t_ps, x2t_sb, logits_ps = map(sem, ("x2_ready", "x2t_ps", "x2t_sb", "logits_ps"))
        top_chain, top_ready, hot_chain, hot_ready = map(sem, ("top_chain", "top_ready", "hot_chain", "hot_ready"))
        ex_ready, rank_ps, cum_ready, slot_chain, slots_ready = map(
            sem, ("ex_ready", "rank_ps", "cum_ready", "slot_chain", "slots_ready"))
        scattered = [sem(f"scattered{i}") for i in range(4)]
        pool_chain, x_eps, row_chain, row_ready = map(sem, ("pool_chain", "x_eps", "row_chain", "row_ready"))
        counts_ps, tab_chain, tab_ready = map(sem, ("counts_ps", "tab_chain", "tab_ready"))
        pads_ready, padded = sem("pads_ready"), sem("padded")
        w1_loaded = [sem(f"w1_loaded{e}") for e in range(E)]
        w2_loaded = [sem(f"w2_loaded{e}") for e in range(E)]
        fb_loaded, w1_hi_done, w2_hi_done, w1_done, w2_done = map(
            sem, ("fb_loaded", "w1_hi_done", "w2_hi_done", "w1_done", "w2_done"))
        xf_loaded = [sem(f"xf_loaded{i}") for i in range(FU)]
        fx_ps, fx_hi_done, fx_done = map(sem, ("fx_ps", "fx_hi_done", "fx_done"))
        h_ps, h_done, ht_ps, ht_hi_done, ht_done = map(sem, ("h_ps", "h_done", "ht_ps", "ht_hi_done", "ht_done"))
        y_ps, y_biased, y_done = map(sem, ("y_ps", "y_biased", "y_done"))
        added = [sem("added0"), sem("added1")]
        meta_chain, gate_ready = sem("meta_chain"), sem("gate_ready")
        block = es.enter_context(nc.Block())

        def over_blocks(eng, body):
            body(0)
            with eng.Fori(1, NB - 1) as qb:
                body(qb)
            body(NB - 1)

        def over_chunks(eng, qb, body):
            if isinstance(qb, int) and qb == 0:
                return
            with eng.Fori(0, qb) as kc:
                body(kc)

        def has_next(qb):
            return not (isinstance(qb, int) and qb == NB - 1)

        def tile(qb, j):
            return qb * TB + j

        def routed(qb, j, back):
            if isinstance(qb, int):
                t = tile(qb, j) - back
                return (t if t >= 0 else None), t % TB
            return tile(qb, j) - back, (j - back) % TB

        def apart(eng):
            eng.nop(nofuse=True)

        def word_registers(eng):
            return [eng.alloc_register(f"{w}_word_{eng.engine.name}") for w in ("last", "next")]

        def load_word(eng, regs, r):
            eng.load(regs[1], tab_words[0:1, bass.ds(r, 1)])

        def next_words(eng, regs):
            words = [eng.snap(reg) for reg in regs]
            eng.reg_mov(regs[0], regs[1])
            return words

        def expert(words, u):
            return (words[1 if u >= 0 else 0] >> (E_BITS * (u % FU))) & (E - 1)

        def pad(eng, e):
            row0 = eng.value_load(pad_slot[0:1, e:e + 1], min_val=0, max_val=ZERO_TILE)
            eng.dma_start(xg[bass.ds(row0, P), :], pad_row[:]).then_inc(padded, 16)

        def to3(ap, n):
            return ap.rearrange("p (c n) -> p c n", n=n)

        @block.sync
        def _(sp):
            for n, w in enumerate((wq, wk, wv, wo)):
                sp.dma_start(raw[:, n], w.rearrange("(c p) n -> p c n", p=P)
                             ).then_inc(wqk_loaded if n < 2 else wvo_loaded, 16)

            def load_pair(nb, k):
                if not (isinstance(nb, int) and nb == 0):
                    sp.wait_ge(x_normed, 2 * nb + k - 1)
                sp.dma_start(x_in[:, k], x_tiles[:, bass.ds(2 * (2 * nb + k), 2), :]).then_inc(x_loaded[k], 16)

            def load_residual(t, j):
                if not (isinstance(t, int) and t < 2):
                    sp.wait_ge(x1_done, t - 1)
                sp.dma_start(x_res[:, j % 2], x_tiles[:, bass.ds(t, 1), :].rearrange("p a d -> p (a d)")
                             ).then_inc(res_loaded[j % 2], 16)

            def store_xt(nb, k):
                sp.wait_ge(xs_done, 2 * nb + k + 1)
                at_tok = bass.ds((2 * nb + k) * 2 * P, 2 * P)
                sp.dma_start(xt_hi[:, :, at_tok].bitcast(F32), xs_hi[:].bitcast(F32)).then_inc(xt_stored[k], 16)
                sp.dma_start(xt_lo[:, :, at_tok].bitcast(F32), xs_lo[:].bitcast(F32)).then_inc(xt_stored[k], 16)

            def store_x1(t, j):
                sp.wait_ge(x1_done, t + 1)
                sp.dma_start(out_tiles[:, bass.ds(t, 1), :].rearrange("p a d -> p (a d)"), x1[:, j % 2]
                             ).then_inc(x1_stored[j % 2], 16)

            def load_b1(half):
                some = slice(half * E // 2, (half + 1) * E // 2)
                sp.dma_start(b1_sb[:, some], b1[None, some, :].to_broadcast([P, E // 2, H])).then_inc(fb_loaded, 16)

            def load_w1_and_biases():
                sp.wait_ge(scores_saved, chunk0(NB, 0))
                for e in range(E):
                    sp.dma_start(w1_lo[:, e].bitcast(F32), w1[e].rearrange("(c p) n -> p c n", p=P)
                                 ).then_inc(w1_loaded[e], 16)
                load_b1(1)
                sp.wait_ge(probs_ready, chunk0(NB - 1, TB - 1))
                sp.dma_start(b2_sb[:], b2[None, :, :].to_broadcast([P, E, D])).then_inc(fb_loaded, 16)

            sp.dma_start(wg_sb[:], wg.rearrange("(c p) e -> p c e", p=P)).then_inc(wg_loaded, 16)
            load_residual(0, 0)
            store_xt(0, 0)
            load_pair(1, 0)
            store_xt(0, 1)
            load_pair(1, 1)

            def body(qb):
                nxt = has_next(qb)
                if nxt and not (isinstance(qb, int) and qb == 0):
                    load_pair(qb + 1, 0)
                    load_pair(qb + 1, 1)
                for j in range(TB):
                    t1, j1 = routed(qb, j, 1)
                    if nxt and j in (1, 2):
                        store_xt(qb + 1, j - 1)
                    if not nxt and j == 0:
                        sp.wait_ge(q_ps, 2 * NB)
                        load_b1(0)
                    if not nxt and j == TB - 1:
                        load_w1_and_biases()
                    if t1 is not None:
                        store_x1(t1, j1)
                    if nxt or j < TB - 1:
                        load_residual(tile(qb, j) + 1, (j + 1) % TB)

            over_blocks(sp, body)
            for i, e in enumerate(W2_ORDER):
                sp.wait_ge(pv_done, chunk0(NB - 1, TB - 1) + i + 1)
                sp.dma_start(w2_lo[:, e].bitcast(F32), w2[e].rearrange("(c p) n -> p c n", p=P)
                             ).then_inc(w2_loaded[e], 16)
            store_x1(NT - 1, TB - 1)

            sp.wait_ge(pads_ready, 1)
            for e in range(E // 2):
                pad(sp, e)

            sp.wait_ge(tab_ready, 1)
            for k in range(4):
                sp.wait_ge(scattered[k], 32 * (NT // 4))
            for k in range(2):
                sp.wait_ge(added[k], 16)
                sp.wait_ge(x1_stored[k], 16 * (NT // 2))
            sp.wait_ge(padded, 16 * E)

            def load_rows(t, u, first):
                if not first:
                    sp.wait_ge(fx_ps, t - FU + 1)
                    sp.wait_ge(gate_ready, t - FU + 1)
                row0 = sp.value_load(tab_rows[0:1, bass.ds(t, 1)], min_val=0, max_val=ZERO_TILE)
                sp.dma_start(xf[:, u, :], xg[bass.ds(row0, P), :]).then_inc(xf_loaded[u], 16)

            for u in range(FU):
                load_rows(u, u, True)
            with sp.Fori(1, FT // FU) as r:
                for u in range(FU):
                    load_rows(r * FU + u, u, False)
            for k in range(2):
                sp.wait_ge(added[k], 16 * (FT // 2 + 1))

        @block.tensor
        def _(pe):
            def three(dst, pairs, start=True, stop=True, check=True):
                n = 3 * len(pairs)
                k = 0
                for (a_hi, a_lo), (b_hi, b_lo) in pairs:
                    for a, b in ((a_hi, b_hi), (a_hi, b_lo), (a_lo, b_hi)):
                        ins = nc.tensor.matmul(dst, a, b, start=start and k == 0, stop=stop and k == n - 1,
                                               skip_group_check=not check)
                        k += 1
                return ins

            pe.wait_ge(wqk_loaded, 32)
            for ic in range(DC):
                for oc in range(DC):
                    ins = nc.tensor.matmul(ps_a[:, ic * D:(ic + 1) * D], raw[:, 0, oc, ic * P:(ic + 1) * P],
                                           raw[:, 1, oc, :], start=(oc == 0), stop=(oc == DC - 1))
            ins.then_inc(wstage_ps, 1)
            pe.wait_ge(consts_ready, 1)
            pe.wait_ge(wvo_loaded, 32)
            for oc in range(DC):
                for cc in range(DC):
                    ins = nc.tensor.transpose(ps_wot[:, oc * D + cc * P:oc * D + (cc + 1) * P],
                                              raw[:, 3, cc, oc * P:(oc + 1) * P], ident[:])
            ins.then_inc(wstage_ps, 1)
            def transpose_pair(nb, k):
                p = 2 * nb + k
                pe.wait_ge(x_normed, p + 1)
                if k == 1:
                    pe.wait_ge(xs_done, p)
                elif not (isinstance(nb, int) and nb == 0):
                    pe.wait_ge(q_done, 2 * nb)
                for c in range(DC):
                    for a in range(2):
                        ins = nc.tensor.transpose(ps_x[:, c * 2 * P + a * P:c * 2 * P + (a + 1) * P],
                                                  xn[:, a, c * P:(c + 1) * P], ident[:])
                ins.then_inc(xt_ps, 1)

            def values(nb, k):
                p = 2 * nb + k
                pe.wait_ge(xs_done, p + 1)
                if not (isinstance(nb, int) and nb == 0 and k == 0):
                    pe.wait_ge(v_done, p)
                for a in range(2):
                    tok = slice(a * P, (a + 1) * P)
                    ins = three(ps_v[:, a * D:(a + 1) * D],
                                [((xs_hi[:, c, tok], xs_lo[:, c, tok]), (wb_hi[:, c], wb_lo[:, c]))
                                 for c in range(DC)])
                ins.then_inc(v_ps, 1)

            def queries(nb, k):
                pe.wait_ge(xt_stored[k], 32 * (nb + 1))
                if k == 0:
                    pe.wait_ge(xs_done, 2 * nb + 2)
                else:
                    pe.wait_ge(q_done, 2 * nb + 1)
                tok = bass.ds((2 * nb + k) * 2 * P, 2 * P)
                for m in range(DC):
                    col = slice(m * P, (m + 1) * P)
                    ins = three(ps_x[:, m * 2 * P:(m + 1) * 2 * P],
                                [((wa_hi[:, c, col], wa_lo[:, c, col]), (xt_hi[:, c, tok], xt_lo[:, c, tok]))
                                 for c in range(DC)])
                ins.then_inc(q_ps, 1)

            def scores(n, j, key0, width):
                if not (isinstance(n, int) and n == 0):
                    pe.wait_ge(scores_saved, n)
                q = slice(j * P, (j + 1) * P)
                keys = bass.ds(key0, width)
                three(ps_s[:, 0:width], [((q_hi[:, c, q], q_lo[:, c, q]), (xt_hi[:, c, keys], xt_lo[:, c, keys]))
                                         for c in range(DC)]).then_inc(scores_ps, 1)

            def transpose_probs(n, blocks):
                pe.wait_ge(probs_ready, n + 1)
                for b in range(blocks):
                    ins = nc.tensor.transpose(ps_pt[:, b // 2, (b % 2) * P:(b % 2 + 1) * P],
                                              probs[:, b * P:(b + 1) * P], ident[:])
                    if b == blocks - 1:
                        ins.then_inc(pt_ps, 2 if blocks <= 2 else 1)
                    elif b == 1:
                        ins.then_inc(pt_ps, 1)

            def weigh_values(n, j, blocks, v0, first, between=None):
                for b in range(blocks):
                    if b == 0:
                        pe.wait_ge(pt_done, 2 * n + (1 if blocks > 2 else 2))
                    if b == 2:
                        if between:
                            between()
                        pe.wait_ge(pt_done, 2 * n + 2)
                    ins = three(ps_o[:, j % 2], [((pt_hi[:, b], pt_lo[:, b]),
                                                  (v_hi[:, v0 + b] if isinstance(v0, int) else
                                                   v_hi[:, bass.ds(v0 + b, 1), :].rearrange("p a d -> p (a d)"),
                                                   v_lo[:, v0 + b] if isinstance(v0, int) else
                                                   v_lo[:, bass.ds(v0 + b, 1), :].rearrange("p a d -> p (a d)")))],
                                start=first and b == 0, stop=b == blocks - 1, check=False)
                ins.then_inc(pv_done, 1)

            def transpose_x2(t, j):
                pe.wait_ge(x2_ready, t + 1)
                for c in range(DC):
                    ins = nc.tensor.transpose(ps_r[:, c * P:(c + 1) * P], rows[:, j, c * P:(c + 1) * P], ident[:])
                ins.then_inc(x2t_ps, 1)

            def logits(t):
                pe.wait_ge(x2t_sb, t + 1)
                if isinstance(t, int) and t == 0:
                    pe.wait_ge(wg_loaded, 16)
                for c in range(DC):
                    ins = nc.tensor.matmul(ps_r[:, D:D + E], x2t[:, c], wg_sb[:, c], start=(c == 0), stop=(c == DC - 1))
                ins.then_inc(logits_ps, 1)

            def rank(t):
                pe.wait_ge(hot_ready, t + 1)
                nc.tensor.matmul(ps_r[:, D + 16:D + 16 + E], upper[:], mask[:], start=True, stop=False)
                nc.tensor.matmul(ps_r[:, D + 16:D + 16 + E], ones[:], cum[:], start=False, stop=True
                                 ).then_inc(rank_ps, 1)

            def routing(qb, j, last=NT - 1):
                t2, j2 = routed(qb, j, 2)
                t3, _ = routed(qb, j, 3)
                t4, _ = routed(qb, j, 4)
                t5, _ = routed(qb, j, 5)
                if t3 is not None:
                    pe.wait_ge(x2t_sb, t3 + 1)
                if t4 is not None:
                    pe.wait_ge(top_ready, t4 + 1)
                if t5 is not None:
                    pe.wait_ge(slots_ready, t5 + 1)
                if t4 is not None:
                    rank(t4)
                if t3 is not None:
                    logits(t3)
                if t2 is not None and (not isinstance(t2, int) or t2 <= last):
                    transpose_x2(t2, j2)

            transpose_pair(0, 0)
            pe.wait_ge(wstage_sb, 2)
            for dc in range(DC):
                for oc in range(DC):
                    ins = nc.tensor.matmul(ps_b[:, dc * D:(dc + 1) * D], raw[:, 2, oc, dc * P:(dc + 1) * P],
                                           wot[:, oc, :], start=(oc == 0), stop=(oc == DC - 1))
            ins.then_inc(wstage_ps, 1)
            pe.wait_ge(wstage_sb, 3)
            values(0, 0)
            transpose_pair(0, 1)
            values(0, 1)
            queries(0, 0)
            queries(0, 1)
            pe.wait_ge(q_done, 1)
            scores(0, 0, 0, P)

            def body(qb):
                nxt = has_next(qb)
                for j in range(TB):
                    t, n0, n1 = tile(qb, j), chunk0(qb, j), chunk0(qb, j) + qb + 1
                    if nxt and j >= 2:
                        values(qb + 1, j - 2)
                    routing(qb, j)
                    if nxt and j in (1, 2):
                        transpose_pair(qb + 1, j - 1)
                    transpose_probs(n0, j + 1)
                    if j < TB - 1:
                        pe.wait_ge(q_done, 2 * qb + (1 if j == 0 else 2))
                        scores(n1, j + 1, qb * QB, (j + 2) * P)
                    elif nxt:
                        pe.wait_ge(q_done, 2 * (qb + 1) + 1)
                        scores(n1, 0, (qb + 1) * QB, P)
                    pe.wait_ge(v_done, 2 * (qb + 1))
                    if not (isinstance(t, int) and t < 2):
                        pe.wait_ge(x1_done, t - 1)
                    weigh_values(n0, j, j + 1, qb * TB, True,
                                 (lambda: scores(n1 + 1, 0, qb * QB, QB)) if nxt and j == TB - 1 else None)

                    def chunk(kc):
                        transpose_probs(n0 + 1 + kc, TB)
                        if j < TB - 1:
                            scores(n1 + 1 + kc, j + 1, kc * QB, QB)
                        elif nxt:
                            scores(n1 + 2 + kc, 0, kc * QB, QB)
                        weigh_values(n0 + 1 + kc, j, TB, kc * TB, False)

                    if nxt or j < TB - 1:
                        over_chunks(pe, qb, chunk)
                    else:
                        for step, (kc0, kc1) in enumerate(LAST_PARTS):
                            with pe.Fori(kc0, kc1) as kc:
                                chunk(kc)
                            if step < 2:
                                routing(NB, step, NT - 2)
                    if nxt and j == 2:
                        queries(qb + 1, 0)
                    if nxt and j == 3:
                        queries(qb + 1, 1)

            over_blocks(pe, body)

            pe.wait_ge(top_ready, NT - 1)
            pe.wait_ge(slots_ready, NT - 2)
            rank(NT - 2)
            pe.wait_ge(slots_ready, NT - 1)
            transpose_x2(NT - 1, TB - 1)
            logits(NT - 1)
            pe.wait_ge(top_ready, NT)
            rank(NT - 1)

            nc.tensor.matmul(ps_s[:, 0:E], ones[:], mask[:], start=True, stop=False)
            nc.tensor.matmul(ps_s[:, 0:E], ones[:], cum[:], start=False, stop=True).then_inc(counts_ps, 1)

            pe.wait_ge(tab_ready, 2)

            def transpose_rows(t, u, early):
                pe.wait_ge(xf_loaded[u], 16 * (t // FU + 1) if isinstance(t, int) else 16 * early)
                if not (isinstance(t, int) and t < 2):
                    pe.wait_ge(fx_done, t - 1)
                for c in range(DC):
                    ins = nc.tensor.transpose(ps[:, 2 + u % 2, c * P:(c + 1) * P], xf[:, u, c * P:(c + 1) * P], ident[:])
                ins.then_inc(fx_ps, 1)

            def up(t, u, e):
                pe.wait_ge(fx_done, t + 1)
                if not (isinstance(t, int) and t < 2):
                    pe.wait_ge(h_done, t - 1)
                w = lambda m, c: m[:, bass.ds(e, 1), c, :].rearrange("p a n -> p (a n)")
                three(ps[:, u % 2, :], [((fx_hi[:, u % 2, c], fx_lo[:, u % 2, c]), (w(w1_hi, c), w(w1_lo, c)))
                                        for c in range(DC)]).then_inc(h_ps, 1)

            def down(t, u, e):
                pe.wait_ge(ht_done, t + 1)
                if not (isinstance(t, int) and t < 2):
                    pe.wait_ge(y_biased, t - 1)
                w = lambda m, c: m[:, bass.ds(e, 1), c, :].rearrange("p a n -> p (a n)")
                three(ps[:, 6 + u % 2, 0:D], [((ht_hi[:, u % 2, c], ht_lo[:, u % 2, c]), (w(w2_hi, c), w(w2_lo, c)))
                                              for c in range(HC)]).then_inc(y_ps, 1)

            def transpose_h(t, u):
                pe.wait_ge(h_done, t + 1)
                if not (isinstance(t, int) and t < 2):
                    pe.wait_ge(ht_done, t - 1)
                for c in range(HC):
                    ins = nc.tensor.transpose(ps[:, 4 + u % 2, c * P:(c + 1) * P], h_sb[:, u % 2, c * P:(c + 1) * P], ident[:])
                ins.then_inc(ht_ps, 1)

            transpose_rows(0, 0, 1)
            pe.wait_ge(w1_done, E)

            def turn(t, u, r):
                up(t, u, expert(words, u))
                if not (isinstance(t, int) and t == FT - 1):
                    transpose_rows(t + 1, (u + 1) % FU, r + 1 if u < FU - 1 else r + 2)
                if not (isinstance(t, int) and t < 2):
                    if isinstance(t, int) and t == 2:
                        pe.wait_ge(w2_done, E)
                    down(t - 2, (u - 2) % FU, expert(words, u - 2))
                transpose_h(t, u)

            regs = word_registers(pe)
            load_word(pe, regs, 0)
            pe.reg_mov(regs[0], regs[1])
            words = next_words(pe, regs)
            load_word(pe, regs, 1)
            for u in range(FU):
                turn(u, u, 0)
            with pe.Fori(1, FT // FU - 1) as r:
                words = next_words(pe, regs)
                for u in range(FU):
                    turn(r * FU + u, u, r)
                    if u == FU // 2:
                        load_word(pe, regs, r + 1)
            words = next_words(pe, regs)
            for u in range(FU):
                turn(FT - FU + u, u, FT // FU - 1)
            for u in (FU - 2, FU - 1):
                down(FT - FU + u, u, expert(words, u))

        @block.scalar
        def _(act):
            copy = nc.scalar.copy
            for k in range(2):
                act.dma_start(x_in[:, k], x_tiles[:, 2 * k:2 * k + 2, :]).then_inc(x_loaded[k], 16)
            act.wait_ge(wstage_ps, 1)
            copy(wa_hi[:].rearrange("p c n -> p (c n)"), ps_a).then_inc(wstage_hi, 1)
            act.wait_ge(wstage_ps, 2)
            copy(wot.rearrange("p c n -> p (c n)"), ps_wot).then_inc(wstage_sb, 1)

            def xs_high(nb, k):
                p = 2 * nb + k
                act.wait_ge(xt_ps, p + 1)
                if k == 1:
                    act.wait_ge(v_ps, p)
                    act.wait_ge(xt_stored[0], 32 * (nb + 1))
                elif not (isinstance(nb, int) and nb == 0):
                    act.wait_ge(v_ps, p)
                    act.wait_ge(xt_stored[1], 32 * nb)
                copy(xs_hi[:].rearrange("p c n -> p (c n)"), ps_x[:]).then_inc(xs_hi_done, 1)

            def v_high(nb, k):
                p = 2 * nb + k
                act.wait_ge(v_ps, p + 1)
                copy(v_hi[:, bass.ds(2 * p, 2), :], to3(ps_v, D)).then_inc(v_hi_done, 1)

            def q_high(nb, k):
                act.wait_ge(q_ps, 2 * nb + k + 1)
                copy(q_hi[:, :, k * 2 * P:(k + 1) * 2 * P], to3(ps_x, 2 * P)).then_inc(q_hi_done, 1)

            def exps(n, j, src, width, col):
                if not (isinstance(n, int) and n == 0):
                    act.wait_ge(pt_ps, 2 * n)
                apart(act)
                nc.scalar.activation(probs[:, 0:width], src, ACT.Exp, bias=neg_max[:, j % 2:j % 2 + 1],
                                     scale=SCALE, accum_out=sums[:, j % 2, col]).then_inc(probs_ready, 1)

            def pt_high(n, blocks):
                if not (isinstance(n, int) and n == 0):
                    act.wait_ge(pv_done, n)
                act.wait_ge(pt_ps, 2 * n + (1 if blocks > 2 else 2))
                w = min(blocks, 2)
                copy(pt_hi[:, 0:w], to3(ps_pt[:, 0, 0:w * P], P)).then_inc(pt_hi_done, 1 if blocks > 2 else 2)
                if blocks > 2:
                    act.wait_ge(pt_ps, 2 * n + 2)
                    w = blocks - 2
                    copy(pt_hi[:, 2:2 + w], to3(ps_pt[:, 1, 0:w * P], P)).then_inc(pt_hi_done, 1)

            def routing(qb, j):
                t2, _ = routed(qb, j, 2)
                if t2 is not None and (not isinstance(t2, int) or t2 < NT):
                    act.wait_ge(x2t_ps, t2 + 1)
                    if not (isinstance(t2, int) and t2 == 0):
                        act.wait_ge(logits_ps, t2)
                    copy(x2t[:].rearrange("p c n -> p (c n)"), ps_r[:, 0:D]).then_inc(x2t_sb, 1)

            def gate_exp(qb, j):
                t3, j3 = routed(qb, j, 3)
                if t3 is not None and (not isinstance(t3, int) or t3 < NT):
                    act.wait_ge(top_ready, t3 + 1)
                    k = j3 % 2
                    if not (isinstance(t3, int) and t3 < 2):
                        act.wait_ge(row_ready, t3 - 1)
                    nc.scalar.activation(ex[:, k:k + 1], top[:, k, 0:1], ACT.Exp, bias=top[:, k, 1:2],
                                         scale=-1.0).then_inc(ex_ready, 1)

            xs_high(0, 0)
            act.wait_ge(wstage_ps, 3)
            copy(wb_hi[:].rearrange("p c n -> p (c n)"), ps_b).then_inc(wstage_hi, 1)
            v_high(0, 0)
            xs_high(0, 1)
            v_high(0, 1)
            q_high(0, 0)
            q_high(0, 1)
            act.wait_ge(consts_ready, 1)

            def diagonal_exps(qb, j):
                act.wait_ge(max_ready, tile(qb, j) + 1)
                if not (isinstance(qb, int) and qb == 0 and j < 2):
                    act.wait_ge(x1_done, tile(qb, j) - 1)
                exps(chunk0(qb, j), j, s_diag[:, j % 2, 0:(j + 1) * P], (j + 1) * P, slice(7, 8))

            diagonal_exps(0, 0)

            def weights_high(hi, raw_at, loaded, done, e):
                act.wait_ge(loaded[e], 16)
                copy(hi[:, e].rearrange("p c n -> p (c n)"), raw_at[:, e].bitcast(F32).rearrange("p c n -> p (c n)")
                     ).then_inc(done, 1)

            def body(qb):
                nxt = has_next(qb)
                for j in range(TB):
                    n0 = chunk0(qb, j)
                    pt_high(n0, j + 1)
                    routing(qb, j)
                    if nxt and j == 1:
                        xs_high(qb + 1, 0)
                    if nxt and j == 2:
                        v_high(qb + 1, 0)
                        xs_high(qb + 1, 1)
                    if nxt and j == 3:
                        v_high(qb + 1, 1)

                    def chunk(kc):
                        exps(n0 + 1 + kc, j, s_sb[:, j % 2, bass.ds(kc * QB, QB)], QB, bass.ds(kc, 1))
                        pt_high(n0 + 1 + kc, TB)

                    if nxt or j < TB - 1:
                        over_chunks(act, qb, chunk)
                    else:
                        for kc in range(NB - 1):
                            exps(n0 + 1 + kc, j, s_sb[:, j % 2, kc * QB:(kc + 1) * QB], QB, slice(kc, kc + 1))
                            weights_high(w1_hi, w1_lo, w1_loaded, w1_hi_done, kc)
                            if kc == LAST_PARTS[1][0]:
                                routing(NB, 0)
                            pt_high(n0 + 1 + kc, TB)
                            if kc == LAST_PARTS[0][1] - 2:
                                gate_exp(qb, j)
                            if kc == LAST_PARTS[1][1] - 1:
                                gate_exp(NB, 0)
                    if j < TB - 1:
                        diagonal_exps(qb, j + 1)
                    elif nxt:
                        diagonal_exps(qb + 1, 0)
                    if nxt and j == 2:
                        q_high(qb + 1, 0)
                    if nxt and j == 3:
                        q_high(qb + 1, 1)
                    if nxt or j < TB - 1:
                        gate_exp(qb, j)

            over_blocks(act, body)

            gate_exp(NB, 1)
            weights_high(w1_hi, w1_lo, w1_loaded, w1_hi_done, E - 1)
            routing(NB, 1)
            for e in W2_ORDER[:2]:
                weights_high(w2_hi, w2_lo, w2_loaded, w2_hi_done, e)
            gate_exp(NB, 2)
            for e in W2_ORDER[2:]:
                weights_high(w2_hi, w2_lo, w2_loaded, w2_hi_done, e)
            act.wait_ge(pads_ready, 1)
            for e in range(E // 2, E):
                pad(act, e)

            def fx_high(t, u):
                act.wait_ge(fx_ps, t + 1)
                if not (isinstance(t, int) and t < 2):
                    act.wait_ge(h_ps, t - 1)
                copy(fx_hi[:, u % 2].rearrange("p c n -> p (c n)"), ps[:, 2 + u % 2, 0:D]).then_inc(fx_hi_done, 1)

            def ht_high(t, u):
                act.wait_ge(ht_ps, t + 1)
                if not (isinstance(t, int) and t < 2):
                    act.wait_ge(y_ps, t - 1)
                nc.scalar.activation(ht_hi[:, u % 2].rearrange("p c n -> p (c n)"), ps[:, 4 + u % 2, :], ACT.Relu
                                     ).then_inc(ht_hi_done, 1)

            def y_gated(t, u, half):
                act.wait_ge(y_biased, t + 1)
                act.wait_ge(gate_ready, t + 1)
                if not (isinstance(t, int) and t < 2):
                    act.wait_ge(added[u % 2], 16 * (half + 1))
                nc.scalar.activation(y_sb[:, u % 2], y_b[:, u % 2], ACT.Copy, scale=gate[:, u:u + 1]).then_inc(y_done, 1)

            fx_high(0, 0)

            def turn(t, u, r):
                if not (isinstance(t, int) and t == FT - 1):
                    fx_high(t + 1, (u + 1) % FU)
                ht_high(t, u)
                if not (isinstance(t, int) and t < 2):
                    y_gated(t - 2, (u - 2) % FU, r * (FU // 2) + u // 2 - 1)

            for u in range(FU):
                turn(u, u, 0)
            with act.Fori(1, FT // FU - 1) as r:
                for u in range(FU):
                    turn(r * FU + u, u, r)
            for u in range(FU):
                turn(FT - FU + u, u, FT // FU - 1)
            for t in (FT - 2, FT - 1):
                y_gated(t, t % FU, t // 2)

        @block.vector
        def _(dve):
            V = nc.vector

            def low(dst, src, high):
                return V.tensor_tensor(dst, src, high.bitcast(F32), ALU.subtract)


            def x_statistics(nb, k):
                p = 2 * nb + k
                dve.wait_ge(x_loaded[k], 16 * (nb + 1))
                for a in range(2):
                    V.bn_stats(stat[:, a], x_in[:, k, a]).then_inc(x_stats1, 1)
                dve.wait_ge(x_stats1, 2 * p + 2)
                if not (isinstance(nb, int) and nb == 0 and k == 0):
                    dve.wait_ge(x_rstd, p)
                apart(dve)
                for a in range(2):
                    ins = V.bn_aggr(mv[:, a], stat[:, a])
                ins.then_inc(x_stats, 1)

            def x_normalise(nb, k):
                p = 2 * nb + k
                dve.wait_ge(x_rstd, p + 1)
                if not (isinstance(nb, int) and nb == 0 and k == 0):
                    dve.wait_ge(xt_ps, p)
                for a in range(2):
                    ins = V.tensor_scalar(xn[:, a], x_in[:, k, a], mv[:, a, 0:1], rstd[:, a, 1:2],
                                          ALU.subtract, ALU.mult)
                ins.then_inc(x_normed, 1)

            def xs_low(nb, k):
                p = 2 * nb + k
                dve.wait_ge(xs_hi_done, p + 1)
                low(xs_lo[:].rearrange("p c n -> p (c n)"), ps_x[:], xs_hi[:].rearrange("p c n -> p (c n)")
                    ).then_inc(xs_done, 1)

            def v_low(nb, k):
                p = 2 * nb + k
                dve.wait_ge(v_hi_done, p + 1)
                pair = bass.ds(2 * p, 2)
                low(v_lo[:, pair, :], to3(ps_v, D), v_hi[:, pair, :]).then_inc(v_done, 1)

            def q_low(nb, k):
                dve.wait_ge(q_hi_done, 2 * nb + k + 1)
                half = slice(k * 2 * P, (k + 1) * 2 * P)
                low(q_lo[:, :, half], to3(ps_x, 2 * P), q_hi[:, :, half]).then_inc(q_done, 1)

            def save_diagonal(n, qb, j):
                dve.wait_ge(scores_ps, n + 1)
                if not (isinstance(n, int) and n <= 1):
                    dve.wait_ge(probs_ready, chunk0(qb, j - 1) if j else chunk0(qb - 1, TB - 1))
                m = run_max[:, j % 2:j % 2 + 1]
                if j:
                    V.tensor_scalar(s_diag[:, j % 2, 0:j * P], ps_s[:, 0:j * P], 1.0, LOW, ALU.mult,
                                    ALU.max, accum_out=m).then_inc(diag_part, 1)
                    dve.wait_ge(diag_part, qb * (TB - 1) + j)
                apart(dve)
                V.tensor_tensor_reduce(s_diag[:, j % 2, j * P:(j + 1) * P], ps_s[:, j * P:(j + 1) * P], causal[:],
                                       1.0, m if j else LOW, ALU.add, ALU.max, m).then_inc(scores_saved, 1)

            def save_scores(n, j, key0):
                dve.wait_ge(scores_ps, n + 1)
                dve.wait_ge(scores_saved, n)
                m = run_max[:, j % 2:j % 2 + 1]
                V.tensor_scalar(s_sb[:, j % 2, bass.ds(key0, QB)], ps_s[:], 1.0, m, ALU.mult, ALU.max,
                                accum_out=m).then_inc(scores_saved, 1)

            def negate_max(t, j, n):
                dve.wait_ge(scores_saved, n)
                V.tensor_scalar(neg_max[:, j % 2:j % 2 + 1], run_max[:, j % 2:j % 2 + 1], -SCALE, None, ALU.mult
                                ).then_inc(max_ready, 1)

            def pt_low(n, blocks):
                dve.wait_ge(pt_hi_done, 2 * n + (1 if blocks > 2 else 2))
                w = min(blocks, 2)
                low(pt_lo[:, 0:w], to3(ps_pt[:, 0, 0:w * P], P), pt_hi[:, 0:w]).then_inc(pt_done, 1 if blocks > 2 else 2)
                if blocks > 2:
                    dve.wait_ge(pt_hi_done, 2 * n + 2)
                    w = blocks - 2
                    low(pt_lo[:, 2:2 + w], to3(ps_pt[:, 1, 0:w * P], P), pt_hi[:, 2:2 + w]).then_inc(pt_done, 1)

            def add_sums(t, j, n_end):
                dve.wait_ge(probs_ready, n_end)
                V.tensor_reduce(lsum[:, 0:1], sums[:, j % 2, :], AX.X, ALU.add).then_inc(x1_chain, 1)

            def invert_sum(t):
                dve.wait_ge(x1_chain, 4 * t + 1)
                V.reciprocal(lsum[:, 1:2], lsum[:, 0:1]).then_inc(x1_chain, 1)

            def attention_out(t, j, n_end, half):
                k = j % 2
                dve.wait_ge(x1_chain, 4 * t + 2)
                dve.wait_ge(res_loaded[k], 16 * half)
                if not (isinstance(t, int) and t < 2):
                    dve.wait_ge(x1_stored[k], 16 * (half - 1))
                dve.wait_ge(pv_done, n_end)
                V.scalar_tensor_tensor(x1[:, k], ps_o[:, k], lsum[:, 1:2], x_res[:, k], ALU.mult, ALU.add
                                       ).then_inc(x1_done, 1)
                dve.wait_ge(x1_done, t + 1)
                V.bn_stats(stat2[:], x1[:, k]).then_inc(x1_chain, 1)
                dve.wait_ge(x1_chain, 4 * t + 3)
                apart(dve)
                V.bn_aggr(mv2[:, k], stat2[:]).then_inc(x1_chain, 1)
                dve.wait_ge(x1_chain, 4 * t + 4)
                V.tensor_scalar(rstd2[:, k, 0:1], mv2[:, k, 1:2], EPS, None, ALU.add).then_inc(x1_stats, 1)

            def x2_normalise(t, j, turn4):
                k = j % 2
                dve.wait_ge(rstd2_ready, t + 1)
                if not (isinstance(t, int) and t < 4):
                    dve.wait_ge(scattered[j], 32 * turn4)
                V.tensor_scalar(rows[:, j, 0:D], x1[:, k], mv2[:, k, 0:1], rstd2[:, k, 1:2], ALU.subtract, ALU.mult
                                ).then_inc(x2_ready, 1)

            def choose(t, j):
                k = j % 2
                dve.wait_ge(logits_ps, t + 1)
                if not (isinstance(t, int) and t < 2):
                    dve.wait_ge(hot_ready, t - 1)
                apart(dve)
                V.max(top[:, k], ps_r[:, D:D + E]).then_inc(top_chain, 1)
                dve.wait_ge(top_chain, t + 1)
                apart(dve)
                V.max_index(top_i[:, k], top[:, k], ps_r[:, D:D + E]).then_inc(top_ready, 1)

            def slots(t, j):
                k = j % 2
                dve.wait_ge(rank_ps, t + 1)
                dve.wait_ge(ex_ready, t + 1)
                if not (isinstance(t, int) and t < 2):
                    dve.wait_ge(row_ready, t - 1)
                for c in range(2):
                    V.tensor_tensor_reduce(junk[:, c], ps_r[:, D + 16:D + 16 + E], hot[:, k, c], 1.0, 0.0, ALU.mult,
                                           ALU.add, slot_f[:, k, c:c + 1])
                V.tensor_scalar(den[:, 0:1], ex[:, k:k + 1], 1.0, None, ALU.add).then_inc(slot_chain, 1)
                dve.wait_ge(slot_chain, t + 1)
                V.reciprocal(den[:, 1 + k:2 + k], den[:, 0:1]).then_inc(slots_ready, 1)

            def routing(qb, j):
                t2, _ = routed(qb, j, 2)
                t3, j3 = routed(qb, j, 3)
                t4, j4 = routed(qb, j, 4)
                live = lambda t: t is not None and (not isinstance(t, int) or t < NT)
                if live(t2) and (not isinstance(qb, int) or tile(qb, j) <= NT):
                    dve.wait_ge(x2t_sb, t2 + 1)
                if live(t3):
                    choose(t3, j3)
                if t4 is not None:
                    slots(t4, j4)

            def t1_half(qb, j):
                return 2 * qb + (j - 1) // 2 + 1

            x_statistics(0, 0)
            x_normalise(0, 0)
            x_statistics(0, 1)
            dve.wait_ge(wstage_hi, 1)
            low(wa_lo[:].rearrange("p c n -> p (c n)"), ps_a, wa_hi[:].rearrange("p c n -> p (c n)")
                ).then_inc(wstage_sb, 1)
            xs_low(0, 0)
            x_normalise(0, 1)
            dve.wait_ge(wstage_hi, 2)
            low(wb_lo[:].rearrange("p c n -> p (c n)"), ps_b, wb_hi[:].rearrange("p c n -> p (c n)")
                ).then_inc(wstage_sb, 1)
            v_low(0, 0)
            xs_low(0, 1)
            x_statistics(1, 0)
            x_normalise(1, 0)
            v_low(0, 1)
            q_low(0, 0)
            q_low(0, 1)
            dve.wait_ge(consts_ready, 1)
            save_diagonal(0, 0, 0)
            negate_max(0, 0, 1)

            def weights_low(lo, hi, hi_done, done, i, e):
                dve.wait_ge(hi_done, i + 1)
                flat = lambda m: m[:, e].rearrange("p c n -> p (c n)")
                V.tensor_tensor(flat(lo), flat(lo).bitcast(F32), flat(hi).bitcast(F32), ALU.subtract).then_inc(done, 1)

            def body(qb):
                nxt = has_next(qb)
                for j in range(TB):
                    t, n0, n1 = tile(qb, j), chunk0(qb, j), chunk0(qb, j) + qb + 1
                    t1, j1 = routed(qb, j, 1)
                    pt_low(n0, j + 1)
                    if j < TB - 1:
                        save_diagonal(n1, qb, j + 1)
                    elif nxt:
                        save_diagonal(n1, qb + 1, 0)
                        save_scores(n1 + 1, 0, qb * QB)
                    if nxt and j == 0 and not (isinstance(qb, int) and qb == 0):
                        x_statistics(qb + 1, 0)
                    if nxt and j == 1:
                        xs_low(qb + 1, 0)
                    if nxt and j == 2:
                        v_low(qb + 1, 0)
                        xs_low(qb + 1, 1)
                    if nxt and j == 3:
                        v_low(qb + 1, 1)

                    def chunk(kc):
                        pt_low(n0 + 1 + kc, TB)
                        if j < TB - 1:
                            save_scores(n1 + 1 + kc, j + 1, kc * QB)
                        elif nxt:
                            save_scores(n1 + 2 + kc, 0, kc * QB)

                    if not (isinstance(qb, int) and qb == 0):
                        chunk(0)
                    if t1 is not None:
                        add_sums(t1, j1, n0)
                    routing(qb, j)
                    if t1 is not None:
                        invert_sum(t1)
                    short = isinstance(qb, int) and qb == 0
                    if nxt and j == 1 and short:
                        x_normalise(qb + 1, 1)
                    if not (isinstance(qb, int) and qb < 2):
                        chunk(1)
                    if t1 is not None:
                        attention_out(t1, j1, n0, t1_half(qb, j))
                    if not nxt and j == TB - 1:
                        for kc in range(2, NB - 1):
                            chunk(kc)
                            if kc == 2:
                                x2_normalise(t1, j1, qb)
                            if kc == LAST_PARTS[1][0]:
                                routing(NB, 0)
                            if kc == LAST_PARTS[2][0]:
                                routing(NB, 1)
                            else:
                                weights_low(w1_lo, w1_hi, w1_hi_done, w1_done, kc - 2, kc - 2)
                    elif not (isinstance(qb, int) and qb <= 2):
                        with dve.Fori(2, qb) as kc:
                            chunk(kc)
                    if j < TB - 1:
                        negate_max(t + 1, j + 1, n1 + qb + 1)
                    elif nxt:
                        negate_max(t + 1, 0, n1 + qb + 2)
                    if t1 is not None and (nxt or j < TB - 1):
                        x2_normalise(t1, j1, qb if j >= 1 else qb - 1)
                    if nxt and j == 1 and not short:
                        x_normalise(qb + 1, 1)
                    if nxt and j == 0:
                        if not (isinstance(qb, int) and qb == 0):
                            x_normalise(qb + 1, 0)
                        x_statistics(qb + 1, 1)
                    if nxt and j == 2:
                        q_low(qb + 1, 0)
                    if nxt and j == 3:
                        q_low(qb + 1, 1)

            body(0)
            body(1)
            body(2)
            with dve.Fori(3, NB - 1) as qb:
                body(qb)
            body(NB - 1)
            add_sums(NT - 1, TB - 1, chunk0(NB, 0))
            invert_sum(NT - 1)
            attention_out(NT - 1, TB - 1, chunk0(NB, 0), NT // 2)
            slots(NT - 2, TB - 2)
            x2_normalise(NT - 1, TB - 1, NB - 1)
            for e in (E - 4, E - 3):
                weights_low(w1_lo, w1_hi, w1_hi_done, w1_done, e, e)
            dve.wait_ge(x2t_sb, NT)
            choose(NT - 1, TB - 1)
            for e in (E - 2, E - 1):
                weights_low(w1_lo, w1_hi, w1_hi_done, w1_done, e, e)
            weights_low(w2_lo, w2_hi, w2_hi_done, w2_done, 0, W2_ORDER[0])
            slots(NT - 1, TB - 1)

            link_n = [0]

            def link(ins):
                link_n[0] += 1
                ins.then_inc(tab_chain, 1)
                dve.wait_ge(tab_chain, link_n[0])

            dve.wait_ge(counts_ps, 1)
            V.tensor_copy(pad_slot[:], ps_s[:, 0:E]).then_inc(pads_ready, 1)
            link(V.scalar_tensor_tensor(cnt[:, 0], iota_e[:], -float(REGION), ps_s[:, 0:E], ALU.mult, ALU.add))
            link(V.tensor_scalar(cnt[:, 1], cnt[:, 0], 1.0 / P, (P - 1.0) / P - 127.5 / 256, ALU.mult, ALU.add))
            link(V.tensor_copy(cnt_i[:], cnt[:, 1]))
            link(V.tensor_copy(cnt[:, 2], cnt_i[:]))
            link(V.tensor_tensor_scan(cnt[:, 3], ones[:, 0:E], cnt[:, 2], 0.0, ALU.mult, ALU.add))
            over_t = lambda ap: ap[:, None, :].to_broadcast([P, FT, E])
            link(V.tensor_tensor(past[:], iota_t[:, :, None].to_broadcast([P, FT, E]), over_t(cnt[:, 3]), ALU.is_ge))
            V.tensor_reduce(tmpf[:, 0, :], past[:], AX.X, ALU.add)
            link(V.tensor_scalar(cnt[:, 1], cnt[:, 2], -float(P), float(REGION), ALU.mult, ALU.add))
            V.tensor_tensor(past_tiles[:], past[:], over_t(cnt[:, 2]), ALU.mult)
            link(V.tensor_tensor(past[:], past[:], over_t(cnt[:, 1]), ALU.mult))
            link(V.tensor_reduce(tmpf[:, 1, :], past[:], AX.X, ALU.add))
            link(V.scalar_tensor_tensor(tmpf[:, 1, :], iota_t[:], float(P), tmpf[:, 1, :], ALU.mult, ALU.add))
            V.tensor_scalar(tile_e[:], tmpf[:, 0, :], E - 1.0, None, ALU.min)
            link(V.tensor_scalar(tmpf[:, 1, :], tmpf[:, 1, :], float(ZERO_TILE), None, ALU.min))
            V.tensor_copy(tab_rows[:], tmpf[:, 1, :]).then_inc(tab_ready, 1)
            link(V.tensor_tensor(digit[:], digit[:], tile_e[:].rearrange("p (r u) -> p r u", u=FU), ALU.mult))
            link(V.tensor_reduce(cnt_w[:], digit[:], AX.X, ALU.add))
            V.tensor_copy(tab_words[:], cnt_w[:]).then_inc(tab_ready, 1)

            def add_b1(t, u, e):
                dve.wait_ge(h_ps, t + 1)
                if not (isinstance(t, int) and t < 2):
                    dve.wait_ge(ht_ps, t - 1)
                V.tensor_tensor(h_sb[:, u % 2], ps[:, u % 2, :],
                                b1_sb[:, bass.ds(e, 1), :].rearrange("p a n -> p (a n)"), ALU.add).then_inc(h_done, 1)

            def fx_low(t, u):
                dve.wait_ge(fx_hi_done, t + 1)
                low(fx_lo[:, u % 2].rearrange("p c n -> p (c n)"), ps[:, 2 + u % 2, 0:D],
                    fx_hi[:, u % 2].rearrange("p c n -> p (c n)")).then_inc(fx_done, 1)

            def ht_low(t, u):
                dve.wait_ge(ht_hi_done, t + 1)
                V.scalar_tensor_tensor(ht_lo[:, u % 2].rearrange("p c n -> p (c n)"), ps[:, 4 + u % 2, :], 0.0,
                                       ht_hi[:, u % 2].rearrange("p c n -> p (c n)").bitcast(F32), ALU.max,
                                       ALU.subtract).then_inc(ht_done, 1)

            def add_b2(t, u, e):
                dve.wait_ge(y_ps, t + 1)
                if not (isinstance(t, int) and t < 2):
                    dve.wait_ge(y_done, t - 1)
                V.tensor_tensor(y_b[:, u % 2], ps[:, 6 + u % 2, 0:D],
                                b2_sb[:, bass.ds(e, 1), :].rearrange("p a n -> p (a n)"), ALU.add).then_inc(y_biased, 1)

            def w2_low(i):
                weights_low(w2_lo, w2_hi, w2_hi_done, w2_done, i, W2_ORDER[i])

            for i in (1, 2, 3):
                w2_low(i)
            fx_low(0, 0)
            V.tensor_reduce(tmpf[:, 1, :], past_tiles[:], AX.X, ALU.add)
            link(V.tensor_scalar(tmpf[:, 0, :], tmpf[:, 0, :], float(E), float(FT), ALU.is_ge, ALU.mult))
            link(V.tensor_tensor(tmpf[:, 1, :], tmpf[:, 0, :], tmpf[:, 1, :], ALU.add))
            link(V.tensor_tensor(tmpf[:, 1, :], tmpf[:, 1, :], iota_t[:], ALU.min))
            V.tensor_copy(fence[:], tmpf[:, 1, :]).then_inc(tab_ready, 1)
            for i in (4, 5):
                w2_low(i)
            dve.wait_ge(fb_loaded, 48)

            def turn(t, u):
                add_b1(t, u, expert(words, u))
                if not (isinstance(t, int) and t == FT - 1):
                    fx_low(t + 1, (u + 1) % FU)
                if isinstance(t, int) and t < 2:
                    w2_low(E - 2 + t)
                if not (isinstance(t, int) and t < 2):
                    add_b2(t - 2, (u - 2) % FU, expert(words, u - 2))
                ht_low(t, u)

            regs = word_registers(dve)
            load_word(dve, regs, 0)
            dve.reg_mov(regs[0], regs[1])
            words = next_words(dve, regs)
            load_word(dve, regs, 1)
            for u in range(FU):
                turn(u, u)
            with dve.Fori(1, FT // FU - 1) as r:
                words = next_words(dve, regs)
                for u in range(FU):
                    turn(r * FU + u, u)
                    if u == FU // 2:
                        load_word(dve, regs, r + 1)
            words = next_words(dve, regs)
            for u in range(FU):
                turn(FT - FU + u, u)
            for u in (FU - 2, FU - 1):
                add_b2(FT - FU + u, u, expert(words, u))

        @block.gpsimd
        def _(pool):
            G = nc.gpsimd
            n = [0]

            def link(ins):
                n[0] += 1
                ins.then_inc(pool_chain, 1)
                pool.wait_ge(pool_chain, n[0])

            G.memset(ident[:], 0.0).then_inc(pool_chain, 1)
            G.memset(upper[:], 0.0).then_inc(pool_chain, 1)
            G.memset(causal[:], LOW).then_inc(pool_chain, 1)
            G.memset(half_neg[:], -0.5).then_inc(pool_chain, 1)
            G.memset(sums[:], 0.0).then_inc(pool_chain, 1)
            G.memset(pad_row[:], 0.0).then_inc(pool_chain, 1)
            G.memset(cum[:], 0.0).then_inc(pool_chain, 1)
            G.memset(ones[:], 1.0).then_inc(pool_chain, 1)
            n[0] = 8
            pool.wait_ge(pool_chain, 8)
            link(G.affine_select(out=ident[:], in_=ident[:], compare_op=ALU.not_equal, fill=1.0, base=0,
                                 pattern=[[-1, P]], channel_multiplier=1))
            link(G.affine_select(out=upper[:], in_=upper[:], compare_op=ALU.is_ge, fill=1.0, base=0,
                                 pattern=[[-1, P]], channel_multiplier=1))
            link(G.affine_select(out=causal[:], in_=causal[:], compare_op=ALU.is_gt, fill=0.0, base=0,
                                 pattern=[[1, P]], channel_multiplier=-1))
            link(G.iota(iota_e[:], pattern=[[1, E]], base=0, channel_multiplier=0, allow_small_or_imprecise_dtypes=True))
            link(G.iota(iota_t[:], pattern=[[1, FT]], base=0, channel_multiplier=0, allow_small_or_imprecise_dtypes=True))
            link(G.iota(lane[:], pattern=[[1, 1]], base=0, channel_multiplier=1, allow_small_or_imprecise_dtypes=True))
            link(G.iota(tok_ids[:], pattern=[[P, NT]], base=0, channel_multiplier=1))
            link(G.iota(pad_row[:, C_TOK:C_TOK + 1].bitcast(I32), pattern=[[1, 1]], base=S, channel_multiplier=1))
            link(G.tensor_scalar(cum[0:1, :], iota_e[0:1, :], float(REGION), None, ALU.mult))
            for u in range(FU):
                G.memset(digit[:, :, u:u + 1], float(E ** u))
            G.tensor_copy(slot_f[:, 0], half_neg[:]).then_inc(consts_ready, 1)
            for k in range(2):
                half = slice(k * P // 2, (k + 1) * P // 2)
                pool.dma_start(xg[ZERO_TILE + k * P // 2:ZERO_TILE + (k + 1) * P // 2, :], pad_row[half]
                               ).then_inc(added[k], 16)

            def x_rsqrt(nb, k):
                p = 2 * nb + k
                pool.wait_ge(x_stats, p + 1)
                if not (isinstance(nb, int) and nb == 0 and k == 0):
                    pool.wait_ge(x_normed, p)
                apart(pool)
                G.tensor_scalar(rstd[:, :, 0:1], mv[:, :, 1:2], EPS, None, ALU.add).then_inc(x_eps, 1)
                pool.wait_ge(x_eps, p + 1)
                G.tensor_tensor(rstd[:, :, 1:2], rstd[:, :, 0:1], half_neg[:].rearrange("p (a b) -> p a b", b=1), ALU.pow
                                ).then_inc(x_rstd, 1)

            x_rsqrt(0, 0)
            x_rsqrt(0, 1)
            x_rsqrt(1, 0)

            def x1_rsqrt(t, j):
                k = j % 2
                pool.wait_ge(x1_stats, t + 1)
                if not (isinstance(t, int) and t < 2):
                    pool.wait_ge(x2_ready, t - 1)
                G.tensor_tensor(rstd2[:, k, 1:2], rstd2[:, k, 0:1], half_neg[:, 0:1], ALU.pow).then_inc(rstd2_ready, 1)

            def one_hots(t, j):
                k = j % 2
                pool.wait_ge(top_ready, t + 1)
                if not (isinstance(t, int) and t == 0):
                    add_choices(t - 1)
                if not (isinstance(t, int) and t < 2):
                    pool.wait_ge(slots_ready, t - 1)
                apart(pool)
                G.tensor_copy(top_f[:, k], top_i[:, k, 0:2]).then_inc(hot_chain, 1)
                pool.wait_ge(hot_chain, 3 * t + 1)
                apart(pool)
                G.tensor_copy(rows[:, j, C_E1:C_E1 + 1], top_f[:, k, 0:1])
                for c in range(2):
                    G.tensor_scalar(hot[:, k, c], iota_e[:], top_f[:, k, c:c + 1], None, ALU.is_equal
                                    ).then_inc(hot_chain, 1)
                pool.wait_ge(hot_chain, 3 * t + 3)
                G.tensor_tensor(mask[:], hot[:, k, 0], hot[:, k, 1], ALU.add).then_inc(hot_ready, 1)

            def add_choices(t):
                pool.wait_ge(rank_ps, t + 1)
                pool.wait_ge(hot_ready, t + 1)
                G.tensor_tensor(cum[:], cum[:], mask[:], ALU.add).then_inc(cum_ready, 1)
                pool.wait_ge(cum_ready, t + 1)

            def prepare_row(t, j):
                k = j % 2
                pool.wait_ge(slots_ready, t + 1)
                apart(pool)
                G.tensor_tensor(rows[:, j, C_G2:C_G2 + 1], ex[:, k:k + 1], den[:, 1 + k:2 + k], ALU.mult
                                ).then_inc(row_chain, 1)
                G.tensor_copy(slot_i[:, j], slot_f[:, k])
                G.tensor_copy(rows[:, j, C_TOK:C_TOK + 1].bitcast(I32), tok_ids[:, bass.ds(t, 1)])
                pool.wait_ge(row_chain, t + 1)
                apart(pool)
                G.tensor_scalar(rows[:, j, C_GD:C_GD + 1], rows[:, j, C_G2:C_G2 + 1], -2.0, 1.0, ALU.mult, ALU.add
                                ).then_inc(row_ready, 1)

            def scatter(t, j):
                pool.wait_ge(row_ready, t + 1)
                apart(pool)
                for c in range(2):
                    G.indirect_dma_start(out=xg, out_offset=bass.IndirectOffsetOnAxis(ap=slot_i[:, j, c:c + 1].bitcast(U32), axis=0),
                                         in_=rows[:, j, :], in_offset=None).then_inc(scattered[j], 16)

            def body(qb):
                nxt = has_next(qb)
                for j in range(TB):
                    if nxt and j < 2 and not (isinstance(qb, int) and qb == 0 and j == 0):
                        x_rsqrt(qb + 1, j)
                    t1, j1 = routed(qb, j, 1)
                    t3, j3 = routed(qb, j, 3)
                    t4, j4 = routed(qb, j, 4)
                    if t3 is not None:
                        one_hots(t3, j3)
                    if t1 is not None:
                        x1_rsqrt(t1, j1)
                    if t4 is not None:
                        prepare_row(t4, j4)
                        scatter(t4, j4)

            over_blocks(pool, body)

            one_hots(NT - 3, 1)
            prepare_row(NT - 4, 0)
            scatter(NT - 4, 0)
            one_hots(NT - 2, 2)
            x1_rsqrt(NT - 1, 3)
            prepare_row(NT - 3, 1)
            scatter(NT - 3, 1)
            one_hots(NT - 1, 3)
            for t in (NT - 2, NT - 1):
                prepare_row(t, t % TB)
                scatter(t, t % TB)

            for k in range(2):
                pool.wait_ge(x1_stored[k], 16 * (NT // 2))
            pool.wait_ge(tab_ready, 3)

            def read_columns(t, u, r):
                pool.wait_ge(xf_loaded[u], 16 * (r + 1))
                if not (isinstance(t, int) and t < FU):
                    pool.wait_ge(y_done, t - FU + 1)
                apart(pool)
                G.tensor_copy(dest[:, u:u + 1], xf[:, u, C_TOK:C_TOK + 1].bitcast(I32))
                G.tensor_copy(e_now[:, u:u + 1], tile_e[:, bass.ds(t, 1)]).then_inc(meta_chain, 1)
                pool.wait_ge(meta_chain, 3 * t + 1)
                apart(pool)
                G.tensor_scalar(gsel[:, u:u + 1], xf[:, u, C_E1:C_E1 + 1], e_now[:, u:u + 1], None, ALU.is_equal
                                ).then_inc(meta_chain, 1)
                pool.wait_ge(meta_chain, 3 * t + 2)
                G.tensor_tensor(gsel[:, u:u + 1], gsel[:, u:u + 1], xf[:, u, C_GD:C_GD + 1], ALU.mult).then_inc(meta_chain, 1)
                pool.wait_ge(meta_chain, 3 * t + 3)
                G.tensor_tensor(gate[:, u:u + 1], gsel[:, u:u + 1], xf[:, u, C_G2:C_G2 + 1], ALU.add).then_inc(gate_ready, 1)

            def add_rows(t, u):
                pool.wait_ge(y_done, t + 1)
                pool.wait_ge(gate_ready, t + 1)
                before = pool.value_load(fence[0:1, bass.ds(t, 1)], min_val=0, max_val=FT)
                for k in range(2):
                    pool.wait_ge(added[k], ((before + (1 - k)) >> 1) * 16 + 16)
                apart(pool)
                G.indirect_dma_start(out=out, out_offset=bass.IndirectOffsetOnAxis(ap=dest[:, u:u + 1].bitcast(U32), axis=0),
                                     in_=y_sb[:, u % 2], in_offset=None, compute_op=ALU.add).then_inc(added[u % 2], 16)

            def turn(t, u, r):
                read_columns(t, u, r)
                if not (isinstance(t, int) and t < 2):
                    add_rows(t - 2, (u - 2) % FU)

            for u in range(FU):
                turn(u, u, 0)
            with pool.Fori(1, FT // FU) as r:
                for u in range(FU):
                    turn(r * FU + u, u, r)
            for t in (FT - 2, FT - 1):
                add_rows(t, t % FU)
            for k in range(2):
                pool.wait_ge(added[k], 16 * (FT // 2 + 1))


_INS = ["L0_attn_in_features", "L0_attn_Wq", "L0_attn_Wk", "L0_attn_Wv", "L0_attn_Wo", "L0_ffn_Wg", "L0_ffn_W1",
        "L0_ffn_b1", "L0_ffn_W2", "L0_ffn_b2"]


def kernel(**inputs):
    import numpy as _np
    import concourse.bacc as _bacc
    from concourse import mybir as _mybir
    from concourse.bass_utils import run_bass_kernel_spmd as _run

    nc = _bacc.Bacc("TRN2", target_bir_lowering=False, num_devices=1)
    arrays, args = {}, []
    for name in _INS:
        a = _np.ascontiguousarray(inputs[name])
        arrays[f"in_{name}"] = a
        args.append(nc.dram_tensor(f"in_{name}", a.shape, _mybir.dt.from_np(a.dtype), kind="ExternalInput").ap())
    args.append(nc.dram_tensor("out_0", (OUT_ROWS, D), _mybir.dt.float32, kind="ExternalOutput").ap())
    moe_block(nc, *args)
    r = _run(nc, [arrays], core_ids=[0])
    return r.results[0]["out_0"][:S].reshape(1, S, D)
```
